# Optimizing a Trainium2 kernel written in Bass

```python
import numpy as np
import jax
import jax.numpy as jnp

def _softmax(x, axis=-1):
    return jax.nn.softmax(x, axis=axis)

def _gelu(x):
    return jax.nn.gelu(x, approximate=True)

def _silu(x):
    return jax.nn.silu(x)

def _sigmoid(x):
    return jax.nn.sigmoid(x)

def _layernorm(x, axis=-1, eps=1e-05):
    m = jnp.mean(x, axis=axis, keepdims=True)
    v = jnp.var(x, axis=axis, keepdims=True)
    return (x - m) / jnp.sqrt(v + eps)

def _scatter_add(tgt, idx, src, axis=0):
    return tgt.at[idx].add(src)

def _segment_sum(src, seg, n):
    return jax.ops.segment_sum(src, seg, n)
kernel_name = 'mk_flamingo_gated_d4_seqx_r8_607e0e'

def setup_inputs(seed: int=0):
    np.random.seed(seed)
    _w = jnp.asarray

    def _rec_inputs():
        import jax
        import jax.numpy as jnp
        _rk = jax.random.key(seed)
        x = 7.22e-05 + 1 * jax.random.normal(jax.random.fold_in(_rk, 1), (16, 128, 128), jnp.float32)
        _lenS = 128 - jax.random.randint(jax.random.fold_in(_rk, 7), (16,), 0, max(1, 128 // 4) + 1, jnp.int32)
        _lenS2 = 128 - jax.random.randint(jax.random.fold_in(_rk, 8), (16,), 0, max(1, 128 // 4) + 1, jnp.int32)
        _ctx_1024P = jax.random.normal(jax.random.fold_in(_rk, 11), (16, 16, 128), jnp.float32)
        _ctx_1024c = jax.random.dirichlet(jax.random.fold_in(_rk, 511), 0.3 * jnp.ones((16,), jnp.float32), (16, 128))
        _ctx_1024t = jnp.einsum('bsk,bkd->bsd', _ctx_1024c, _ctx_1024P)
        _ctx_1024t = _ctx_1024t * jax.lax.rsqrt(jnp.mean(jnp.square(_ctx_1024t)) + 1e-12) * 0.953939
        ctx_1024 = 4.13588e-05 + 0.999923 * (_ctx_1024t + 0.3 * jax.random.normal(jax.random.fold_in(_rk, 611), (16, 128, 128), jnp.float32))
        _g = jax.random.normal(jax.random.fold_in(_rk, 9001), (2, 4), jnp.float32)
        _g = jnp.sign(_g) * jnp.maximum(jnp.abs(_g), 1.0) + (_g == 0) * 1.0
        g_xattn = _g[0]
        g_ffn = _g[1]
        return (x, ctx_1024, g_xattn, g_ffn)
    x, ctx_1024, g_xattn, g_ffn = _rec_inputs()

    def _L0_xattn_setup():
        import jax, jax.numpy as jnp
        import numpy as np
        D = 128
        key = jax.random.key(seed)
        ks = jax.random.split(key, 11)
        B, Sq, Skv = (4, 256, 256)
        s = 0.02
        return {'query': jax.random.normal(ks[0], (B, Sq, D), jnp.float32), 'key': jax.random.normal(ks[1], (B, Skv, D), jnp.float32), 'value': jax.random.normal(ks[2], (B, Skv, D), jnp.float32), 'Wq': jax.random.normal(ks[3], (D, D), jnp.float32) * s, 'bq': jnp.zeros((D,), jnp.float32), 'Wk': jax.random.normal(ks[4], (D, D), jnp.float32) * s, 'bk': jnp.zeros((D,), jnp.float32), 'Wv': jax.random.normal(ks[5], (D, D), jnp.float32) * s, 'bv': jnp.zeros((D,), jnp.float32), 'Wo': jax.random.normal(ks[6], (D, D), jnp.float32) * s, 'bo': jnp.zeros((D,), jnp.float32)}
    _L0_xattn_all = _L0_xattn_setup()
    _L0_xattn_in = {k: v for k, v in _L0_xattn_all.items() if k in ('Wq', 'bq', 'Wk', 'bk', 'Wv', 'bv', 'Wo', 'bo')}
    del _L0_xattn_all

    def _L0_ffn_setup():
        import jax, jax.numpy as jnp
        import numpy as np
        B, S, D = (2, 256, 128)
        E, G, K = (32, 8, 4)
        H, SH = (256, 256)
        CAP_FACTOR = 1.25

        def _l2norm(v):
            n = jnp.linalg.norm(v, axis=-1, keepdims=True)
            return v / jnp.maximum(n, 1e-12)
        key = jax.random.key(seed)
        ks = jax.random.split(key, 10)
        x = jax.random.normal(ks[0], (B, S, D), jnp.float32)
        group_centroids = jax.random.normal(ks[1], (G, D), jnp.float32) * 0.02
        expert_centroids = jax.random.normal(ks[2], (E, D), jnp.float32) * 0.02
        bias = jnp.zeros((E,), jnp.float32)
        sd_in = 1.0 / np.sqrt(D).astype(np.float32)
        sd_h = 1.0 / np.sqrt(H).astype(np.float32)
        wg = jax.random.normal(ks[3], (E, D, H), jnp.float32) * sd_in
        wu = jax.random.normal(ks[4], (E, D, H), jnp.float32) * sd_in
        wd = jax.random.normal(ks[5], (E, H, D), jnp.float32) * sd_h
        sg = jax.random.normal(ks[6], (D, SH), jnp.float32) * sd_in
        su = jax.random.normal(ks[7], (D, SH), jnp.float32) * sd_in
        sd_w = jax.random.normal(ks[8], (SH, D), jnp.float32) * sd_h
        return dict(x=x, group_centroids=group_centroids, expert_centroids=expert_centroids, bias=bias, wg=wg, wu=wu, wd=wd, sg=sg, su=su, sd=sd_w)
    _L0_ffn_all = _L0_ffn_setup()
    _L0_ffn_in = {k: v for k, v in _L0_ffn_all.items() if k in ('group_centroids', 'expert_centroids', 'bias', 'wg', 'wu', 'wd', 'sg', 'su', 'sd')}
    del _L0_ffn_all

    def _L1_xattn_setup():
        import jax, jax.numpy as jnp
        import numpy as np
        EMBED_DIM = 128
        NUM_HEADS = 16
        HEAD_DIM = EMBED_DIM // NUM_HEADS
        B, T_Q, T_K = (2, 256, 256)
        key = jax.random.key(seed)
        ks = jax.random.split(key, 11)
        s = 1.0 / np.sqrt(EMBED_DIM)
        return {'query': jax.random.normal(ks[0], (B, T_Q, EMBED_DIM), jnp.float32), 'key': jax.random.normal(ks[1], (B, T_K, EMBED_DIM), jnp.float32), 'value': jax.random.normal(ks[2], (B, T_K, EMBED_DIM), jnp.float32), 'Wq': jax.random.normal(ks[3], (EMBED_DIM, EMBED_DIM), jnp.float32) * s, 'bq': jnp.zeros((EMBED_DIM,), jnp.float32), 'Wk': jax.random.normal(ks[4], (EMBED_DIM, EMBED_DIM), jnp.float32) * s, 'bk': jnp.zeros((EMBED_DIM,), jnp.float32), 'Wv': jax.random.normal(ks[5], (EMBED_DIM, EMBED_DIM), jnp.float32) * s, 'bv': jnp.zeros((EMBED_DIM,), jnp.float32), 'Wo': jax.random.normal(ks[6], (EMBED_DIM, EMBED_DIM), jnp.float32) * s, 'bo': jnp.zeros((EMBED_DIM,), jnp.float32)}
    _L1_xattn_all = _L1_xattn_setup()
    _L1_xattn_in = {k: v for k, v in _L1_xattn_all.items() if k in ('Wq', 'bq', 'Wk', 'bk', 'Wv', 'bv', 'Wo', 'bo')}
    del _L1_xattn_all

    def _L1_ffn_setup():
        import jax, jax.numpy as jnp
        import numpy as np
        B, S, H = (2, 128, 128)
        E, F = (16, 64)
        G, TOPK_G, TOPK = (4, 2, 4)
        N_SHARED = 2
        ROUTE_SCALE = 1.0
        FS = N_SHARED * F

        def _gate(x, w_gate):
            T = x.shape[0]
            scores = jax.nn.sigmoid(x @ w_gate.T)
            sv = scores.reshape(T, G, E // G)
            group_scores = jax.lax.top_k(sv, 2)[0].sum(-1)
            top_groups = jax.lax.top_k(group_scores, TOPK_G)[1]
            allowed = jnp.zeros((T, G), dtype=bool).at[jnp.arange(T)[:, None], top_groups].set(True)
            masked = jnp.where(allowed[:, :, None], sv, -jnp.inf).reshape(T, E)
            _, idx = jax.lax.top_k(masked, TOPK)
            w = jnp.take_along_axis(scores, idx, axis=1)
            w = w / (w.sum(-1, keepdims=True) + 1e-06) * ROUTE_SCALE
            return (w, idx)

        def _swiglu(x, w1, w3, w2):
            return jax.nn.silu(x @ w1.T) * (x @ w3.T) @ w2.T
        key = jax.random.key(seed)
        ks = jax.random.split(key, 8)
        scale = 0.02
        return {'hidden_states': jax.random.normal(ks[0], (B, S, H), dtype=jnp.float32), 'w_gate': jax.random.normal(ks[1], (E, H), dtype=jnp.float32) * scale, 'w1_e': jax.random.normal(ks[2], (E, F, H), dtype=jnp.float32) * scale, 'w3_e': jax.random.normal(ks[3], (E, F, H), dtype=jnp.float32) * scale, 'w2_e': jax.random.normal(ks[4], (E, H, F), dtype=jnp.float32) * scale, 'w1_s': jax.random.normal(ks[5], (FS, H), dtype=jnp.float32) * scale, 'w3_s': jax.random.normal(ks[6], (FS, H), dtype=jnp.float32) * scale, 'w2_s': jax.random.normal(ks[7], (H, FS), dtype=jnp.float32) * scale}
    _L1_ffn_all = _L1_ffn_setup()
    _L1_ffn_in = {k: v for k, v in _L1_ffn_all.items() if k in ('w_gate', 'w1_e', 'w3_e', 'w2_e', 'w1_s', 'w3_s', 'w2_s')}
    del _L1_ffn_all

    def _L2_xattn_setup():
        import jax, jax.numpy as jnp
        import numpy as np
        D1, D2, D3 = (128, 128, 128)
        key = jax.random.key(seed)
        k1, k2, kw, kb = jax.random.split(key, 4)
        x1 = jax.random.normal(k1, (8, 256, D1), dtype=jnp.float32)
        x2 = jax.random.normal(k2, (8, 256, D2), dtype=jnp.float32)
        bound = 1.0 / np.sqrt(D1 + D2)
        W = jax.random.uniform(kw, (D3, D1 + D2), minval=-bound, maxval=bound, dtype=jnp.float32)
        b = jax.random.uniform(kb, (D3,), minval=-bound, maxval=bound, dtype=jnp.float32)
        return {'x1': x1, 'x2': x2, 'W': W, 'b': b}
    _L2_xattn_all = _L2_xattn_setup()
    _L2_xattn_in = {k: v for k, v in _L2_xattn_all.items() if k in ('W', 'b')}
    del _L2_xattn_all

    def _L2_ffn_setup():
        import jax, jax.numpy as jnp
        import numpy as np
        from jax import lax
        DIM = 128
        N_EXPERTS = 16
        TOPK = 4
        N_GROUPS = 4
        TOPK_GROUPS = 2
        ROUTE_SCALE = 1.0
        INTER = 64
        SHARED_INTER = 2 * INTER

        def _gate(x, gate_w):
            T = x.shape[0]
            logits = x @ gate_w.T
            scores = jax.nn.softmax(logits.astype(jnp.float32), axis=-1)
            original_scores = scores
            g = scores.reshape(T, N_GROUPS, N_EXPERTS // N_GROUPS)
            group_scores = g.max(axis=-1)
            _, gidx = lax.top_k(group_scores, TOPK_GROUPS)
            gmask = jnp.zeros_like(group_scores).at[jnp.arange(T)[:, None], gidx].set(1.0)
            masked = (g * gmask[..., None]).reshape(T, N_EXPERTS)
            _, indices = lax.top_k(masked, TOPK)
            weights = jnp.take_along_axis(original_scores, indices, axis=1)
            weights = weights * ROUTE_SCALE
            return (weights.astype(x.dtype), indices)
        key = jax.random.key(seed)
        ks = jax.random.split(key, 8)
        s = lambda fan_in: 1.0 / np.sqrt(fan_in)
        return {'x': jax.random.normal(ks[0], (2, 128, DIM), dtype=jnp.float32), 'gate_w': jax.random.normal(ks[1], (N_EXPERTS, DIM), dtype=jnp.float32) * s(DIM), 'w1': jax.random.normal(ks[2], (N_EXPERTS, DIM, INTER), dtype=jnp.float32) * s(DIM), 'w2': jax.random.normal(ks[3], (N_EXPERTS, INTER, DIM), dtype=jnp.float32) * s(INTER), 'w3': jax.random.normal(ks[4], (N_EXPERTS, DIM, INTER), dtype=jnp.float32) * s(DIM), 'ws1': jax.random.normal(ks[5], (DIM, SHARED_INTER), dtype=jnp.float32) * s(DIM), 'ws2': jax.random.normal(ks[6], (SHARED_INTER, DIM), dtype=jnp.float32) * s(SHARED_INTER), 'ws3': jax.random.normal(ks[7], (DIM, SHARED_INTER), dtype=jnp.float32) * s(DIM)}
    _L2_ffn_all = _L2_ffn_setup()
    _L2_ffn_in = {k: v for k, v in _L2_ffn_all.items() if k in ('gate_w', 'w1', 'w2', 'w3', 'ws1', 'ws2', 'ws3')}
    del _L2_ffn_all

    def _L3_xattn_setup():
        import jax, jax.numpy as jnp
        import numpy as np
        key = jax.random.key(seed)
        k1, k2, k3 = jax.random.split(key, 3)
        B, N, D = (4, 512, 128)
        return {'q': jax.random.normal(k1, (B, N, D), dtype=jnp.float32), 'k': jax.random.normal(k2, (B, N, D), dtype=jnp.float32), 'v': jax.random.normal(k3, (B, N, D), dtype=jnp.float32), 'ctx': 128}
    _L3_xattn_all = _L3_xattn_setup()
    _L3_xattn_in = {k: v for k, v in _L3_xattn_all.items() if k in ()}
    del _L3_xattn_all

    def _L3_ffn_setup():
        import jax, jax.numpy as jnp
        import numpy as np
        TOP_K = 2

        def _ffn(x, gw, uw, dw):
            return jax.nn.silu(x @ gw.T) * (x @ uw.T) @ dw.T
        key = jax.random.key(seed)
        ks = jax.random.split(key, 8)
        w = lambda k, shape: jax.random.normal(k, shape, jnp.float32) * 0.02
        return dict(x=jax.random.normal(ks[0], (4, 256, 128), jnp.float32), gate_w=w(ks[1], (8, 128)), expert_gate=w(ks[2], (8, 352, 128)), expert_up=w(ks[3], (8, 352, 128)), expert_down=w(ks[4], (8, 128, 352)), shared_gate=w(ks[5], (352, 128)), shared_up=w(ks[6], (352, 128)), shared_down=w(ks[7], (128, 352)))
    _L3_ffn_all = _L3_ffn_setup()
    _L3_ffn_in = {k: v for k, v in _L3_ffn_all.items() if k in ('gate_w', 'expert_gate', 'expert_up', 'expert_down', 'shared_gate', 'shared_up', 'shared_down')}
    del _L3_ffn_all
    return {'x': x, 'ctx_1024': ctx_1024, 'g_xattn': g_xattn, 'g_ffn': g_ffn, 'L0_xattn_Wq': _L0_xattn_in['Wq'], 'L0_xattn_bq': _L0_xattn_in['bq'], 'L0_xattn_Wk': _L0_xattn_in['Wk'], 'L0_xattn_bk': _L0_xattn_in['bk'], 'L0_xattn_Wv': _L0_xattn_in['Wv'], 'L0_xattn_bv': _L0_xattn_in['bv'], 'L0_xattn_Wo': _L0_xattn_in['Wo'], 'L0_xattn_bo': _L0_xattn_in['bo'], 'L0_ffn_group_centroids': _L0_ffn_in['group_centroids'], 'L0_ffn_expert_centroids': _L0_ffn_in['expert_centroids'], 'L0_ffn_bias': _L0_ffn_in['bias'], 'L0_ffn_wg': _L0_ffn_in['wg'], 'L0_ffn_wu': _L0_ffn_in['wu'], 'L0_ffn_wd': _L0_ffn_in['wd'], 'L0_ffn_sg': _L0_ffn_in['sg'], 'L0_ffn_su': _L0_ffn_in['su'], 'L0_ffn_sd': _L0_ffn_in['sd'], 'L1_xattn_Wq': _L1_xattn_in['Wq'], 'L1_xattn_bq': _L1_xattn_in['bq'], 'L1_xattn_Wk': _L1_xattn_in['Wk'], 'L1_xattn_bk': _L1_xattn_in['bk'], 'L1_xattn_Wv': _L1_xattn_in['Wv'], 'L1_xattn_bv': _L1_xattn_in['bv'], 'L1_xattn_Wo': _L1_xattn_in['Wo'], 'L1_xattn_bo': _L1_xattn_in['bo'], 'L1_ffn_w_gate': _L1_ffn_in['w_gate'], 'L1_ffn_w1_e': _L1_ffn_in['w1_e'], 'L1_ffn_w3_e': _L1_ffn_in['w3_e'], 'L1_ffn_w2_e': _L1_ffn_in['w2_e'], 'L1_ffn_w1_s': _L1_ffn_in['w1_s'], 'L1_ffn_w3_s': _L1_ffn_in['w3_s'], 'L1_ffn_w2_s': _L1_ffn_in['w2_s'], 'L2_xattn_W': _L2_xattn_in['W'], 'L2_xattn_b': _L2_xattn_in['b'], 'L2_ffn_gate_w': _L2_ffn_in['gate_w'], 'L2_ffn_w1': _L2_ffn_in['w1'], 'L2_ffn_w2': _L2_ffn_in['w2'], 'L2_ffn_w3': _L2_ffn_in['w3'], 'L2_ffn_ws1': _L2_ffn_in['ws1'], 'L2_ffn_ws2': _L2_ffn_in['ws2'], 'L2_ffn_ws3': _L2_ffn_in['ws3'], 'L3_ffn_gate_w': _L3_ffn_in['gate_w'], 'L3_ffn_expert_gate': _L3_ffn_in['expert_gate'], 'L3_ffn_expert_up': _L3_ffn_in['expert_up'], 'L3_ffn_expert_down': _L3_ffn_in['expert_down'], 'L3_ffn_shared_gate': _L3_ffn_in['shared_gate'], 'L3_ffn_shared_up': _L3_ffn_in['shared_up'], 'L3_ffn_shared_down': _L3_ffn_in['shared_down']}

def reference(x, ctx_1024, g_xattn, g_ffn, L0_xattn_Wq, L0_xattn_bq, L0_xattn_Wk, L0_xattn_bk, L0_xattn_Wv, L0_xattn_bv, L0_xattn_Wo, L0_xattn_bo, L0_ffn_group_centroids, L0_ffn_expert_centroids, L0_ffn_bias, L0_ffn_wg, L0_ffn_wu, L0_ffn_wd, L0_ffn_sg, L0_ffn_su, L0_ffn_sd, L1_xattn_Wq, L1_xattn_bq, L1_xattn_Wk, L1_xattn_bk, L1_xattn_Wv, L1_xattn_bv, L1_xattn_Wo, L1_xattn_bo, L1_ffn_w_gate, L1_ffn_w1_e, L1_ffn_w3_e, L1_ffn_w2_e, L1_ffn_w1_s, L1_ffn_w3_s, L1_ffn_w2_s, L2_xattn_W, L2_xattn_b, L2_ffn_gate_w, L2_ffn_w1, L2_ffn_w2, L2_ffn_w3, L2_ffn_ws1, L2_ffn_ws2, L2_ffn_ws3, L3_ffn_gate_w, L3_ffn_expert_gate, L3_ffn_expert_up, L3_ffn_expert_down, L3_ffn_shared_gate, L3_ffn_shared_up, L3_ffn_shared_down):
    import jax
    import jax.numpy as jnp

    def _L0_xattn_ref(query, key, value, Wq, bq, Wk, bk, Wv, bv, Wo, bo):
        import jax, jax.numpy as jnp
        import numpy as np
        D = 128
        Q = jnp.einsum('bsd,de->bse', query, Wq) + bq
        K = jnp.einsum('bsd,de->bse', key, Wk) + bk
        V = jnp.einsum('bsd,de->bse', value, Wv) + bv
        scale = 1.0 / jnp.sqrt(jnp.asarray(D, Q.dtype))
        scores = jnp.einsum('bqd,bkd->bqk', Q, K) * scale
        attn = jax.nn.softmax(scores, axis=-1)
        out = jnp.einsum('bqk,bkd->bqd', attn, V)
        return jnp.einsum('bsd,de->bse', out, Wo) + bo

    def _L0_ffn_ref(x, group_centroids, expert_centroids, bias, wg, wu, wd, sg, su, sd):
        import jax, jax.numpy as jnp
        import numpy as np
        B, S, D = (2, 256, 128)
        E, G, K = (32, 8, 4)
        H, SH = (256, 256)
        CAP_FACTOR = 1.25

        def _l2norm(v):
            n = jnp.linalg.norm(v, axis=-1, keepdims=True)
            return v / jnp.maximum(n, 1e-12)
        b, s, d = x.shape
        xf = x.reshape(-1, d)
        N = xf.shape[0]
        shared = jax.nn.silu(xf @ sg) * (xf @ su) @ sd
        xn = _l2norm(xf)
        group_scores = xn @ _l2norm(group_centroids).T
        n_top_groups = max(1, G // 2)
        _, top_group_idx = jax.lax.top_k(group_scores, n_top_groups)
        expert_scores = xn @ _l2norm(expert_centroids).T + bias
        expert_to_group = jnp.arange(E) // (E // G)
        sel = jnp.zeros((N, G), xf.dtype).at[jnp.arange(N)[:, None], top_group_idx].set(1.0)
        group_mask = sel[:, expert_to_group]
        masked = expert_scores * group_mask + (1.0 - group_mask) * -1000000000.0
        top_scores, top_idx = jax.lax.top_k(masked, K)
        gates = jax.nn.softmax(top_scores, axis=-1)
        capacity = max(1, int(N / E * K * CAP_FACTOR))
        flat_e = top_idx.reshape(-1)
        flat_g = gates.reshape(-1)
        tok = jnp.repeat(jnp.arange(N), K)
        onehot = jax.nn.one_hot(flat_e, E, dtype=jnp.int32)
        pos = jnp.cumsum(onehot, axis=0)[jnp.arange(N * K), flat_e] - 1
        keep = pos < capacity
        e_s = jnp.where(keep, flat_e, E)
        p_s = jnp.where(keep, pos, 0)
        buf = jnp.zeros((E + 1, capacity, d), xf.dtype).at[e_s, p_s].set(xf[tok])[:E]
        h = jax.nn.silu(jnp.einsum('ecd,edh->ech', buf, wg)) * jnp.einsum('ecd,edh->ech', buf, wu)
        out_e = jnp.einsum('ech,ehd->ecd', h, wd)
        gathered = out_e[flat_e, jnp.minimum(pos, capacity - 1)]
        contrib = gathered * (flat_g * keep.astype(xf.dtype))[:, None]
        routed = jnp.zeros_like(xf).at[tok].add(contrib)
        return (shared + routed).reshape(b, s, d)

    def _L1_xattn_ref(query, key, value, Wq, bq, Wk, bk, Wv, bv, Wo, bo):
        import jax, jax.numpy as jnp
        import numpy as np
        EMBED_DIM = 128
        NUM_HEADS = 16
        HEAD_DIM = EMBED_DIM // NUM_HEADS
        B, T_Q, T_K = (2, 256, 256)
        b, tq, _ = query.shape
        tk = key.shape[1]
        q = (query @ Wq.T + bq).reshape(b, tq, NUM_HEADS, HEAD_DIM).transpose(0, 2, 1, 3)
        k = (key @ Wk.T + bk).reshape(b, tk, NUM_HEADS, HEAD_DIM).transpose(0, 2, 1, 3)
        v = (value @ Wv.T + bv).reshape(b, tk, NUM_HEADS, HEAD_DIM).transpose(0, 2, 1, 3)
        scores = jnp.einsum('bhqd,bhkd->bhqk', q, k) / np.sqrt(HEAD_DIM)
        attn = jax.nn.softmax(scores, axis=-1)
        attn = jnp.nan_to_num(attn, nan=0.0)
        out = jnp.einsum('bhqk,bhkd->bhqd', attn, v)
        out = out.transpose(0, 2, 1, 3).reshape(b, tq, EMBED_DIM)
        return out @ Wo.T + bo

    def _L1_ffn_ref(hidden_states, w_gate, w1_e, w3_e, w2_e, w1_s, w3_s, w2_s):
        import jax, jax.numpy as jnp
        import numpy as np
        B, S, H = (2, 128, 128)
        E, F = (16, 64)
        G, TOPK_G, TOPK = (4, 2, 4)
        N_SHARED = 2
        ROUTE_SCALE = 1.0
        FS = N_SHARED * F

        def _gate(x, w_gate):
            T = x.shape[0]
            scores = jax.nn.sigmoid(x @ w_gate.T)
            sv = scores.reshape(T, G, E // G)
            group_scores = jax.lax.top_k(sv, 2)[0].sum(-1)
            top_groups = jax.lax.top_k(group_scores, TOPK_G)[1]
            allowed = jnp.zeros((T, G), dtype=bool).at[jnp.arange(T)[:, None], top_groups].set(True)
            masked = jnp.where(allowed[:, :, None], sv, -jnp.inf).reshape(T, E)
            _, idx = jax.lax.top_k(masked, TOPK)
            w = jnp.take_along_axis(scores, idx, axis=1)
            w = w / (w.sum(-1, keepdims=True) + 1e-06) * ROUTE_SCALE
            return (w, idx)

        def _swiglu(x, w1, w3, w2):
            return jax.nn.silu(x @ w1.T) * (x @ w3.T) @ w2.T
        shape = hidden_states.shape
        x = hidden_states.reshape(-1, H)
        weights, idx = _gate(x, w_gate)
        combine = (jax.nn.one_hot(idx, E, dtype=x.dtype) * weights[..., None]).sum(1)
        g = jax.nn.silu(jnp.einsum('th,efh->tef', x, w1_e))
        u = jnp.einsum('th,efh->tef', x, w3_e)
        routed = jnp.einsum('tef,ehf,te->th', g * u, w2_e, combine)
        shared = _swiglu(x, w1_s, w3_s, w2_s)
        return (routed + shared).reshape(shape)

    def _L2_xattn_ref(x1, x2, W, b):
        import jax, jax.numpy as jnp
        import numpy as np
        D1, D2, D3 = (128, 128, 128)
        d1 = x1.shape[-1]
        W1 = W[:, :d1]
        W2 = W[:, d1:]
        part1 = jnp.einsum('bld,ed->ble', x1, W1)
        part2 = jnp.einsum('bld,ed->be', x2, W2) / x2.shape[1]
        return part1 + part2[:, None, :] + b

    def _L2_ffn_ref(x, gate_w, w1, w2, w3, ws1, ws2, ws3):
        import jax, jax.numpy as jnp
        import numpy as np
        from jax import lax
        DIM = 128
        N_EXPERTS = 16
        TOPK = 4
        N_GROUPS = 4
        TOPK_GROUPS = 2
        ROUTE_SCALE = 1.0
        INTER = 64
        SHARED_INTER = 2 * INTER

        def _gate(x, gate_w):
            T = x.shape[0]
            logits = x @ gate_w.T
            scores = jax.nn.softmax(logits.astype(jnp.float32), axis=-1)
            original_scores = scores
            g = scores.reshape(T, N_GROUPS, N_EXPERTS // N_GROUPS)
            group_scores = g.max(axis=-1)
            _, gidx = lax.top_k(group_scores, TOPK_GROUPS)
            gmask = jnp.zeros_like(group_scores).at[jnp.arange(T)[:, None], gidx].set(1.0)
            masked = (g * gmask[..., None]).reshape(T, N_EXPERTS)
            _, indices = lax.top_k(masked, TOPK)
            weights = jnp.take_along_axis(original_scores, indices, axis=1)
            weights = weights * ROUTE_SCALE
            return (weights.astype(x.dtype), indices)
        shape = x.shape
        xt = x.reshape(-1, DIM)
        T = xt.shape[0]
        weights, indices = _gate(xt, gate_w)
        c = jnp.zeros((T, N_EXPERTS), dtype=xt.dtype)
        c = c.at[jnp.arange(T)[:, None], indices].add(weights)
        h1 = jnp.einsum('td,edi->tei', xt, w1)
        h3 = jnp.einsum('td,edi->tei', xt, w3)
        a = jax.nn.silu(h1) * h3
        y = jnp.einsum('tei,eid,te->td', a, w2, c)
        z = jax.nn.silu(xt @ ws1) * (xt @ ws3) @ ws2
        return (y + z).reshape(shape)

    def _L3_xattn_ref(q, k, v, ctx):
        import jax, jax.numpy as jnp
        import numpy as np
        N = q.shape[1]
        g = jax.nn.relu(k) * v
        c = jnp.cumsum(g, axis=1)
        i = jnp.arange(N)
        hi = jnp.minimum(i + ctx, N - 1)
        lo = i - ctx - 1
        upper = c[:, hi, :]
        lower = jnp.where((lo >= 0)[None, :, None], c[:, jnp.clip(lo, 0, N - 1), :], jnp.zeros((), dtype=c.dtype))
        attn = upper - lower
        return jax.nn.relu(q) * attn

    def _L3_ffn_ref(x, gate_w, expert_gate, expert_up, expert_down, shared_gate, shared_up, shared_down):
        import jax, jax.numpy as jnp
        import numpy as np
        TOP_K = 2

        def _ffn(x, gw, uw, dw):
            return jax.nn.silu(x @ gw.T) * (x @ uw.T) @ dw.T
        B, S, H = x.shape
        xf = x.reshape(-1, H)
        T = xf.shape[0]
        E = expert_gate.shape[0]
        shared = _ffn(xf, shared_gate, shared_up, shared_down)
        logits = xf @ gate_w.T
        probs = jax.nn.softmax(logits, axis=-1)
        topw, topi = jax.lax.top_k(probs, TOP_K)
        topw = topw / (topw.sum(-1, keepdims=True) + 1e-20)
        comb = jnp.zeros((T, E), xf.dtype).at[jnp.arange(T)[:, None], topi].add(topw)

        def body(acc, ws):
            gw, uw, dw, wcol = ws
            return (acc + _ffn(xf, gw, uw, dw) * wcol[:, None], None)
        routed, _ = jax.lax.scan(body, jnp.zeros_like(xf), (expert_gate, expert_up, expert_down, comb.T))
        return (shared + routed).reshape(B, S, H)
    x = x + jnp.tanh(g_xattn[0]) * _L0_xattn_ref(_layernorm(x, axis=-1), ctx_1024, ctx_1024, L0_xattn_Wq, L0_xattn_bq, L0_xattn_Wk, L0_xattn_bk, L0_xattn_Wv, L0_xattn_bv, L0_xattn_Wo, L0_xattn_bo)
    x = x + jnp.tanh(g_ffn[0]) * _L0_ffn_ref(_layernorm(x, axis=-1), L0_ffn_group_centroids, L0_ffn_expert_centroids, L0_ffn_bias, L0_ffn_wg, L0_ffn_wu, L0_ffn_wd, L0_ffn_sg, L0_ffn_su, L0_ffn_sd)
    x = x + jnp.tanh(g_xattn[1]) * _L1_xattn_ref(_layernorm(x, axis=-1), ctx_1024, ctx_1024, L1_xattn_Wq, L1_xattn_bq, L1_xattn_Wk, L1_xattn_bk, L1_xattn_Wv, L1_xattn_bv, L1_xattn_Wo, L1_xattn_bo)
    x = x + jnp.tanh(g_ffn[1]) * _L1_ffn_ref(_layernorm(x, axis=-1), L1_ffn_w_gate, L1_ffn_w1_e, L1_ffn_w3_e, L1_ffn_w2_e, L1_ffn_w1_s, L1_ffn_w3_s, L1_ffn_w2_s)
    x = x + jnp.tanh(g_xattn[2]) * _L2_xattn_ref(_layernorm(x, axis=-1), ctx_1024, L2_xattn_W, L2_xattn_b)
    x = x + jnp.tanh(g_ffn[2]) * _L2_ffn_ref(_layernorm(x, axis=-1), L2_ffn_gate_w, L2_ffn_w1, L2_ffn_w2, L2_ffn_w3, L2_ffn_ws1, L2_ffn_ws2, L2_ffn_ws3)
    x = x + jnp.tanh(g_xattn[3]) * _L3_xattn_ref(_layernorm(x, axis=-1), ctx_1024, ctx_1024, 128)
    x = x + jnp.tanh(g_ffn[3]) * _L3_ffn_ref(_layernorm(x, axis=-1), L3_ffn_gate_w, L3_ffn_expert_gate, L3_ffn_expert_up, L3_ffn_expert_down, L3_ffn_shared_gate, L3_ffn_shared_up, L3_ffn_shared_down)
    return x

_drawn_inputs = setup_inputs


def setup_inputs(seed=0):
    import zlib

    import numpy as np

    out = dict(_drawn_inputs(seed))
    spreads = {'L0_xattn_bq': (0.0, 0.8),
     'L0_xattn_bk': (0.0, 2.0),
     'L0_xattn_bv': (0.0, 0.1),
     'L0_xattn_bo': (0.0, 0.1),
     'L0_ffn_bias': (0.0, 0.1),
     'L1_xattn_bq': (0.0, 0.377),
     'L1_xattn_bk': (0.0, 2.0),
     'L1_xattn_bv': (0.0, 0.1),
     'L1_xattn_bo': (0.0, 0.1)}
    factors = {'g_ffn': 8.0,
     'L0_xattn_Wq': 8.0,
     'L0_xattn_Wk': 8.0,
     'L1_ffn_w_gate': 8.0,
     'L1_ffn_w1_e': 8.0,
     'L1_ffn_w3_e': 8.0,
     'L1_ffn_w2_e': 8.0,
     'L1_ffn_w1_s': 8.0,
     'L1_ffn_w3_s': 8.0,
     'L1_ffn_w2_s': 8.0,
     'L3_ffn_gate_w': 8.0,
     'L3_ffn_expert_gate': 8.0,
     'L3_ffn_expert_up': 8.0,
     'L3_ffn_expert_down': 8.0,
     'L3_ffn_shared_gate': 8.0,
     'L3_ffn_shared_up': 8.0,
     'L3_ffn_shared_down': 8.0,
     'L2_xattn_b': 6.193}
    for name, (base, spread) in spreads.items():
        noise = np.random.default_rng([zlib.crc32(name.encode()), seed]).standard_normal(out[name].shape)
        drawn = base * np.exp(spread * noise) if base else spread * noise
        out[name] = jnp.asarray(drawn.astype(out[name].dtype))
    for name, factor in factors.items():
        out[name] = (out[name] * factor).astype(out[name].dtype)
    return out
```

```python
from contextlib import ExitStack

import numpy as np
import concourse.bass as bass
from concourse import mybir

F32 = mybir.dt.float32
F32R = mybir.dt.float32r
BF16 = mybir.dt.bfloat16
I32 = mybir.dt.int32
U32 = mybir.dt.uint32
ALU = mybir.AluOpType
ACT = mybir.ActivationFunctionType
AX = mybir.AxisListType


class Names(dict):

    def __getattr__(self, name):
        return self[name]

    def __setattr__(self, name, value):
        self[name] = value


P = 128
SEQS = 16
T = 4
CHUNKS = SEQS // T
CW = T * P
EPS = 1e-5

E0, G0, K0, HID0 = 32, 8, 4, 256
CAP = int(SEQS * P / E0 * K0 * 1.25)
ROWS = (112, 112, 96)
RT = 112
SLOTS = E0 * CAP
W0C = 3 * HID0
E1, G1, K1 = 16, 4, 4
NB1 = E1 // 2 + 1
W1C = 3 * P
E3, K3 = 8, 2
FF3 = 352
M3 = (128, 128, 96)
W3C = 2 * FF3 + 3 * P
HEADS, HD = 16, 8

C_ID = 0
C_SPLIT = 128
C_R8 = 130
C_R16 = C_R8 + T * 8
C_ALL = C_R16 + T * E1
L_U, L_ONE = 0, 128
L_TRASH = 256
L_START = 257
L_R8 = L_START + E0
L_R32 = L_R8 + SEQS * 8
L_R16T = L_R32 + SEQS * E0
L_SPREAD = L_R16T + SEQS * E0
L_ALL = L_SPREAD + K0 * SEQS
B_BV0, B_BO0, B_BIAS0, B_BV1, B_BO1, B_B2, B_G = 0, 128, 256, 288, 416, 544, 672
B_ALL = 680


def constants():
    c = np.zeros((P, C_ALL), np.float32)
    c[:, C_ID:C_ID + P] = np.eye(P)
    part = (np.arange(P) % 32) // HD
    c[:, C_SPLIT] = -1.0 * (part == 1)
    c[:, C_SPLIT + 1] = -1.0 * (part == 2)
    c[:, C_R8:C_R8 + T * 8] = np.arange(T * 8) % 8 > 0
    c[:, C_R16:C_R16 + T * E1] = np.arange(T * E1) % E1 > 0
    return c


def constants_layer0():
    c = np.zeros((P, L_ALL), np.float32)
    c[:, L_U:L_U + P] = np.triu(np.ones((P, P)), 1)
    c[:, L_ONE:L_ONE + P] = 1
    c[:, L_TRASH] = SLOTS + np.arange(P)
    c[:, L_START:L_START + E0] = np.arange(E0) * CAP
    c[:, L_R8:L_R8 + SEQS * 8] = np.arange(SEQS * 8) % 8 > 0
    c[:, L_R32:L_R32 + SEQS * E0] = np.arange(SEQS * E0) % E0 > 0
    c[:, L_R16T:L_R16T + SEQS * E0] = np.arange(SEQS * E0) % SEQS > 0
    c[:, L_SPREAD:L_SPREAD + K0 * SEQS] = np.arange(K0 * SEQS) * P
    return c


def selectors():
    s = np.zeros((E1, (NB1 - 1) * P), np.float32)
    for b in range(NB1 - 1):
        for p in range(P):
            s[2 * b + p // 64, b * P + p] = 1
    return s


def topk_mask(v, s, m8, k, mask, gt, eq, pre, count, reset):
    tiles, n = s.shape[1], s.shape[2]
    full = [P, tiles, n]
    for t in range(tiles):
        v.max(m8[:, t, :], s[:, t, :])
    v.drain()
    tau = m8[:, :, k - 1:k].to_broadcast(full)
    v.tensor_tensor(gt, s, tau, ALU.is_gt)
    v.tensor_tensor(eq, s, tau, ALU.is_equal)
    v.drain()
    v.reduce_sum(count, gt, axis=AX.X)
    v.tensor_tensor_scan(pre.rearrange("p t n -> p (t n)"), reset, eq.rearrange("p t n -> p (t n)"), 0.0,
                         ALU.mult, ALU.add)
    v.drain()
    v.tensor_tensor(pre, pre, count.unsqueeze(2).to_broadcast(full), ALU.add)
    v.drain()
    v.scalar_tensor_tensor(eq, pre, float(k) + 0.5, eq, ALU.is_lt, ALU.mult)
    v.drain()
    v.tensor_tensor(mask, gt, eq, ALU.add)
    v.drain()


def three_pass(pe, out, lh, ll, rh, rl, start=True, stop=True, skip=False):
    pe.matmul(out, lh, rl, start=start, stop=False, skip_group_check=skip)
    pe.matmul(out, ll, rh, start=False, stop=False, skip_group_check=skip)
    return pe.matmul(out, lh, rh, start=False, stop=stop, skip_group_check=skip)


class Norm:

    def __init__(self, k, name):
        self.k = k
        self.stats = k.sem(name + "_stats")
        self.eps = k.sem(name + "_eps")
        self.rstd = k.sem(name + "_rstd")
        self.ready = k.sem(name + "_ready")

    def vector(self, v, n, x):
        k = self.k
        for j in range(T):
            v.bn_stats(k.st6[:, j, :], x[j])
        v.drain()
        for j in range(T):
            last = v.bn_aggr(k.mv[:, j, :], k.st6[:, j, :])
        last.then_inc(self.stats, 1)
        v.wait_ge(self.rstd, n + 1)
        for j in range(T):
            last = v.tensor_scalar(k.xn[:, j, :], x[j], k.mv[:, j, 0:1], k.rs[:, j:j + 1],
                                   ALU.subtract, ALU.mult)
        last.then_inc(self.ready, 1)

    def pool(self, g, n):
        k = self.k
        g.wait_ge(self.stats, n + 1)
        g.tensor_tensor(k.ve[:], k.mv[:, :, 1], k.eps4[:], ALU.add).then_inc(self.eps, 1)
        g.wait_ge(self.eps, n + 1)
        g.tensor_tensor(k.rs[:], k.ve[:], k.mhalf[:], ALU.pow).then_inc(self.rstd, 1)


class Blocks:

    def __init__(self, k, name, gu, s, h, hh, hl):
        self.gu, self.s, self.h, self.hh, self.hl = gu, s, h, hh, hl
        self.gu_ready = k.sem(name + "_gu_ready")
        self.gu_free = k.sem(name + "_gu_free")
        self.silu = k.sem(name + "_silu")
        self.h_ready = k.sem(name + "_h_ready")
        self.hi = k.sem(name + "_hi")
        self.lo = k.sem(name + "_lo")
        self.h_free = k.sem(name + "_h_free")

    def credits(self, v):
        v.sem_inc(self.gu_free, len(self.gu))
        v.sem_inc(self.h_free, len(self.h))

    def tensor_gu(self, pe, a, g, wh, wl, g0, u0, m, xh, xl, back=2):
        w = xh.shape[1]
        pe.wait_ge(self.gu_free, a + 1 + len(self.gu) - back)
        for c0, bank in ((g0, 0), (u0, 1)):
            last = three_pass(pe, self.gu[g][bank][0:m, 0:w], wh[:, c0:c0 + m], wl[:, c0:c0 + m], xh, xl)
        last.then_inc(self.gu_ready, 1)

    def scalar_silu(self, act, a, g, m, w):
        act.wait_ge(self.gu_ready, a + 1)
        act.activation(self.s[g][0:m, 0:w], self.gu[g][0][0:m, 0:w], ACT.Silu).then_inc(self.silu, 1)

    def vector_h(self, v, a, g, h, m, w, back, weights=None, ready=None, free=None):
        v.wait_ge(self.h_free, a + 1 + len(self.h) - back)
        v.wait_ge(self.silu, a + 1)
        hid = self.h[h][0:m, 0:w]
        v.tensor_tensor(hid, self.s[g][0:m, 0:w], self.gu[g][1][0:m, 0:w], ALU.mult).then_inc(self.gu_free, 1)
        if weights is not None:
            v.drain()
            v.wait_ge(*ready)
            v.tensor_tensor(hid, hid, weights, ALU.mult).then_inc(free, 1)
        v.drain().then_inc(self.h_ready, 1)

    def scalar_hi(self, act, a, h, m, w):
        act.wait_ge(self.h_ready, a + 1)
        act.activation(self.hh[h][0:m, 0:w], self.h[h][0:m, 0:w], ACT.Copy).then_inc(self.hi, 1)

    def pool_lo(self, g, a, h, m, w):
        g.wait_ge(self.hi, a + 1)
        g.tensor_tensor(self.hl[h][0:m, 0:w], self.h[h][0:m, 0:w], self.hh[h][0:m, 0:w].bitcast(F32),
                        ALU.subtract).then_inc(self.lo, 1)

    def tensor_down(self, pe, a, h, m, tiles, out, w, wl, first, skip):
        pe.wait_ge(self.lo, a + 1)
        for j, (c0, c1) in enumerate(tiles):
            last = three_pass(pe, out(j), self.hh[h][0:m, c0:c1], self.hl[h][0:m, c0:c1], w, wl,
                              start=first and (j == 0 or not skip), stop=True, skip=skip)
        last.then_inc(self.h_free, 1)


def load_and_split(nc, k, name, jobs):
    loaded, hi, lo = [k.sem(f"{name}_loaded{i}") for i in range(2)], k.sem(name + "_hi"), k.sem(name + "_lo")

    raw = lambda i: k.raw[i % 2][0:jobs[i][0].shape[0], 0:jobs[i][0].shape[1]]

    def sync(sp):
        for i, (src, _, _) in enumerate(jobs):
            if i >= 2:
                sp.wait_ge(hi, i - 1)
                sp.wait_ge(lo, i - 1)
            sp.dma_start(raw(i), src).then_inc(loaded[i % 2], 16)

    def scalar(act):
        for i, (_, high, _) in enumerate(jobs):
            act.wait_ge(loaded[i % 2], 16 * (i // 2 + 1))
            act.activation(high, raw(i), ACT.Copy).then_inc(hi, 1)

    def vector(v):
        for i, (_, high, low) in enumerate(jobs):
            v.wait_ge(hi, i + 1)
            if low is None:
                v.drain().then_inc(lo, 1)
            else:
                v.tensor_tensor(low, raw(i), high.bitcast(F32), ALU.subtract).then_inc(lo, 1)

    return sync, scalar, vector


def setup(nc, k, d):
    s = Names(**{n: k.sem("setup_" + n) for n in (
        "loaded", "ctx", "zero", "tanh", "square", "norm", "cent", "centT", "gh", "csum", "rsum", "mix0", "mix1",
        "mix", "stored")})
    sync_w, scalar_w, vector_w = load_and_split(nc, k, "setup_w", [
        (d.w0[E0], k.sh0h[:], k.sh0l[:]), (d.l2w[:, 0:P], k.l2wh[:], k.l2wl[:])])
    loads = 8
    with nc.Block() as block:
        @block.sync
        def _(sp):
            sp.dma_start(k.x[:], d.x.rearrange("t p d -> p t d")).then_inc(s.loaded, 16)
            sp.dma_start(k.const[:], d.const[:, :]).then_inc(s.loaded, 16)
            sp.dma_start(k.const0[:], d.const0[:, :]).then_inc(s.loaded, 16)
            sp.dma_start(k.rows[:], d.rows[0, :].partition_broadcast(P)).then_inc(s.loaded, 16)
            sp.dma_start(k.wa0[:], d.wa0[:, :]).then_inc(s.loaded, 16)
            sp.dma_start(k.bcol[:], d.bcol[:, :]).then_inc(s.loaded, 16)
            sp.dma_start(k.cent[:], d.cent[:, :]).then_inc(s.loaded, 16)
            sp.dma_start(k.w2t[:], d.l2w[:, P:2 * P]).then_inc(s.loaded, 16)
            sp.dma_start(k.ctxT[:], d.ctxT[:, :]).then_inc(s.ctx, 16)
            sync_w(sp)
            sp.wait_ge(s.zero, 1)
            n = SLOTS // 8
            for i in range(8):
                sp.dma_start(d.buf[i * n:(i + 1) * n, :].rearrange("(p r) d -> p (r d)", p=P),
                             k.zero[:]).then_inc(s.stored, 16)
            sp.dma_start(d.oute[SLOTS:SLOTS + P, :], k.zero[:, 0:P]).then_inc(s.stored, 16)
            sp.wait_ge(s.mix, 1)
            sp.dma_start(d.mix[:, :], k.mix[:]).then_inc(s.stored, 16)
            sp.wait_ge(s.stored, 160)

        @block.gpsimd
        def _(g):
            g.memset(k.eps4[:], EPS)
            g.memset(k.mhalf[:], -0.5)
            g.drain()
            g.wait_ge(s.square, 1)
            g.tensor_tensor(k.cs[:, 2:3], k.cs[:, 1:2], k.mhalf[0:40, 0:1], ALU.pow).then_inc(s.norm, 1)

        @block.scalar
        def _(act):
            act.wait_ge(s.loaded, 16 * loads)
            act.activation(k.tg[:], k.rows[:, B_G:B_G + 8], ACT.Tanh).then_inc(s.tanh, 1)
            scalar_w(act)
            act.wait_ge(s.centT, 1)
            act.activation(k.g0h[:], k.ps[7][:, 0:40], ACT.Copy).then_inc(s.gh, 1)

        @block.vector
        def _(v):
            v.memset(k.zero[:], 0.0).then_inc(s.zero, 1)
            v.wait_ge(s.loaded, 16 * loads)
            v.wait_ge(s.tanh, 1)
            for b, g in ((B_BO0, 0), (B_BO1, 1)):
                v.tensor_scalar(k.rows[:, b:b + P], k.rows[:, b:b + P], k.tg[:, g:g + 1], None, ALU.mult)
            v.tensor_copy(k.ub[:], k.const0[:, L_U:L_U + 2 * P])
            v.tensor_tensor(k.junk[0:40, 0:P], k.cent[:], k.cent[:], ALU.mult)
            v.drain()
            v.reduce_sum(k.cs[:, 0:1], k.junk[0:40, 0:P], axis=AX.X)
            v.drain()
            v.tensor_scalar(k.cs[:, 1:2], k.cs[:, 0:1], 1e-24, None, ALU.max).then_inc(s.square, 1)
            v.wait_ge(s.norm, 1)
            v.tensor_scalar(k.cent[:], k.cent[:], k.cs[:, 2:3], None, ALU.mult).then_inc(s.cent, 1)
            v.wait_ge(s.ctx, 16)
            seqs = k.ctxT[:].rearrange("p (s t) -> p s t", t=P)
            v.reduce_sum(k.csum[:], seqs, axis=AX.X).then_inc(s.csum, 1)
            v.drain()
            v.scalar_tensor_tensor(k.ctxT[:], k.ctxT[:], 0.0, k.ctxT[:], ALU.max, ALU.mult)
            v.drain()
            v.reduce_sum(k.rsum[:], seqs, axis=AX.X).then_inc(s.rsum, 1)
            vector_w(v)
            v.wait_ge(s.gh, 1)
            v.tensor_tensor(k.g0l[:], k.ps[7][:, 0:40], k.g0h[:].bitcast(F32), ALU.subtract)
            v.wait_ge(s.mix0, 1)
            v.scalar_tensor_tensor(k.mix[:, 0:P], k.ps[6][0:SEQS, 0:P], 1.0 / P, k.rows[0:SEQS, B_B2:B_B2 + P],
                                   ALU.mult, ALU.add)
            v.wait_ge(s.mix1, 1)
            v.tensor_scalar(k.mix[:, P:2 * P], k.ps[5][0:SEQS, 0:P], k.tg[0:SEQS, 3:4], None, ALU.mult)
            v.drain()
            v.tensor_scalar(k.mix[:, 0:P], k.mix[:, 0:P], k.tg[0:SEQS, 2:3], None, ALU.mult).then_inc(s.mix, 1)

        @block.tensor
        def _(pe):
            pe.wait_ge(s.loaded, 16 * loads)
            pe.wait_ge(s.cent, 1)
            pe.transpose(k.ps[7][:, 0:40], k.cent[:], k.ident[0:40, 0:40]).then_inc(s.centT, 1)
            pe.wait_ge(s.csum, 1)
            pe.matmul(k.ps[6][0:SEQS, 0:P], k.csum[:], k.w2t[:], start=True, stop=True).then_inc(s.mix0, 1)
            pe.wait_ge(s.rsum, 1)
            pe.transpose(k.ps[5][0:SEQS, 0:P], k.rsum[:], k.ident).then_inc(s.mix1, 1)


def layer0_attention(nc, k, d):
    s = Names(**{n: k.sem("a0_" + n) for n in (
        "ctx_loaded", "ctx_free", "xT", "xTs", "qkv", "qk_read", "v_read", "scores", "centred", "exp", "probs",
        "pT", "pTs", "o", "os", "out", "fT", "hi", "lo", "square", "norm_max", "norm_inv", "logits",
        "logits_read", "copied", "done")})
    norm = Norm(k, "a0_norm")
    blocks = Blocks(k, "a0_blk", k.gu, k.s, k.h[0:2], k.hh[0:2], k.hl[0:2])
    pT, pQ, pK, pV = k.ps[4], k.ps[5], k.ps[6], k.ps[7]
    tile = [slice(j * P, (j + 1) * P) for j in range(T)]
    by_tile = lambda ps: ps[:].rearrange("p (t d) -> p t d", d=P)
    row = lambda b: k.rows[:, b:b + P].unsqueeze(1).to_broadcast([P, T, P])
    each = lambda col: col.unsqueeze(2).to_broadcast([P, T, P])
    with nc.Block() as block:
        @block.sync
        def _(sp):
            with sp.Fori(0, CHUNKS) as it:
                sp.wait_ge(s.ctx_free, it + 1)
                sp.dma_start(k.ctxr[:], d.ctxT[:, bass.ds(it * CW, CW)]).then_inc(s.ctx_loaded, 16)

        @block.gpsimd
        def _(g):
            with g.Fori(0, CHUNKS) as it:
                norm.pool(g, it * 2)
                norm.pool(g, it * 2 + 1)
                g.wait_ge(s.norm_max, it + 1)
                g.tensor_tensor(k.rn[:], k.ss2[:], k.mhalf[:], ALU.pow).then_inc(s.norm_inv, 1)
                g.tensor_copy(k.xn_all[:, bass.ds(it * T, T), :], k.xn[:]).then_inc(s.copied, 1)
                for n in range(2):
                    blocks.pool_lo(g, it * 2 + n, n, P, CW)

        @block.vector
        def _(v):
            v.sem_inc(s.ctx_free, 1)
            blocks.credits(v)
            with v.Fori(0, CHUNKS) as it:
                x = k.x[:, bass.ds(it * T, T), :]
                norm.vector(v, it * 2, [k.x[:, it * T + j, :] for j in range(T)])
                v.wait_ge(s.qkv, it + 1)
                v.tensor_tensor(k.v0[:], by_tile(pV), row(B_BV0), ALU.add).then_inc(s.v_read, 1)
                v.wait_ge(s.scores, it + 1)
                v.reduce_max(k.mx[:, 0:T], by_tile(pV), axis=AX.X)
                v.drain()
                v.tensor_tensor(k.pr[:], by_tile(pV), each(k.mx[:, 0:T]), ALU.subtract).then_inc(s.centred, 1)
                v.wait_ge(s.exp, it + 1)
                v.reduce_sum(k.mx[:, T:2 * T], k.pr[:], axis=AX.X)
                v.drain()
                v.reciprocal(k.mx[:, 2 * T:3 * T], k.mx[:, T:2 * T])
                v.drain()
                v.tensor_tensor(k.pr[:], k.pr[:], each(k.mx[:, 2 * T:3 * T]), ALU.mult).then_inc(s.probs, 1)
                v.tensor_tensor(x, x, row(B_BO0), ALU.add)
                v.drain()
                v.wait_ge(s.out, it + 1)
                v.scalar_tensor_tensor(x, by_tile(pK), k.tg[:, 0:1], x, ALU.mult, ALU.add)
                v.drain()
                norm.vector(v, it * 2 + 1, [k.x[:, it * T + j, :] for j in range(T)])
                v.wait_ge(s.hi, it + 1)
                v.tensor_tensor(k.xl[:], pT[:], k.xh[:].bitcast(F32), ALU.subtract).then_inc(s.lo, 1)
                v.wait_ge(s.square, it + 1)
                v.tensor_scalar(k.ss2[:], k.ss[:], 1e-24, None, ALU.max).then_inc(s.norm_max, 1)
                for n in range(2):
                    blocks.vector_h(v, it * 2 + n, n, n, P, CW, 2)
                v.wait_ge(s.norm_inv, it + 1)
                v.wait_ge(s.logits, it + 1)
                v.tensor_tensor(k.sc[:, bass.ds(it * T, T), :], pQ[:, 0:T * 40].rearrange("p (t n) -> p t n", n=40),
                                k.rn[:].unsqueeze(2).to_broadcast([P, T, 40]), ALU.mult).then_inc(s.logits_read, 1)
                v.wait_ge(blocks.h_free, it * 2 + 4)
                v.scalar_tensor_tensor(x, by_tile(pK), k.tg[:, 4:5], x, ALU.mult, ALU.add).then_inc(s.done, 1)
                v.drain()
                v.wait_ge(s.copied, it + 1)

        @block.scalar
        def _(act):
            with act.Fori(0, CHUNKS) as it:
                act.wait_ge(s.xT, it + 1)
                act.activation(k.xT[:], pT[:], ACT.Copy).then_inc(s.xTs, 1)
                act.wait_ge(s.qkv, it + 1)
                act.activation(k.qT[:], pQ[:], ACT.Identity, bias=k.bcol[:, 0:1])
                act.activation(k.kT[:], pK[:], ACT.Identity, bias=k.bcol[:, 1:2]).then_inc(s.qk_read, 1)
                act.wait_ge(s.centred, it + 1)
                act.activation(k.pr[:], k.pr[:], ACT.Exp, scale=float(P) ** -0.5).then_inc(s.exp, 1)
                act.wait_ge(s.pT, it + 1)
                act.activation(k.pT[:], pT[:], ACT.Copy).then_inc(s.pTs, 1)
                act.wait_ge(s.o, it + 1)
                act.activation(k.oT[:], pQ[:], ACT.Copy).then_inc(s.os, 1)
                act.wait_ge(norm.ready, it * 2 + 2)
                for j in range(T):
                    last = act.activation(k.junk[:, tile[j]], k.xn[:, j, :], ACT.Square, accum_out=k.ss[:, j:j + 1])
                last.then_inc(s.square, 1)
                act.wait_ge(s.fT, it + 1)
                act.activation(k.xh[:], pT[:], ACT.Copy).then_inc(s.hi, 1)
                for n in range(2):
                    blocks.scalar_silu(act, it * 2 + n, n, P, CW)
                for n in range(2):
                    blocks.scalar_hi(act, it * 2 + n, n, P, CW)

        @block.tensor
        def _(pe):
            with pe.Fori(0, CHUNKS) as it:
                pe.wait_ge(s.ctx_loaded, it * 16 + 16)
                pe.matmul(pK[:], k.wa0[:, P:2 * P], k.ctxr[:], start=True, stop=True)
                for j in range(T):
                    last = pe.matmul(pV[:, tile[j]], k.ctxr[:, tile[j]], k.wa0[:, 2 * P:3 * P], start=True, stop=True)
                last.then_inc(s.ctx_free, 1)
                pe.wait_ge(norm.ready, it * 2 + 1)
                for j in range(T):
                    last = pe.transpose(pT[:, tile[j]], k.xn[:, j, :], k.ident)
                last.then_inc(s.xT, 1)
                pe.wait_ge(s.xTs, it + 1)
                pe.matmul(pQ[:], k.wa0[:, 0:P], k.xT[:], start=True, stop=True).then_inc(s.qkv, 1)
                pe.wait_ge(s.v_read, it + 1)
                pe.wait_ge(s.qk_read, it + 1)
                for j in range(T):
                    last = pe.matmul(pV[:, tile[j]], k.qT[:, tile[j]], k.kT[:, tile[j]], start=True, stop=True)
                last.then_inc(s.scores, 1)
                pe.wait_ge(s.probs, it + 1)
                for j in range(T):
                    last = pe.transpose(pT[:, tile[j]], k.pr[:, j, :], k.ident)
                last.then_inc(s.pT, 1)
                pe.wait_ge(s.pTs, it + 1)
                for j in range(T):
                    last = pe.matmul(pQ[:, tile[j]], k.v0[:, j, :], k.pT[:, tile[j]], start=True, stop=True)
                last.then_inc(s.o, 1)
                pe.wait_ge(s.os, it + 1)
                for j in range(T):
                    last = pe.matmul(pK[:, tile[j]], k.oT[:, tile[j]], k.wa0[:, 3 * P:4 * P], start=True, stop=True)
                last.then_inc(s.out, 1)
                pe.wait_ge(norm.ready, it * 2 + 2)
                for j in range(T):
                    last = pe.transpose(pT[:, tile[j]], k.xn[:, j, :], k.ident)
                last.then_inc(s.fT, 1)
                pe.wait_ge(s.lo, it + 1)
                for n in range(2):
                    blocks.tensor_gu(pe, it * 2 + n, n, k.sh0h, k.sh0l, n * P, HID0 + n * P, P, k.xh[:], k.xl[:])
                for j in range(T):
                    last = three_pass(pe, pQ[:, j * 40:(j + 1) * 40], k.xh[:, tile[j]], k.xl[:, tile[j]],
                                      k.g0h[:], k.g0l[:])
                last.then_inc(s.logits, 1)
                for n in range(2):
                    w = slice(2 * HID0 + n * P, 2 * HID0 + (n + 1) * P)
                    blocks.tensor_down(pe, it * 2 + n, n, P, [(j * P, (j + 1) * P) for j in range(T)],
                                       lambda j: pK[:, tile[j]], k.sh0h[:, w], k.sh0l[:, w], n == 0, True)
                pe.wait_ge(s.logits_read, it + 1)
                pe.wait_ge(s.done, it + 1)


def layer0_route(nc, k, d):
    s = Names(**{n: k.sem("route_" + n) for n in ("centred", "exp", "mask", "ranks", "index", "sent", "split")})
    jobs = [(d.wa1[:, 4 * P:8 * P], k.wkh[:, 0:4 * P], k.wkl[:, 0:4 * P]),
            (d.wa1[:, 8 * P:9 * P], k.wkh[:, 4 * P:5 * P], k.wkl[:, 4 * P:5 * P]),
            (d.brow[:, 4 * P:8 * P], k.bkh[:], k.bkl[:])]
    for src, h, l in ((d.w1, k.w1h, k.w1l), (d.w2, k.w2h, k.w2l)):
        jobs += [(src[:, c:c + 864], h[:, c:c + 864], l[:, c:c + 864]) for c in range(0, NB1 * W1C, 864)]
    sync_w, scalar_w, vector_w = load_and_split(nc, k, "route_w", jobs)
    sync_k, scalar_k, vector_k, tensor_k = layer1_keys(nc, k, d)
    flat = lambda a: a.rearrange("p t n -> p (t n)")
    r = k.route
    full = [P, SEQS, E0]
    with nc.Block() as block:
        @block.sync
        def _(sp):
            sync_w(sp)
            sync_k(sp)

        @block.vector
        def _(v):
            g8 = r.gmask[:]
            topk_mask(v, k.sc[:, :, 0:G0], r.m8, K0, g8, r.t8a[:], r.t8b[:], r.t8c[:], r.cnt[:],
                      k.const0[:, L_R8:L_R8 + SEQS * G0])
            v.tensor_tensor(r.es[:], k.sc[:, :, G0:G0 + E0],
                            k.rows[:, B_BIAS0:B_BIAS0 + E0].unsqueeze(1).to_broadcast(full), ALU.add)
            v.tensor_scalar(r.t8a[:], g8, 1e9, -1e9, ALU.mult, ALU.add)
            v.drain()
            groups = r.es[:].rearrange("p t (g f) -> p (t g) f", f=E0 // G0)
            per_group = lambda a: flat(a).unsqueeze(2).to_broadcast([P, SEQS * G0, E0 // G0])
            v.tensor_tensor(groups, groups, per_group(g8), ALU.mult)
            v.drain()
            v.tensor_tensor(groups, groups, per_group(r.t8a[:]), ALU.add)
            v.drain()
            topk_mask(v, r.es[:], r.m8, K0, r.mask[:], r.gt[:], r.eq[:], r.pre[:], r.cnt[:],
                      k.const0[:, L_R32:L_R32 + SEQS * E0])
            v.tensor_copy(r.maskb[:], flat(r.mask[:])).then_inc(s.mask, 1)
            v.tensor_tensor(r.es[:], r.es[:], r.m8[:, :, 0:1].to_broadcast(full), ALU.subtract).then_inc(s.centred, 1)
            v.tensor_tensor_scan(flat(r.pre[:]), k.const0[:, L_R32:L_R32 + SEQS * E0], flat(r.mask[:]), 0.0,
                                 ALU.mult, ALU.add)
            v.drain()
            v.tensor_tensor(r.pre[:], r.pre[:], r.mask[:], ALU.mult)
            v.wait_ge(s.ranks, 1)
            v.tensor_copy(r.tot[:], k.ps[1][:].rearrange("p (t n) -> p n t", n=E0))
            v.drain()
            v.tensor_tensor_scan(flat(r.cum[:]), k.const0[:, L_R16T:L_R16T + SEQS * E0], flat(r.tot[:]), 0.0,
                                 ALU.mult, ALU.add)
            v.drain()
            v.tensor_tensor(r.cum[:], r.cum[:], r.tot[:], ALU.subtract)
            v.drain()
            v.tensor_tensor(r.slot[:], k.ps[0][:].rearrange("p (t n) -> p t n", n=E0),
                            r.cum[:].rearrange("p n t -> p t n"), ALU.add)
            v.drain()
            v.tensor_scalar(r.gt[:], r.slot[:], float(CAP), None, ALU.is_lt)
            v.tensor_tensor(r.slot[:], r.slot[:], k.const0[:, L_START:L_START + E0].unsqueeze(1).to_broadcast(full), ALU.add)
            v.drain()
            v.scalar_tensor_tensor(r.slot[:], r.slot[:], k.const0[:, L_TRASH:L_TRASH + 1], r.gt[:],
                                   ALU.subtract, ALU.mult)
            v.drain()
            for n in range(K0):
                v.scalar_tensor_tensor(r.eq[:], r.pre[:], n + 1.0, r.slot[:], ALU.is_equal, ALU.mult)
                v.drain()
                v.reduce_sum(r.sl[:, n, :], r.eq[:], axis=AX.X)
                v.drain()
            sl = r.sl[:].rearrange("p k t -> p (k t)")
            v.tensor_scalar(k.index[:], sl, k.const0[:, L_TRASH:L_TRASH + 1], None, ALU.add)
            v.scalar_tensor_tensor(r.own[:], sl, 0.0, k.const0[:, L_SPREAD:L_SPREAD + K0 * SEQS], ALU.is_equal, ALU.mult)
            v.drain()
            v.scalar_tensor_tensor(r.dest[:], sl, k.const0[:, L_TRASH:L_TRASH + 1], r.own[:], ALU.add, ALU.add)\
                .then_inc(s.index, 1)
            v.wait_ge(s.exp, 1)
            v.tensor_tensor(r.es[:], r.es[:], r.mask[:], ALU.mult)
            v.drain()
            v.reduce_sum(r.cnt[:], r.es[:], axis=AX.X)
            v.drain()
            v.reciprocal(r.rec[:], r.cnt[:])
            v.tensor_tensor(r.es[:], r.es[:], r.gt[:], ALU.mult)
            v.drain()
            v.tensor_scalar(r.rec[:], r.rec[:], k.tg[:, 4:5], None, ALU.mult)
            v.drain()
            v.tensor_tensor(r.es[:], r.es[:], r.rec[:].unsqueeze(2).to_broadcast(full), ALU.mult)
            v.drain()
            for n in range(K0):
                v.scalar_tensor_tensor(r.eq[:], r.pre[:], n + 1.0, r.es[:], ALU.is_equal, ALU.mult)
                v.drain()
                v.reduce_sum(k.gate[:, n, :], r.eq[:], axis=AX.X)
                v.drain()
            vector_w(v)
            v.drain().then_inc(s.split, 1)
            vector_k(v)

        @block.scalar
        def _(act):
            act.wait_ge(s.centred, 1)
            act.activation(r.es[:], r.es[:], ACT.Exp).then_inc(s.exp, 1)
            act.activation(k.one_r[:], k.const0[0:1, L_ONE:L_ONE + P], ACT.Copy)
            scalar_w(act)
            scalar_k(act)

        @block.tensor
        def _(pe):
            pe.wait_ge(s.mask, 1)
            pe.matmul(k.ps[0][:], k.ub[:, 0:P], r.maskb[:], start=True, stop=True)
            pe.matmul(k.ps[1][:], k.ub[:, P:2 * P], r.maskb[:], start=True, stop=True).then_inc(s.ranks, 1)
            pe.wait_ge(s.split, 1)
            tensor_k(pe)

        @block.gpsimd
        def _(g):
            g.wait_ge(s.index, 1)
            for n in range(K0):
                for t in range(SEQS):
                    c = n * SEQS + t
                    g.indirect_dma_start(
                        out=d.buf[:, :], out_offset=bass.IndirectOffsetOnAxis(ap=r.dest[:, c:c + 1].bitcast(U32), axis=0),
                        in_=k.xn_all[:, t, :], in_offset=None).then_inc(s.sent, 16)
            g.wait_ge(s.sent, 16 * K0 * SEQS)


def layer0_experts(nc, k, d):
    s = Names(**{n: k.sem("ex_" + n) for n in (
        "gu0", "gu1", "dn0", "dn1", "rows0", "rows1", "gu_free", "dn_free", "rows_free", "gu_split", "dn_split",
        "turned", "x_hi", "x_lo", "out_sb", "stored0", "stored1")})
    raw_gu, raw_dn, rows, stored = (s.gu0, s.gu1), (s.dn0, s.dn1), (s.rows0, s.rows1), (s.stored0, s.stored1)
    e_ = k.ex
    blocks = Blocks(k, "ex_blk", k.gu, k.s, e_.h, e_.hh, e_.hl)
    pX, pO = (k.ps[4], k.ps[7]), (k.ps[5], k.ps[6])
    starts = [j * RT for j in range(3)]
    tiles = [(c, c + m) for c, m in zip(starts, ROWS)]
    last = E0 - 1

    def experts(i, first):
        return [(i * 2 + first, i, first), (i * 2 + first + 1, i + (first + 1) // 2, (first + 1) % 2)]

    with nc.Block() as block:
        @block.sync
        def _(sp):
            def load(e, half, q):
                sp.wait_ge(s.gu_free, e + 1)
                sp.dma_start(e_.raw_gu[q][:], d.w0[e, :, 0:2 * HID0]).then_inc(raw_gu[q], 16)
                sp.wait_ge(s.rows_free, e + 1)
                sp.dma_start(e_.rows[q][0:RT, 0:2, :],
                             d.buf[bass.ds(e * CAP, 2 * RT), :].rearrange("(r p) d -> p r d", p=RT)).then_inc(rows[q], 16)
                sp.dma_start(e_.rows[q][0:ROWS[2], 2, :],
                             d.buf[bass.ds(e * CAP + 2 * RT, ROWS[2]), :]).then_inc(rows[q], 16)
                sp.wait_ge(s.dn_free, e + 1)
                sp.dma_start(e_.raw_dn[q][:], d.w0[e, :, 2 * HID0:3 * HID0]).then_inc(raw_dn[q], 16)

            def store(e, half, q):
                sp.wait_ge(s.out_sb, e + 3)
                sp.dma_start(d.oute[bass.ds(e * CAP, 2 * RT), :].rearrange("(r p) d -> p r d", p=RT),
                             e_.out[q][0:RT, 0:2, :]).then_inc(stored[q], 16)
                sp.dma_start(d.oute[bass.ds(e * CAP + 2 * RT, ROWS[2]), :],
                             e_.out[q][0:ROWS[2], 2, :]).then_inc(stored[q], 16)

            for e in range(4):
                load(e, e // 2, e % 2)
            with sp.Fori(0, E0 // 2 - 2) as i:
                for e, half, q in experts(i, 0):
                    load(e + 4, half + 2, q)
                    store(e, half, q)
            for e in range(E0 - 4, E0):
                store(e, e // 2, e % 2)
            for q in range(2):
                sp.wait_ge(stored[q], 1 + 16 * E0)

        @block.gpsimd
        def _(g):
            with g.Fori(0, E0 // 2) as i:
                for e, half, q in experts(i, 0):
                    for n in range(2):
                        blocks.pool_lo(g, e * 2 + n, 2 * q + n, P, CAP)

        @block.vector
        def _(v):
            def split(e, half, q, raw, loaded, hi, lo, done, free):
                v.wait_ge(loaded, half * 16 + 16)
                v.tensor_copy(hi[:], raw[:])
                v.drain()
                v.tensor_tensor(lo[:], raw[:], hi[:].bitcast(F32), ALU.subtract).then_inc(done, 1)
                v.drain().then_inc(free, 1)

            def split_gu(e, half, q, used=True):
                if used:
                    v.wait_ge(blocks.gu_ready, e * 2 - 2)
                split(e, half, q, e_.raw_gu[q], raw_gu[q], e_.guh[q], e_.gul[q], s.gu_split, s.gu_free)

            def split_dn(e, half, q):
                v.wait_ge(blocks.h_free, e * 2 + 2)
                split(e, half, q, e_.raw_dn[q], raw_dn[q], e_.dnh[q], e_.dnl[q], s.dn_split, s.dn_free)

            def x_low(e, half, q):
                v.wait_ge(s.x_hi, e + 1)
                v.tensor_tensor(e_.xl[q][:], pX[q][:, 0:CAP], e_.xh[q][:].bitcast(F32), ALU.subtract).then_inc(s.x_lo, 1)
                v.drain().then_inc(s.rows_free, 1)

            def turn(e, half, q, gu=True, more=True):
                for n in range(2):
                    blocks.vector_h(v, e * 2 + n, n, 2 * q + n, P, CAP, 4)
                if more:
                    x_low(e + 1, half + q, 1 - q)
                if gu:
                    split_gu(e + 2, half + 1, q)
                if more:
                    split_dn(e + 1, half + q, 1 - q)

            blocks.credits(v)
            for sem in (s.gu_free, s.dn_free, s.rows_free, s.out_sb):
                v.sem_inc(sem, 2)
            for q in range(2):
                v.sem_inc(stored[q], 1)
            split_gu(0, 0, 0, used=False)
            x_low(0, 0, 0)
            split_gu(1, 0, 1, used=False)
            split_dn(0, 0, 0)
            with v.Fori(0, E0 // 2 - 1) as i:
                for e, half, q in experts(i, 0):
                    turn(e, half, q)
            turn(last - 1, last // 2, 0, gu=False)
            turn(last, last // 2, 1, gu=False, more=False)

        @block.scalar
        def _(act):
            def x_high(e, q):
                act.wait_ge(s.turned, e + 1)
                act.activation(e_.xh[q][:], pX[q][:, 0:CAP], ACT.Copy).then_inc(s.x_hi, 1)

            def out(e, half, q):
                act.wait_ge(blocks.h_free, e * 2 + 6)
                act.wait_ge(stored[q], half * 32 + 1)
                act.activation(e_.out[q][0:RT, 0:2, :], pO[q][0:RT, 0:2 * P].rearrange("p (r d) -> p r d", d=P), ACT.Copy)
                act.activation(e_.out[q][0:ROWS[2], 2, :], pO[q][0:ROWS[2], 2 * P:3 * P], ACT.Copy)
                act.drain().then_inc(s.out_sb, 1)

            def turn(e, half, q, x=True, before=None):
                for n in range(2):
                    blocks.scalar_silu(act, e * 2 + n, n, P, CAP)
                if x:
                    x_high(e + 1, 1 - q)
                for n in range(2):
                    blocks.scalar_hi(act, e * 2 + n, 2 * q + n, P, CAP)
                if before is not None:
                    out(*before)

            x_high(0, 0)
            turn(0, 0, 0)
            with act.Fori(0, E0 // 2 - 1) as i:
                for e, half, q in experts(i, 1):
                    turn(e, half, q, before=(e - 1, half if q else half - 1, 1 - q))
            turn(last, last // 2, 1, x=False, before=(last - 1, last // 2, 0))
            out(last, last // 2, 1)

        @block.tensor
        def _(pe):
            def rows_turned(e, half, q):
                pe.wait_ge(rows[q], half * 32 + 32)
                for j, m in enumerate(ROWS):
                    last = pe.transpose(pX[q][:, starts[j]:starts[j] + m], e_.rows[q][0:m, j, :], k.ident[0:m, 0:m])
                last.then_inc(s.turned, 1)

            def gate_up(e, half, q):
                pe.wait_ge(s.gu_split, e + 1)
                pe.wait_ge(s.x_lo, e + 1)
                for n in range(2):
                    blocks.tensor_gu(pe, e * 2 + n, n, e_.guh[q], e_.gul[q], n * P, HID0 + n * P, P, e_.xh[q][:], e_.xl[q][:])

            def down(e, half, q):
                pe.wait_ge(s.dn_split, e + 1)
                pe.wait_ge(s.out_sb, e + 1)
                for n in range(2):
                    w = slice(n * P, (n + 1) * P)
                    blocks.tensor_down(pe, e * 2 + n, 2 * q + n, P, tiles,
                                       lambda j: pO[q][0:ROWS[j], j * P:(j + 1) * P],
                                       e_.dnh[q][:, w], e_.dnl[q][:, w], n == 0, True)

            rows_turned(0, 0, 0)
            gate_up(0, 0, 0)
            rows_turned(1, 0, 1)
            with pe.Fori(0, E0 // 2 - 1) as i:
                for e, half, q in experts(i, 1):
                    gate_up(e, half, q)
                    rows_turned(e + 1, half + q, 1 - q)
                    down(e - 1, half if q else half - 1, 1 - q)
            gate_up(last, last // 2, 1)
            down(last - 1, last // 2, 0)
            down(last, last // 2, 1)


def layer0_combine(nc, k, d):
    RING = 16
    got = [k.sem(f"comb_got{i}") for i in range(4)]
    used = k.sem("comb_used")
    jobs = [(d.w3[e], k.w3h[:, e * W3C:(e + 1) * W3C], k.w3l[:, e * W3C:(e + 1) * W3C]) for e in range(E3 + 1)]
    jobs += [(d.wa1[:, 0:4 * P], k.wa1h[:, 0:4 * P], k.wa1l[:, 0:4 * P]),
             (d.wa1[:, 9 * P:10 * P], k.wa1h[:, 4 * P:5 * P], k.wa1l[:, 4 * P:5 * P]),
             (d.gates, k.gth[:], k.gtl[:]), (d.sel, k.selh[:], None), (d.brow[:, 0:4 * P], k.bqh[:], k.bql[:])]
    sync_w, scalar_w, vector_w = load_and_split(nc, k, "comb_w", jobs)
    with nc.Block() as block:
        @block.sync
        def _(sp):
            sync_w(sp)

        @block.scalar
        def _(act):
            scalar_w(act)

        @block.gpsimd
        def _(g):
            for i in range(SEQS * K0):
                t, n = divmod(i, K0)
                if i >= RING and i % 4 == 0:
                    g.wait_ge(used, (i - RING) // 4 + 1)
                c = n * SEQS + t
                g.indirect_dma_start(
                    out=k.y[:, i % RING, :], out_offset=None, in_=d.oute[:, :],
                    in_offset=bass.IndirectOffsetOnAxis(ap=k.index[:, c:c + 1].bitcast(U32), axis=0)).then_inc(got[t % 4], 16)

        @block.vector
        def _(v):
            vector_w(v)
            for t in range(SEQS):
                v.wait_ge(got[t % 4], 16 * K0 * (t // 4 + 1))
                for n in range(K0):
                    v.scalar_tensor_tensor(k.x[:, t, :], k.y[:, (t * K0 + n) % RING, :], k.gate[:, n, t:t + 1],
                                           k.x[:, t, :], ALU.mult, ALU.add)
                    last = v.drain()
                last.then_inc(used, 1)


def layer1_keys(nc, k, d):
    s = Names(**{n: k.sem("key_" + n) for n in ("loaded", "free", "hi", "lo", "kv", "high", "done", "stored")})

    def sync(sp):
        with sp.Fori(0, SEQS) as i:
            sp.wait_ge(s.free, i + 1)
            sp.dma_start(k.ctx1[:], d.ctxT[:, bass.ds(i * P, P)]).then_inc(s.loaded, 16)
            sp.wait_ge(s.done, i + 1)
            sp.dma_start(d.keys1[i, :, :], k.k3[:].bitcast(F32)).then_inc(s.stored, 16)
            sp.dma_start(d.values1[i, :, :], k.v9k[:].rearrange("p h d -> p (h d)")).then_inc(s.stored, 16)
        sp.wait_ge(s.stored, SEQS * 32 + 1)

    def scalar(act):
        with act.Fori(0, SEQS) as i:
            act.wait_ge(s.loaded, i * 16 + 16)
            act.activation(k.cth[:], k.ctx1[:], ACT.Copy).then_inc(s.hi, 1)
            act.wait_ge(s.kv, i + 1)
            act.activation(k.kh[:], k.ps[2][:], ACT.Copy).then_inc(s.high, 1)

    def vector(v):
        v.memset(k.v9k[:], 1.0)
        v.sem_inc(s.free, 1)
        v.sem_inc(s.stored, 1)
        v.drain()
        with v.Fori(0, SEQS) as i:
            v.wait_ge(s.hi, i + 1)
            v.tensor_tensor(k.ctl[:], k.ctx1[:], k.cth[:].bitcast(F32), ALU.subtract).then_inc(s.lo, 1)
            v.drain().then_inc(s.free, 1)
            v.wait_ge(s.high, i + 1)
            v.wait_ge(s.stored, i * 32 + 1)
            v.scalar_tensor_tensor(k.k3[:], k.kh[:].bitcast(F32), k.const[:, C_SPLIT + 1:C_SPLIT + 2], k.ps[2][:],
                                   ALU.mult, ALU.add)
            v.tensor_tensor(k.v9k[:, :, 0:HD], k.ps[3][:, 0:P].rearrange("p (h d) -> p h d", d=HD),
                            k.rows[:, B_BV1:B_BV1 + P].rearrange("p (h d) -> p h d", d=HD), ALU.add)
            v.drain().then_inc(s.done, 1)

    def tensor(pe):
        with pe.Fori(0, SEQS) as i:
            pe.wait_ge(s.lo, i + 1)
            for q in range(4):
                c = slice(q * P, (q + 1) * P)
                three_pass(pe, k.ps[2][:, c], k.wkh[:, c], k.wkl[:, c], k.cth[:], k.ctl[:], stop=False)
                pe.matmul(k.ps[2][:, c], k.bkh[:, c], k.one_r[:], start=False, stop=False)
                pe.matmul(k.ps[2][:, c], k.bkl[:, c], k.one_r[:], start=False, stop=True)
            three_pass(pe, k.ps[3][:, 0:P], k.cth[:], k.ctl[:], k.wkh[:, 4 * P:5 * P], k.wkl[:, 4 * P:5 * P])\
                .then_inc(s.kv, 1)
            pe.wait_ge(s.done, i + 1)

    return sync, scalar, vector, tensor


def layer0_experts_all(nc, k, d, sb):
    with ExitStack() as rt:
        r = k.route = Names()
        r.m8 = sb("r_m8", [P, SEQS, 8], c=rt)
        r.gmask, r.t8a, r.t8b, r.t8c = (sb("r_" + n, [P, SEQS, 8], c=rt) for n in ("gmask", "t8a", "t8b", "t8c"))
        r.cnt, r.rec = sb("r_cnt", [P, SEQS], c=rt), sb("r_rec", [P, SEQS], c=rt)
        r.sl, r.own = sb("r_sl", [P, K0, SEQS], c=rt), sb("r_own", [P, K0 * SEQS], c=rt)
        r.dest = sb("r_dest", [P, K0 * SEQS], I32, rt)
        r.es, r.mask, r.gt, r.eq, r.pre, r.slot = (
            sb("r_" + n, [P, SEQS, E0], c=rt) for n in ("es", "mask", "gt", "eq", "pre", "slot"))
        r.tot, r.cum = sb("r_tot", [P, E0, SEQS], c=rt), sb("r_cum", [P, E0, SEQS], c=rt)
        r.maskb = sb("r_maskb", [P, SEQS * E0], BF16, rt)
        k.wkh, k.wkl = sb("wkh", [P, 5 * P], F32R, rt), sb("wkl", [P, 5 * P], F32R, rt)
        k.bkh, k.bkl = sb("bkh", [1, 4 * P], F32R, rt), sb("bkl", [1, 4 * P], F32R, rt)
        k.ctx1 = sb("ctx1", [P, P], c=rt)
        k.cth, k.ctl = sb("cth", [P, P], F32R, rt), sb("ctl", [P, P], F32R, rt)
        k.kh, k.k3 = sb("kh", [P, 4 * P], F32R, rt), sb("k3", [P, 4 * P], F32R, rt)
        k.v9k = sb("v9k", [P, HEADS, HD + 1], c=rt)
        layer0_route(nc, k, d)
    with ExitStack() as ex:
        e = k.ex = Names()
        two = lambda name, shape, dt=F32: [sb(f"e_{name}{i}", shape, dt, ex) for i in range(2)]
        e.raw_gu, e.raw_dn, e.rows = two("rgu", [P, 2 * HID0]), two("rdn", [P, HID0]), two("rows", [P, 3, P])
        e.guh, e.gul = two("guh", [P, 2 * HID0], F32R), two("gul", [P, 2 * HID0], F32R)
        e.dnh, e.dnl = two("dnh", [P, HID0], F32R), two("dnl", [P, HID0], F32R)
        e.xh, e.xl = two("xh", [P, CAP], F32R), two("xl", [P, CAP], F32R)
        e.out = two("out", [P, 3, P])
        e.h = [sb(f"e_h{i}", [P, CAP], c=ex) for i in range(4)]
        e.hh = [sb(f"e_hh{i}", [P, CAP], F32R, ex) for i in range(4)]
        e.hl = [sb(f"e_hl{i}", [P, CAP], F32R, ex) for i in range(4)]
        layer0_experts(nc, k, d)


class Gate:

    def __init__(self, k, norm):
        self.k, self.norm = k, norm
        (self.turned, self.hi, self.lo, self.logits, self.act, self.centred, self.ready, self.wT, self.wT_hi,
         self.wT_lo) = (k.sem("gate_" + n) for n in (
            "turned", "hi", "lo", "logits", "act", "centred", "ready", "wT", "wT_hi", "wT_lo"))
        self.n = (E1, E1, E3)
        self.c0 = (0, E1, 2 * E1)

    def tensor(self, pe, it, l, norm_at):
        k, a, n, c0 = self.k, it * 3 + l, self.n[l], self.c0[l]
        pe.wait_ge(self.norm.ready, norm_at + 1)
        for j in range(T):
            last = pe.transpose(k.ps[4][:, j * P:(j + 1) * P], k.xn[:, j, :], k.ident)
        last.then_inc(self.turned, 1)
        pe.wait_ge(self.lo, a + 1)
        for j in range(T):
            c = slice(j * P, (j + 1) * P)
            last = three_pass(pe, k.ps[7][:, j * n:(j + 1) * n], k.xh[:, c], k.xl[:, c],
                              k.gth[:, c0:c0 + n], k.gtl[:, c0:c0 + n])
        last.then_inc(self.logits, 1)

    def tensor_weights(self, pe, it, l):
        k, a = self.k, it * 2 + l
        pe.wait_ge(self.ready, it * 3 + l + 1)
        for j in range(T):
            last = pe.transpose(k.ps[4][0:E1, j * P:(j + 1) * P], k.c16[:, j, :], k.ident)
        last.then_inc(self.wT, 1)
        pe.wait_ge(self.wT_lo, a + 1)

    def scalar(self, act, it, l):
        k, a, n = self.k, it * 3 + l, self.n[l]
        act.wait_ge(self.turned, a + 1)
        act.activation(k.xh[:], k.ps[4][:], ACT.Copy).then_inc(self.hi, 1)
        if l == 0:
            act.wait_ge(self.logits, a + 1)
            act.activation(k.sg[:], k.ps[7][:, 0:T * n].rearrange("p (t n) -> p t n", n=n), ACT.Sigmoid).then_inc(self.act, 1)
        else:
            act.wait_ge(self.centred, it * 2 + l)
            sg = k.sg[:, :, 0:n]
            act.activation(sg, sg, ACT.Exp).then_inc(self.act, 1)
        if l < 2:
            act.wait_ge(self.wT, it * 2 + l + 1)
            act.activation(k.wTh, k.ps[4][0:E1, :], ACT.Copy).then_inc(self.wT_hi, 1)

    def vector(self, v, it, l):
        k, a, n = self.k, it * 3 + l, self.n[l]
        v.wait_ge(self.hi, a + 1)
        v.tensor_tensor(k.xl[:], k.ps[4][:], k.xh[:].bitcast(F32), ALU.subtract).then_inc(self.lo, 1)
        sg = k.sg[:, :, 0:n]
        each = lambda c: c.unsqueeze(2).to_broadcast([P, T, n])
        if l == 0:
            v.wait_ge(self.act, a + 1)
        else:
            lg = k.ps[7][:, 0:T * n].rearrange("p (t n) -> p t n", n=n)
            v.wait_ge(self.logits, a + 1)
            v.reduce_max(k.r1[:], lg, axis=AX.X)
            v.drain()
            v.tensor_tensor(sg, lg, each(k.r1[:]), ALU.subtract).then_inc(self.centred, 1)
            v.wait_ge(self.act, a + 1)
            v.reduce_sum(k.r1[:], sg, axis=AX.X)
            v.drain()
            v.reciprocal(k.r2[:], k.r1[:])
            v.drain()
            v.tensor_tensor(sg, sg, each(k.r2[:]), ALU.mult)
            v.drain()
        if l < 2:
            g4 = k.sg[:].rearrange("p t (g f) -> p (t g) f", f=4)
            if l == 0:
                for n0, n1, f0, f1, g0 in ((0, 3, 0, 3, 1), (3, 5, 0, 2, 2), (5, 6, 0, 1, 3)):
                    v.tensor_tensor(k.pairs[:, :, n0:n1], g4[:, :, f0:f1], g4[:, :, g0:g0 + f1 - f0], ALU.add)
                v.drain()
                v.reduce_max(k.g8[:, :, 0:4], k.pairs[:].rearrange("p (t g) f -> p t g f", g=4), axis=AX.X)
            else:
                v.reduce_max(k.g8[:, :, 0:4], k.sg[:].rearrange("p t (g f) -> p t g f", f=4), axis=AX.X)
            v.drain()
            topk_mask(v, k.g8[:], k.m8[:], 2, k.gm[:], k.q8[0][:], k.q8[1][:], k.q8[2][:], k.r1[:], k.const[:, C_R8:C_R8 + T * 8])
            inner = lambda x: x.unsqueeze(3).to_broadcast([P, T, 4, 4])
            ms = k.ms[:].rearrange("p t (g f) -> p t g f", f=4)
            v.tensor_tensor(ms, k.sg[:].rearrange("p t (g f) -> p t g f", f=4), inner(k.gm[:, :, 0:4]), ALU.mult)
            if l == 0:
                v.drain()
                v.tensor_scalar(k.gm[:], k.gm[:], 2.0, -2.0, ALU.mult, ALU.add)
                v.drain()
                v.tensor_tensor(ms, ms, inner(k.gm[:, :, 0:4]), ALU.add)
            v.drain()
            topk_mask(v, k.ms[:], k.m8[:], K1, k.mask[:], k.q16[0][:], k.q16[1][:], k.q16[2][:], k.r1[:],
                      k.const[:, C_R16:C_R16 + T * E1])
            mask, c = k.mask[:], k.c16[:]
        else:
            topk_mask(v, k.sg[:, :, 0:E3], k.m8[:], K3, k.gm[:], k.q8[0][:], k.q8[1][:], k.q8[2][:], k.r1[:],
                      k.const[:, C_R8:C_R8 + T * 8])
            mask, c = k.gm[:], k.c8[:]
        v.tensor_tensor(c, mask, sg, ALU.mult)
        if l != 1:
            v.drain()
            v.reduce_sum(k.r1[:], c, axis=AX.X)
            v.drain()
            v.tensor_scalar(k.r1[:], k.r1[:], 1e-6 if l == 0 else 1e-20, None, ALU.add)
            v.drain()
            v.reciprocal(k.r2[:], k.r1[:])
            v.drain()
            v.tensor_tensor(c, c, each(k.r2[:]), ALU.mult)
        v.drain().then_inc(self.ready, 1)
        if l < 2:
            v.wait_ge(self.wT_hi, it * 2 + l + 1)
            v.tensor_tensor(k.wTl, k.ps[4][0:E1, :], k.wTh.bitcast(F32), ALU.subtract).then_inc(self.wT_lo, 1)


def later_layers(nc, k, d, stop):
    names = ("kv_free", "mixed_loaded", "mix_free", "q", "q_hi", "q3", "scores", "centred", "exp", "turned", "taken",
             "e_free", "pv", "pv_read", "oT", "o_hi", "o_lo", "out", "l2", "xT2", "x2_hi", "x2_lo",
             "cb", "cb_free", "sum", "sum_read", "done", "stored")
    s = Names(**{n: k.sem("m_" + n) for n in names})
    k_loaded = [k.sem(f"m_k_loaded{i}") for i in range(2)]
    norm = Norm(k, "m_norm")
    gate = Gate(k, norm)
    blocks = Blocks(k, "m_blk", k.gu, k.s, k.h, k.hh, k.hl)
    NB = 2 * NB1 + 3 * (E3 + 1)
    tile = [slice(j * P, (j + 1) * P) for j in range(T)]
    chunk_tiles = [(j * P, (j + 1) * P) for j in range(T)]
    by_tile = lambda ps: ps.rearrange("p (t d) -> p t d", d=P)
    row = lambda b: k.rows[:, b:b + P].unsqueeze(1).to_broadcast([P, T, P])
    gback = lambda n: 2 if n >= 2 else (1, 3)[n]
    b3 = [(e, m) for e in range(E3 + 1) for m in range(3)]
    SUM = (k.ps[6], k.ps[7])

    with nc.Block() as block:
        @block.sync
        def _(sp):
            with sp.Fori(0, CHUNKS) as it:
                for j in range(T):
                    a = it * T + j
                    sp.wait_ge(s.kv_free, a + 1)
                    sp.dma_start(k.k3m[j % 2][:].bitcast(F32), d.keys1[a, :, :]).then_inc(k_loaded[j % 2], 16)
                    sp.dma_start(k.v9[j % 2][:].rearrange("p h d -> p (h d)"), d.values1[a, :, :]).then_inc(k_loaded[j % 2], 16)
                    if j == 0:
                        sp.wait_ge(s.mix_free, it + 1)
                        for t in range(T):
                            sp.dma_start(k.mixr[:, t, :], d.mix[it * T + t, :].partition_broadcast(P)).then_inc(s.mixed_loaded, 16)
                sp.wait_ge(s.done, it + 1)
                sp.dma_start(d.out[bass.ds(it * T, T), :, :].rearrange("t p d -> p t d"),
                             k.x[:, bass.ds(it * T, T), :]).then_inc(s.stored, 16)
            sp.wait_ge(s.stored, 16 * CHUNKS)

        @block.gpsimd
        def _(g):
            with g.Fori(0, CHUNKS) as it:
                for n in range(6):
                    norm.pool(g, it * 6 + n)
                    if n == 1:
                        for b in range(NB1):
                            blocks.pool_lo(g, it * NB + b, b % 3, P, CW)
                    if n == 3:
                        for b in range(NB1, 2 * NB1):
                            blocks.pool_lo(g, it * NB + b, b % 3, P, CW)
                    if n == 5:
                        for i, (e, m) in enumerate(b3):
                            blocks.pool_lo(g, it * NB + 2 * NB1 + i, i % 3, M3[m], CW)

        @block.vector
        def _(v):
            def experts(it, l):
                for b in range(NB1):
                    n = l * NB1 + b
                    c = it * 2 * (NB1 - 1) + l * (NB1 - 1) + b
                    w = dict(weights=k.ps[5][:], ready=(s.cb, c + 1), free=s.cb_free) if b < NB1 - 1 else {}
                    blocks.vector_h(v, it * NB + n, n % 2, n % 3, P, CW, 3, **w)

            def add(x, ps, col):
                v.scalar_tensor_tensor(x, by_tile(ps), k.tg[:, col:col + 1], x, ALU.mult, ALU.add)
                v.drain()

            v.sem_inc(s.kv_free, 2)
            v.sem_inc(s.mix_free, 1)
            v.sem_inc(s.cb_free, 1)
            v.sem_inc(s.e_free, 1)
            blocks.credits(v)
            v.memset(k.g8[:], -3e38)
            v.drain()
            with v.Fori(0, CHUNKS) as it:
                x = k.x[:, bass.ds(it * T, T), :]
                xs = [k.x[:, it * T + j, :] for j in range(T)]
                norm.vector(v, it * 6, xs)
                v.wait_ge(s.x2_hi, it * 2 + 1)
                v.tensor_tensor(k.xl[:], k.ps[4][:], k.xh[:].bitcast(F32), ALU.subtract).then_inc(s.x2_lo, 1)
                v.tensor_tensor(x, x, row(B_BO1), ALU.add)
                v.memset(k.o[:], 0.0)

                def q3(j):
                    v.wait_ge(s.q_hi, it * T + j + 1)
                    v.scalar_tensor_tensor(k.q3[j % 2][:], k.qh[:].bitcast(F32), k.const[:, C_SPLIT:C_SPLIT + 1], k.ps[6][:],
                                           ALU.mult, ALU.add)
                    v.drain().then_inc(s.q3, 1)

                def normalize(j):
                    a = it * T + j
                    pv = k.ps[7][:, 0:HEADS * (HD + 1)].rearrange("p (h d) -> p h d", d=HD + 1)
                    v.wait_ge(s.pv, a + 1)
                    v.tensor_copy(k.den[:], pv[:, :, HD])
                    v.drain()
                    v.tensor_tensor(k.good[:], k.den[:], k.den[:], ALU.is_equal)
                    v.reciprocal(k.rec[:], k.den[:])
                    v.drain()
                    v.tensor_tensor(k.ot[:], pv[:, :, 0:HD], k.rec[:].unsqueeze(2).to_broadcast([P, HEADS, HD]), ALU.mult)
                    v.drain()
                    v.copy_predicated(k.o[:, j, :].rearrange("p (h d) -> p h d", d=HD),
                                      k.good[:].unsqueeze(2).to_broadcast([P, HEADS, HD]), k.ot[:])
                    v.drain().then_inc(s.pv_read, 1)

                q3(0)
                for j in range(T):
                    a = it * T + j
                    heads = k.e.rearrange("p (h t) -> p h t", t=P)
                    v.wait_ge(s.scores, a + 1)
                    for b in range(4):
                        v.reduce_max(k.mx16[:, 4 * b:4 * b + 4], k.ps[b][:].rearrange("p (h t) -> p h t", t=P), axis=AX.X)
                    v.drain()
                    v.wait_ge(s.e_free, a + 1)
                    for b in range(4):
                        last = v.tensor_tensor(heads[:, 4 * b:4 * b + 4, :], k.ps[b][:].rearrange("p (h t) -> p h t", t=P),
                                               k.mx16[:, 4 * b:4 * b + 4].unsqueeze(2).to_broadcast([P, 4, P]), ALU.subtract)
                    last.then_inc(s.centred, 1)
                    if j < T - 1:
                        q3(j + 1)
                    v.drain()
                    if j:
                        normalize(j - 1)
                normalize(T - 1)
                v.wait_ge(s.o_hi, it + 1)
                v.tensor_tensor(k.ol[:], k.ps[4][:], k.oh[:].bitcast(F32), ALU.subtract).then_inc(s.o_lo, 1)
                v.wait_ge(s.out, it + 1)
                add(x, k.ps[6][:], 1)
                norm.vector(v, it * 6 + 1, xs)
                gate.vector(v, it, 0)
                experts(it, 0)
                v.wait_ge(s.sum, it * (E3 + 3) + 1)
                add(x, k.ps[6][:], 5)
                v.sem_inc(s.sum_read, 1)
                norm.vector(v, it * 6 + 2, xs)
                v.wait_ge(s.x2_hi, it * 2 + 2)
                v.tensor_tensor(k.xl[:], k.ps[4][:], k.xh[:].bitcast(F32), ALU.subtract).then_inc(s.x2_lo, 1)
                v.wait_ge(s.mixed_loaded, it * 16 * T + 16 * T)
                v.tensor_tensor(x, x, k.mixr[:, :, 0:P], ALU.add)
                v.drain()
                v.wait_ge(s.l2, it + 1)
                add(x, k.ps[6][:], 2)
                norm.vector(v, it * 6 + 3, xs)
                gate.vector(v, it, 1)
                experts(it, 1)
                v.wait_ge(s.sum, it * (E3 + 3) + 2)
                add(x, k.ps[6][:], 6)
                v.sem_inc(s.sum_read, 1)
                norm.vector(v, it * 6 + 4, xs)
                v.drain()
                v.scalar_tensor_tensor(k.xn[:], k.xn[:], 0.0, k.mixr[:, :, P:2 * P], ALU.max, ALU.mult)
                v.drain().then_inc(s.mix_free, 1)
                v.tensor_tensor(x, x, k.xn[:], ALU.add)
                v.drain()
                norm.vector(v, it * 6 + 5, xs)
                gate.vector(v, it, 2)
                for i, (e, m) in enumerate(b3):
                    n = 2 * NB1 + i
                    if i >= 5 and (i - 5) % 3 == 0:
                        collect = (i - 5) // 3
                        sum3(v, k, s, it, collect, SUM, by_tile)
                    blocks.vector_h(v, it * NB + n, n % 2, n % 3, M3[m], CW, 3)
                for collect in range((len(b3) - 1 - 5) // 3 + 1, E3 + 1):
                    sum3(v, k, s, it, collect, SUM, by_tile)
                v.scalar_tensor_tensor(x, k.acc[:], k.tg[:, 7:8], x, ALU.mult, ALU.add)
                v.drain().then_inc(s.done, 1)

        @block.scalar
        def _(act):
            def experts(it, l):
                for b in range(NB1 + 1):
                    n = l * NB1 + b
                    if b < NB1:
                        blocks.scalar_silu(act, it * NB + n, n % 2, P, CW)
                    if b:
                        blocks.scalar_hi(act, it * NB + n - 1, (n - 1) % 3, P, CW)

            def x_high(n):
                act.wait_ge(s.xT2, n)
                act.activation(k.xh[:], k.ps[4][:], ACT.Copy).then_inc(s.x2_hi, 1)

            with act.Fori(0, CHUNKS) as it:
                x_high(it * 2 + 1)
                def q_high(j):
                    act.wait_ge(s.q, it * T + j + 1)
                    act.activation(k.qh[:], k.ps[6][:], ACT.Copy).then_inc(s.q_hi, 1)
                q_high(0)
                for j in range(T):
                    a = it * T + j
                    act.wait_ge(s.centred, a + 1)
                    act.activation(k.e, k.e, ACT.Exp, scale=float(HD) ** -0.5).then_inc(s.exp, 1)
                    if j < T - 1:
                        q_high(j + 1)
                    for b in range(4):
                        act.wait_ge(s.turned, a * 4 + b + 1)
                        act.activation(k.pt[b % 2][:], k.ps[4 + b % 2][:], ACT.Copy).then_inc(s.taken, 1)
                act.wait_ge(s.oT, it + 1)
                act.activation(k.oh[:], k.ps[4][:], ACT.Copy).then_inc(s.o_hi, 1)
                gate.scalar(act, it, 0)
                experts(it, 0)
                x_high(it * 2 + 2)
                gate.scalar(act, it, 1)
                experts(it, 1)
                gate.scalar(act, it, 2)
                for i in range(len(b3) + 1):
                    n = 2 * NB1 + i
                    if i < len(b3):
                        blocks.scalar_silu(act, it * NB + n, n % 2, M3[b3[i][1]], CW)
                    if i:
                        blocks.scalar_hi(act, it * NB + n - 1, (n - 1) % 3, M3[b3[i - 1][1]], CW)

        @block.tensor
        def _(pe):
            def x_turned(norm_at, n):
                pe.wait_ge(norm.ready, norm_at + 1)
                for j in range(T):
                    last = pe.transpose(k.ps[4][:, tile[j]], k.xn[:, j, :], k.ident)
                last.then_inc(s.xT2, 1)
                pe.wait_ge(s.x2_lo, n)

            def experts(it, l, wh, wl):
                def down(b):
                    n = l * NB1 + b
                    w = slice(b * W1C + 2 * P, (b + 1) * W1C)
                    blocks.tensor_down(pe, it * NB + n, n % 3, P, chunk_tiles, lambda j: k.ps[6][:, tile[j]],
                                       wh[:, w], wl[:, w], b == 0, True)

                for b in range(NB1):
                    n = l * NB1 + b
                    blocks.tensor_gu(pe, it * NB + n, n % 2, wh, wl, b * W1C, b * W1C + P, P, k.xh[:], k.xl[:], gback(n))
                    if b < NB1 - 1:
                        if b == 0:
                            gate.tensor_weights(pe, it, l)
                        c = it * 2 * (NB1 - 1) + l * (NB1 - 1) + b
                        pe.wait_ge(s.cb_free, c + 1)
                        pe.matmul(k.ps[5][:], k.selh[:, tile_of(b)], k.wTl, start=True, stop=False)
                        pe.matmul(k.ps[5][:], k.selh[:, tile_of(b)], k.wTh, start=False, stop=True).then_inc(s.cb, 1)
                    if b >= 2:
                        down(b - 2)
                down(NB1 - 2)
                down(NB1 - 1)
                pe.drain().then_inc(s.sum, 1)
                pe.wait_ge(s.sum_read, it * (E3 + 3) + l + 1)

            tile_of = lambda b: slice(b * P, (b + 1) * P)
            with pe.Fori(0, CHUNKS) as it:
                x_turned(it * 6, it * 2 + 1)

                def queries(j):
                    a = it * T + j
                    for q in range(4):
                        c = slice(q * P, (q + 1) * P)
                        three_pass(pe, k.ps[6][:, c], k.wa1h[:, c], k.wa1l[:, c], k.xh[:, tile[j]], k.xl[:, tile[j]], stop=False)
                        pe.matmul(k.ps[6][:, c], k.bqh[:, c], k.one_r[:], start=False, stop=False)
                        last = pe.matmul(k.ps[6][:, c], k.bql[:, c], k.one_r[:], start=False, stop=True)
                    last.then_inc(s.q, 1)
                    pe.wait_ge(s.q3, a + 1)
                    pe.wait_ge(k_loaded[j % 2], it * 64 + j // 2 * 32 + 32)
                    if j:
                        pe.wait_ge(s.centred, a)
                    for q in range(4):
                        for g in range(4):
                            r = slice(32 * g, 32 * g + 3 * HD)
                            last = pe.matmul(k.ps[g][:, q * P:(q + 1) * P], k.q3[j % 2][r, q * P:(q + 1) * P],
                                             k.k3m[j % 2][r, q * P:(q + 1) * P], start=True, stop=True)
                    last.then_inc(s.scores, 1)

                def values(j):
                    a = it * T + j
                    pe.wait_ge(s.exp, a + 1)
                    if j:
                        pe.wait_ge(s.pv_read, a)
                    for b in range(4):
                        if not (j == 0 and b < 2):
                            pe.wait_ge(s.taken, a * 4 + b - 1)
                        for q in range(4):
                            last = pe.transpose(k.ps[4 + b % 2][:, tile[q]], k.e[:, (b * 4 + q) * P:(b * 4 + q + 1) * P], k.ident)
                        last.then_inc(s.turned, 1)
                        if b == 3:
                            pe.drain().then_inc(s.e_free, 1)
                        pe.wait_ge(s.taken, a * 4 + b + 1)
                        for q in range(4):
                            h = 4 * q + b
                            last = pe.matmul(k.ps[7][:, h * (HD + 1):(h + 1) * (HD + 1)], k.pt[b % 2][:, tile[q]],
                                             k.v9[j % 2][:, h, :], start=True, stop=True)
                    last.then_inc(s.pv, 1)
                    pe.drain().then_inc(s.kv_free, 1)

                queries(0)
                for j in range(T):
                    if j < T - 1:
                        queries(j + 1)
                    values(j)
                pe.wait_ge(s.pv_read, it * T + T)
                for j in range(T):
                    last = pe.transpose(k.ps[4][:, tile[j]], k.o[:, j, :], k.ident)
                last.then_inc(s.oT, 1)
                pe.wait_ge(s.o_lo, it + 1)
                for j in range(T):
                    last = three_pass(pe, k.ps[6][:, tile[j]], k.oh[:, tile[j]], k.ol[:, tile[j]],
                                      k.wa1h[:, 4 * P:5 * P], k.wa1l[:, 4 * P:5 * P])
                last.then_inc(s.out, 1)
                gate.tensor(pe, it, 0, it * 6 + 1)
                experts(it, 0, k.w1h, k.w1l)
                x_turned(it * 6 + 2, it * 2 + 2)
                for j in range(T):
                    last = three_pass(pe, k.ps[6][:, tile[j]], k.xh[:, tile[j]], k.xl[:, tile[j]], k.l2wh[:], k.l2wl[:])
                last.then_inc(s.l2, 1)
                gate.tensor(pe, it, 1, it * 6 + 3)
                experts(it, 1, k.w2h, k.w2l)
                gate.tensor(pe, it, 2, it * 6 + 5)
                pe.wait_ge(gate.ready, it * 3 + 3)
                for i in range(len(b3) + 2):
                    n = 2 * NB1 + i
                    if i < len(b3):
                        e, m = b3[i]
                        g0 = e * W3C + m * P
                        blocks.tensor_gu(pe, it * NB + n, n % 2, k.w3h, k.w3l, g0, g0 + FF3, M3[m], k.xh[:], k.xl[:])
                    if i >= 2:
                        e, m = b3[i - 2]
                        w = slice(e * W3C + 2 * FF3 + m * P, e * W3C + 2 * FF3 + (m + 1) * P)
                        if m == 0 and e >= 2:
                            pe.wait_ge(s.sum_read, it * (E3 + 3) + 2 + e - 1)
                        blocks.tensor_down(pe, it * NB + n - 2, (n - 2) % 3, M3[m], chunk_tiles,
                                           lambda j: SUM[e % 2][:, tile[j]], k.w3h[0:M3[m], w], k.w3l[0:M3[m], w], m == 0, True)
                        if m == 2:
                            pe.drain().then_inc(s.sum, 1)
                pe.wait_ge(s.done, it + 1)


def sum3(v, k, s, it, e, banks, by_tile):
    v.wait_ge(s.sum, it * (E3 + 3) + 2 + e + 1)
    ps = banks[e % 2]
    if e == 0:
        v.tensor_copy(k.acc[:], by_tile(ps[:]))
    else:
        for j in range(T):
            v.scalar_tensor_tensor(k.acc[:, j, :], ps[:, j * P:(j + 1) * P], k.c8[:, j, e - 1:e], k.acc[:, j, :],
                                   ALU.mult, ALU.add)
    v.drain().then_inc(s.sum_read, 1)


def program(nc, d, stop=9):
    k = Names()
    with ExitStack() as ctx:
        def sb(name, shape, dt=F32, c=ctx):
            return c.enter_context(nc.sbuf_tensor(name, shape, dt))

        k.sem = lambda name: nc.alloc_semaphore(name=name)
        k.ps = [ctx.enter_context(nc.psum_tensor(f"ps{i}", [P, 512], F32)) for i in range(8)]
        k.gu = [(k.ps[0], k.ps[1]), (k.ps[2], k.ps[3])]
        k.x = sb("x", [P, SEQS, P])
        k.const = sb("const", [P, C_ALL])
        k.ident = k.const[:, C_ID:C_ID + P]
        k.rows = sb("rows", [P, B_ALL])
        k.tg = sb("tg", [P, 8])
        k.eps4, k.mhalf = sb("eps4", [P, T]), sb("mhalf", [P, T])
        k.st6, k.mv = sb("st6", [P, T, 6]), sb("mv", [P, T, 2])
        k.ve, k.rs = sb("ve", [P, T]), sb("rs", [P, T])
        k.xn = sb("xn", [P, T, P])
        k.xh, k.xl = sb("xh", [P, CW], F32R), sb("xl", [P, CW], F32R)
        k.hs = sb("hs", [P, 5 * CW])
        slot = [k.hs[:, i * CW:(i + 1) * CW] for i in range(5)]
        k.h, k.s = slot[0:3], slot[3:5]
        k.hh = [sb(f"hh{i}", [P, CW], F32R) for i in range(3)]
        k.hl = [sb(f"hl{i}", [P, CW], F32R) for i in range(3)]
        k.l2wh, k.l2wl = sb("l2wh", [P, P], F32R), sb("l2wl", [P, P], F32R)
        k.w1h, k.w1l, k.w2h, k.w2l = (sb(n, [P, NB1 * W1C], F32R) for n in ("w1h", "w1l", "w2h", "w2l"))
        k.index, k.gate = sb("index", [P, K0 * SEQS], I32), sb("gate", [P, K0, SEQS])
        k.one_r = sb("one_r", [1, P], F32R)
        unused = nc.snapshot_sems()
        with ExitStack() as l0:
            k.const0 = sb("const0", [P, L_ALL], c=l0)
            k.raw = [sb(f"raw{i}", [P, W3C], c=l0) for i in range(2)]
            k.xn_all = sb("xn_all", [P, SEQS, P], c=l0)
            k.sc = sb("sc", [P, SEQS, 40], c=l0)
            k.ub = sb("ub", [P, 2 * P], BF16, l0)
            with ExitStack() as a0:
                k.junk = sb("junk", [P, CW], c=a0)
                k.sh0h, k.sh0l = sb("sh0h", [P, W0C], F32R, a0), sb("sh0l", [P, W0C], F32R, a0)
                k.g0h, k.g0l = sb("g0h", [P, 40], F32R, a0), sb("g0l", [P, 40], F32R, a0)
                k.wa0, k.bcol = sb("wa0", [P, 4 * P], c=a0), sb("bcol", [P, 2], c=a0)
                with ExitStack() as su:
                    k.cent, k.cs = sb("cent", [40, P], c=su), sb("cs", [40, 3], c=su)
                    k.w2t, k.ctxT = sb("w2t", [P, P], c=su), sb("ctxT", [P, SEQS * P], c=su)
                    k.csum, k.rsum = sb("csum", [P, SEQS], c=su), sb("rsum", [P, SEQS], c=su)
                    k.zero, k.mix = sb("zero", [P, SLOTS // 8], c=su), sb("mix", [SEQS, 2 * P], c=su)
                    setup(nc, k, d)
                k.ctxr = sb("ctxr", [P, CW], c=a0)
                k.xT, k.qT, k.kT, k.pT, k.oT = (sb(n, [P, CW], c=a0) for n in ("xT", "qT", "kT", "pT", "oT"))
                k.v0, k.pr = sb("v0", [P, T, P], c=a0), sb("pr", [P, T, P], c=a0)
                k.mx = sb("mx", [P, 3 * T], c=a0)
                k.ss, k.ss2, k.rn = (sb(n, [P, T], c=a0) for n in ("ss", "ss2", "rn"))
                layer0_attention(nc, k, d)
            nc.clear_and_free_semaphores(nc.allocated_since(unused))
            nc.all_engine_barrier()
            layer0_experts_all(nc, k, d, sb)
        k.w3h, k.w3l = sb("w3h", [P, (E3 + 1) * W3C], F32R), sb("w3l", [P, (E3 + 1) * W3C], F32R)
        k.wa1h, k.wa1l = sb("wa1h", [P, 5 * P], F32R), sb("wa1l", [P, 5 * P], F32R)
        k.gth, k.gtl = sb("gth", [P, 2 * E1 + E3], F32R), sb("gtl", [P, 2 * E1 + E3], F32R)
        k.selh = sb("selh", [E1, (NB1 - 1) * P], F32R)
        k.bqh, k.bql = sb("bqh", [1, 4 * P], F32R), sb("bql", [1, 4 * P], F32R)
        with ExitStack() as comb:
            k.y = sb("y", [P, 16, P], c=comb)
            k.raw = [sb(f"raw_w3_{i}", [P, W3C], c=comb) for i in range(2)]
            layer0_combine(nc, k, d)
        if stop == 2:
            stored = k.sem("stored")
            with nc.Block() as block:
                @block.sync
                def _(sp):
                    sp.dma_start(d.out.rearrange("t p d -> p t d"), k.x[:]).then_inc(stored, 16)
                    sp.wait_ge(stored, 16)
            return
        k.q3, k.k3m = ([sb(f"{n}{i}", [P, 4 * P], F32R) for i in range(2)] for n in ("q3", "k3m"))
        k.v9 = [sb(f"v9{i}", [P, HEADS, HD + 1]) for i in range(2)]
        k.qh, k.oh, k.ol = k.hh[0], k.hh[1], k.hh[2]
        k.acc = sb("acc", [P, T, P])
        k.e = k.hs[:, 0:4 * CW]
        k.pt = [slot[4], k.acc[:].rearrange("p t d -> p (t d)")]
        k.o = k.xn
        k.mixr = sb("mixr", [P, T, 2 * P])
        k.mx16, k.den, k.rec = (sb(n, [P, HEADS]) for n in ("mx16", "den", "recd"))
        k.good, k.ot = sb("good", [P, HEADS], I32), sb("ot", [P, HEADS, HD])
        k.sg, k.ms, k.mask, k.c16 = (sb(n, [P, T, E1]) for n in ("sg", "ms", "mask", "c16"))
        k.pairs = sb("pairs", [P, T * 4, 6])
        k.g8, k.m8, k.gm, k.c8 = (sb(n, [P, T, 8]) for n in ("g8", "m8", "gm", "c8"))
        k.q8 = [sb(f"q8_{i}", [P, T, 8]) for i in range(3)]
        k.q16 = [sb(f"q16_{i}", [P, T, E1]) for i in range(3)]
        k.r1, k.r2 = sb("r1", [P, T]), sb("r2", [P, T])
        k.wTh, k.wTl = k.q3[0][0:E1, :], k.q3[1][0:E1, :]
        later_layers(nc, k, d, stop)


def laid_out(i):
    t = lambda a: np.ascontiguousarray(np.swapaxes(a, -1, -2))
    cat = lambda *a: np.ascontiguousarray(np.concatenate(a, axis=-1))
    z = lambda *s: np.zeros(s, np.float32)
    o = {"x": i["x"], "const": constants(), "const0": constants_layer0()}
    o["ctxT"] = t(i["ctx_1024"].reshape(SEQS * P, P))
    o["rows"] = cat(i["L0_xattn_bv"], i["L0_xattn_bo"], i["L0_ffn_bias"], i["L1_xattn_bv"], i["L1_xattn_bo"],
                    i["L2_xattn_b"], i["g_xattn"], i["g_ffn"])[None]
    o["wa0"] = cat(i["L0_xattn_Wq"], i["L0_xattn_Wk"], i["L0_xattn_Wv"], i["L0_xattn_Wo"])
    o["cent"] = np.concatenate([i["L0_ffn_group_centroids"], i["L0_ffn_expert_centroids"]])
    halves = lambda w: cat(w[..., 0:P, :], w[..., P:2 * P, :])
    o["w0"] = np.concatenate([cat(i["L0_ffn_wg"], i["L0_ffn_wu"], halves(i["L0_ffn_wd"])),
                              cat(i["L0_ffn_sg"], i["L0_ffn_su"], halves(i["L0_ffn_sd"]))[None]])
    pair = lambda w: np.concatenate([w[0::2], w[1::2]], axis=2)
    down = lambda w: np.concatenate([w[0::2], w[1::2]], axis=1)
    pack = lambda g, u, dn: np.ascontiguousarray(np.concatenate(list(cat(g, u, dn)), axis=1))
    o["w1"] = pack(np.concatenate([pair(t(i["L1_ffn_w1_e"])), t(i["L1_ffn_w1_s"])[None]]),
                   np.concatenate([pair(t(i["L1_ffn_w3_e"])), t(i["L1_ffn_w3_s"])[None]]),
                   np.concatenate([down(t(i["L1_ffn_w2_e"])), t(i["L1_ffn_w2_s"])[None]]))
    o["w2"] = pack(np.concatenate([pair(i["L2_ffn_w1"]), i["L2_ffn_ws1"][None]]),
                   np.concatenate([pair(i["L2_ffn_w3"]), i["L2_ffn_ws3"][None]]),
                   np.concatenate([down(i["L2_ffn_w2"]), i["L2_ffn_ws2"][None]]))
    o["l2w"] = cat(t(i["L2_xattn_W"][:, 0:P]), t(i["L2_xattn_W"][:, P:2 * P]))
    gate = np.concatenate([i["L3_ffn_shared_gate"][None], i["L3_ffn_expert_gate"]])
    up = np.concatenate([i["L3_ffn_shared_up"][None], i["L3_ffn_expert_up"]])
    dn = t(np.concatenate([i["L3_ffn_shared_down"][None], i["L3_ffn_expert_down"]]))
    dn = np.concatenate([dn, z(E3 + 1, 3 * P - FF3, P)], axis=1).reshape(E3 + 1, 3, P, P)
    o["w3"] = cat(t(gate), t(up), np.swapaxes(dn, 1, 2).reshape(E3 + 1, P, 3 * P))
    def quads(w):
        a = w.reshape(*w.shape[:-1], HEADS, 1, HD)
        a = np.concatenate([a, a, a, np.zeros_like(a)], axis=-2)
        return a.reshape(*w.shape[:-1], 4 * P)
    o["wa1"] = cat(quads(t(i["L1_xattn_Wq"])), quads(t(i["L1_xattn_Wk"])), t(i["L1_xattn_Wv"]), t(i["L1_xattn_Wo"]))
    o["brow"] = cat(quads(i["L1_xattn_bq"]), quads(i["L1_xattn_bk"]))[None]
    o["bcol"] = np.stack([i["L0_xattn_bq"], i["L0_xattn_bk"]], 1)
    o["gates"] = cat(t(i["L1_ffn_w_gate"]), t(i["L2_ffn_gate_w"]), t(i["L3_ffn_gate_w"]))
    o["sel"] = selectors()
    return {n: np.ascontiguousarray(a) for n, a in o.items()}


STOP = 9


def kernel(**inputs):
    import concourse.bacc as bacc
    from concourse.bass_utils import run_bass_kernel_spmd as run

    nc = bacc.Bacc("TRN2", target_bir_lowering=False, num_devices=1)
    arrays = laid_out({n: np.asarray(a) for n, a in inputs.items()})
    d = Names()
    for name, a in arrays.items():
        d[name] = nc.dram_tensor("in_" + name, a.shape, mybir.dt.from_np(a.dtype), kind="ExternalInput").ap()
    d.out = nc.dram_tensor("out_0", (SEQS, P, P), F32, kind="ExternalOutput").ap()
    d.buf = nc.dram_tensor("slot_in", (SLOTS + K0 * SEQS * P, P), F32, kind="Internal").ap()
    d.oute = nc.dram_tensor("slot_out", (SLOTS + P, P), F32, kind="Internal").ap()
    d.mix = nc.dram_tensor("seq_rows", (SEQS, 2 * P), F32, kind="Internal").ap()
    d.keys1 = nc.dram_tensor("l1_keys", (SEQS, P, 4 * P), F32, kind="Internal").ap()
    d.values1 = nc.dram_tensor("l1_values", (SEQS, P, HEADS * (HD + 1)), F32, kind="Internal").ap()
    program(nc, d, STOP)
    r = run(nc, [{"in_" + n: a for n, a in arrays.items()}], core_ids=[0])
    return r.results[0]["out_0"]
```

```python
from contextlib import ExitStack

import numpy as np
import concourse.bass as bass
from concourse import mybir

F32 = mybir.dt.float32
F32R = mybir.dt.float32r
BF16 = mybir.dt.bfloat16
I32 = mybir.dt.int32
U32 = mybir.dt.uint32
ALU = mybir.AluOpType
ACT = mybir.ActivationFunctionType
AX = mybir.AxisListType


class Names(dict):

    def __getattr__(self, name):
        return self[name]

    def __setattr__(self, name, value):
        self[name] = value


P = 128
SEQS = 16
T = 4
CHUNKS = SEQS // T
CW = T * P
EPS = 1e-5

E0, G0, K0, HID0 = 32, 8, 4, 256
CAP = int(SEQS * P / E0 * K0 * 1.25)
ROWS = (112, 112, 96)
RT = 112
SLOTS = E0 * CAP
W0C = 3 * HID0
E1, G1, K1 = 16, 4, 4
NB1 = E1 // 2 + 1
W1C = 3 * P
E3, K3 = 8, 2
FF3 = 352
M3 = (128, 128, 96)
W3C = 2 * FF3 + 3 * P
HEADS, HD = 16, 8

C_ID = 0
C_SPLIT = 128
C_R8 = 130
C_R16 = C_R8 + T * 8
C_ALL = C_R16 + T * E1
L_U, L_ONE = 0, 128
L_TRASH = 256
L_START = 257
L_R8 = L_START + E0
L_R32 = L_R8 + SEQS * 8
L_R16T = L_R32 + SEQS * E0
L_SPREAD = L_R16T + SEQS * E0
L_ALL = L_SPREAD + K0 * SEQS
B_BV0, B_BO0, B_BIAS0, B_BV1, B_BO1, B_B2, B_G = 0, 128, 256, 288, 416, 544, 672
B_ALL = 680


def constants():
    c = np.zeros((P, C_ALL), np.float32)
    c[:, C_ID:C_ID + P] = np.eye(P)
    part = (np.arange(P) % 32) // HD
    c[:, C_SPLIT] = -1.0 * (part == 1)
    c[:, C_SPLIT + 1] = -1.0 * (part == 2)
    c[:, C_R8:C_R8 + T * 8] = np.arange(T * 8) % 8 > 0
    c[:, C_R16:C_R16 + T * E1] = np.arange(T * E1) % E1 > 0
    return c


def constants_layer0():
    c = np.zeros((P, L_ALL), np.float32)
    c[:, L_U:L_U + P] = np.triu(np.ones((P, P)), 1)
    c[:, L_ONE:L_ONE + P] = 1
    c[:, L_TRASH] = SLOTS + np.arange(P)
    c[:, L_START:L_START + E0] = np.arange(E0) * CAP
    c[:, L_R8:L_R8 + SEQS * 8] = np.arange(SEQS * 8) % 8 > 0
    c[:, L_R32:L_R32 + SEQS * E0] = np.arange(SEQS * E0) % E0 > 0
    c[:, L_R16T:L_R16T + SEQS * E0] = np.arange(SEQS * E0) % SEQS > 0
    c[:, L_SPREAD:L_SPREAD + K0 * SEQS] = np.arange(K0 * SEQS) * P
    return c


def selectors():
    s = np.zeros((E1, (NB1 - 1) * P), np.float32)
    for b in range(NB1 - 1):
        for p in range(P):
            s[2 * b + p // 64, b * P + p] = 1
    return s


def topk_mask(v, s, m8, k, mask, gt, eq, pre, count, reset):
    tiles, n = s.shape[1], s.shape[2]
    full = [P, tiles, n]
    for t in range(tiles):
        v.max(m8[:, t, :], s[:, t, :])
    v.drain()
    tau = m8[:, :, k - 1:k].to_broadcast(full)
    v.tensor_tensor(gt, s, tau, ALU.is_gt)
    v.tensor_tensor(eq, s, tau, ALU.is_equal)
    v.drain()
    v.reduce_sum(count, gt, axis=AX.X)
    v.tensor_tensor_scan(pre.rearrange("p t n -> p (t n)"), reset, eq.rearrange("p t n -> p (t n)"), 0.0,
                         ALU.mult, ALU.add)
    v.drain()
    v.tensor_tensor(pre, pre, count.unsqueeze(2).to_broadcast(full), ALU.add)
    v.drain()
    v.scalar_tensor_tensor(eq, pre, float(k) + 0.5, eq, ALU.is_lt, ALU.mult)
    v.drain()
    v.tensor_tensor(mask, gt, eq, ALU.add)
    v.drain()


def three_pass(pe, out, lh, ll, rh, rl, start=True, stop=True, skip=False):
    pe.matmul(out, lh, rl, start=start, stop=False, skip_group_check=skip)
    pe.matmul(out, ll, rh, start=False, stop=False, skip_group_check=skip)
    return pe.matmul(out, lh, rh, start=False, stop=stop, skip_group_check=skip)


class Norm:

    def __init__(self, k, name):
        self.k = k
        self.stats = k.sem(name + "_stats")
        self.eps = k.sem(name + "_eps")
        self.rstd = k.sem(name + "_rstd")
        self.ready = k.sem(name + "_ready")

    def vector(self, v, n, x):
        k = self.k
        for j in range(T):
            v.bn_stats(k.st6[:, j, :], x[j])
        v.drain()
        for j in range(T):
            last = v.bn_aggr(k.mv[:, j, :], k.st6[:, j, :])
        last.then_inc(self.stats, 1)
        v.wait_ge(self.rstd, n + 1)
        for j in range(T):
            last = v.tensor_scalar(k.xn[:, j, :], x[j], k.mv[:, j, 0:1], k.rs[:, j:j + 1],
                                   ALU.subtract, ALU.mult)
        last.then_inc(self.ready, 1)

    def pool(self, g, n):
        k = self.k
        g.wait_ge(self.stats, n + 1)
        g.tensor_tensor(k.ve[:], k.mv[:, :, 1], k.eps4[:], ALU.add).then_inc(self.eps, 1)
        g.wait_ge(self.eps, n + 1)
        g.tensor_tensor(k.rs[:], k.ve[:], k.mhalf[:], ALU.pow).then_inc(self.rstd, 1)


class Blocks:

    def __init__(self, k, name, gu, s, h, hh, hl):
        self.gu, self.s, self.h, self.hh, self.hl = gu, s, h, hh, hl
        self.gu_ready = k.sem(name + "_gu_ready")
        self.gu_free = k.sem(name + "_gu_free")
        self.silu = k.sem(name + "_silu")
        self.h_ready = k.sem(name + "_h_ready")
        self.hi = k.sem(name + "_hi")
        self.lo = k.sem(name + "_lo")
        self.h_free = k.sem(name + "_h_free")

    def credits(self, v):
        v.sem_inc(self.gu_free, len(self.gu))
        v.sem_inc(self.h_free, len(self.h))

    def tensor_gu(self, pe, a, g, wh, wl, g0, u0, m, xh, xl, back=2):
        w = xh.shape[1]
        pe.wait_ge(self.gu_free, a + 1 + len(self.gu) - back)
        for c0, bank in ((g0, 0), (u0, 1)):
            last = three_pass(pe, self.gu[g][bank][0:m, 0:w], wh[:, c0:c0 + m], wl[:, c0:c0 + m], xh, xl)
        last.then_inc(self.gu_ready, 1)

    def scalar_silu(self, act, a, g, m, w):
        act.wait_ge(self.gu_ready, a + 1)
        act.activation(self.s[g][0:m, 0:w], self.gu[g][0][0:m, 0:w], ACT.Silu).then_inc(self.silu, 1)

    def vector_h(self, v, a, g, h, m, w, back, weights=None, ready=None, free=None):
        v.wait_ge(self.h_free, a + 1 + len(self.h) - back)
        v.wait_ge(self.silu, a + 1)
        hid = self.h[h][0:m, 0:w]
        v.tensor_tensor(hid, self.s[g][0:m, 0:w], self.gu[g][1][0:m, 0:w], ALU.mult).then_inc(self.gu_free, 1)
        if weights is not None:
            v.drain()
            v.wait_ge(*ready)
            v.tensor_tensor(hid, hid, weights, ALU.mult).then_inc(free, 1)
        v.drain().then_inc(self.h_ready, 1)

    def scalar_hi(self, act, a, h, m, w):
        act.wait_ge(self.h_ready, a + 1)
        act.activation(self.hh[h][0:m, 0:w], self.h[h][0:m, 0:w], ACT.Copy).then_inc(self.hi, 1)

    def pool_lo(self, g, a, h, m, w):
        g.wait_ge(self.hi, a + 1)
        g.tensor_tensor(self.hl[h][0:m, 0:w], self.h[h][0:m, 0:w], self.hh[h][0:m, 0:w].bitcast(F32),
                        ALU.subtract).then_inc(self.lo, 1)

    def tensor_down(self, pe, a, h, m, tiles, out, w, wl, first, skip):
        pe.wait_ge(self.lo, a + 1)
        for j, (c0, c1) in enumerate(tiles):
            last = three_pass(pe, out(j), self.hh[h][0:m, c0:c1], self.hl[h][0:m, c0:c1], w, wl,
                              start=first and (j == 0 or not skip), stop=True, skip=skip)
        last.then_inc(self.h_free, 1)


def load_and_split(nc, k, name, jobs):
    loaded, hi, lo = [k.sem(f"{name}_loaded{i}") for i in range(2)], k.sem(name + "_hi"), k.sem(name + "_lo")


    def raw(i):
        rows, cols = jobs[i][0].shape
        first = 32 if name == "comb_w" and rows == 1 else 0
        return k.raw[i % 2][first:first + rows, 0:cols]


    def sync(sp, first=0, end=len(jobs)):
        for i in range(first, end):
            if i >= 2:
                sp.wait_ge(hi, i - 1)
                sp.wait_ge(lo, i - 1)
            sp.dma_start(raw(i), jobs[i][0]).then_inc(loaded[i % 2], 16)

    def scalar(act, first=0, end=len(jobs)):
        for i in range(first, end):
            act.wait_ge(loaded[i % 2], 16 * (i // 2 + 1))
            act.activation(jobs[i][1], raw(i), ACT.Copy).then_inc(hi, 1)

    def vector(v, first=0, end=len(jobs)):
        for i in range(first, end):
            _, high, low = jobs[i]
            v.wait_ge(hi, i + 1)
            if low is None:
                v.drain().then_inc(lo, 1)
            else:
                v.tensor_tensor(low, raw(i), high.bitcast(F32), ALU.subtract).then_inc(lo, 1)

    return sync, scalar, vector


def setup(nc, k, d):
    s = Names(**{n: k.sem("setup_" + n) for n in (
        "loaded", "ctx", "zero", "tanh", "square", "norm", "cent", "centT", "gh", "csum", "rsum", "mix0", "mix1",
        "mix", "stored")})
    sync_w, scalar_w, vector_w = load_and_split(nc, k, "setup_w", [
        (d.w0[E0], k.sh0h[:], k.sh0l[:]), (d.l2w[:, 0:P], k.l2wh[:], k.l2wl[:])])
    loads = 8
    with nc.Block() as block:
        @block.sync
        def _(sp):
            sp.dma_start(k.x[:], d.x.rearrange("t p d -> p t d")).then_inc(s.loaded, 16)
            sp.dma_start(k.const[:], d.const[:, :]).then_inc(s.loaded, 16)
            sp.dma_start(k.const0[:], d.const0[:, :]).then_inc(s.loaded, 16)
            sp.dma_start(k.rows[:], d.rows[0, :].partition_broadcast(P)).then_inc(s.loaded, 16)
            sp.dma_start(k.wa0[:], d.wa0[:, :]).then_inc(s.loaded, 16)
            sp.dma_start(k.bcol[:], d.bcol[:, :]).then_inc(s.loaded, 16)
            sp.dma_start(k.cent[:], d.cent[:, :]).then_inc(s.loaded, 16)
            sp.dma_start(k.w2t[:], d.l2w[:, P:2 * P]).then_inc(s.loaded, 16)
            sp.dma_start(k.ctxT[:], d.ctxT[:, :]).then_inc(s.ctx, 16)
            sync_w(sp)
            sp.wait_ge(s.zero, 1)
            n = SLOTS // 8
            for i in range(8):
                sp.dma_start(d.buf[i * n:(i + 1) * n, :].rearrange("(p r) d -> p (r d)", p=P),
                             k.zero[:]).then_inc(s.stored, 16)
            sp.dma_start(d.oute[SLOTS:SLOTS + P, :], k.zero[:, 0:P]).then_inc(s.stored, 16)
            sp.wait_ge(s.mix, 1)
            sp.dma_start(d.mix[:, :], k.mix[:]).then_inc(s.stored, 16)
            sp.wait_ge(s.stored, 160)

        @block.gpsimd
        def _(g):
            g.memset(k.eps4[:], EPS)
            g.memset(k.mhalf[:], -0.5)
            g.drain()
            g.wait_ge(s.square, 1)
            g.tensor_tensor(k.cs[:, 2:3], k.cs[:, 1:2], k.mhalf[0:40, 0:1], ALU.pow).then_inc(s.norm, 1)

        @block.scalar
        def _(act):
            act.wait_ge(s.loaded, 16 * loads)
            act.activation(k.tg[:], k.rows[:, B_G:B_G + 8], ACT.Tanh).then_inc(s.tanh, 1)
            scalar_w(act)
            act.wait_ge(s.centT, 1)
            act.activation(k.g0h[:], k.ps[7][:, 0:40], ACT.Copy).then_inc(s.gh, 1)

        @block.vector
        def _(v):
            v.memset(k.zero[:], 0.0).then_inc(s.zero, 1)
            v.wait_ge(s.loaded, 16 * loads)
            v.wait_ge(s.tanh, 1)
            for out, b, g in ((k.rows[:, B_BO0:B_BO0 + P], B_BO0, 0), (k.bo1[:], B_BO1, 1)):
                v.tensor_scalar(out, k.rows[:, b:b + P], k.tg[:, g:g + 1], None, ALU.mult)
            v.tensor_copy(k.ub[:], k.const0[:, L_U:L_U + 2 * P])
            v.tensor_tensor(k.junk[0:40, 0:P], k.cent[:], k.cent[:], ALU.mult)
            v.drain()
            v.reduce_sum(k.cs[:, 0:1], k.junk[0:40, 0:P], axis=AX.X)
            v.drain()
            v.tensor_scalar(k.cs[:, 1:2], k.cs[:, 0:1], 1e-24, None, ALU.max).then_inc(s.square, 1)
            v.wait_ge(s.norm, 1)
            v.tensor_scalar(k.cent[:], k.cent[:], k.cs[:, 2:3], None, ALU.mult).then_inc(s.cent, 1)
            v.wait_ge(s.ctx, 16)
            seqs = k.ctxT[:].rearrange("p (s t) -> p s t", t=P)
            v.reduce_sum(k.csum[:], seqs, axis=AX.X).then_inc(s.csum, 1)
            v.drain()
            v.scalar_tensor_tensor(k.ctxT[:], k.ctxT[:], 0.0, k.ctxT[:], ALU.max, ALU.mult)
            v.drain()
            v.reduce_sum(k.rsum[:], seqs, axis=AX.X).then_inc(s.rsum, 1)
            vector_w(v)
            v.wait_ge(s.gh, 1)
            v.tensor_tensor(k.g0l[:], k.ps[7][:, 0:40], k.g0h[:].bitcast(F32), ALU.subtract)
            v.wait_ge(s.mix0, 1)
            v.scalar_tensor_tensor(k.mix[:, 0:P], k.ps[6][0:SEQS, 0:P], 1.0 / P, k.rows[0:SEQS, B_B2:B_B2 + P],
                                   ALU.mult, ALU.add)
            v.wait_ge(s.mix1, 1)
            v.tensor_scalar(k.mix[:, P:2 * P], k.ps[5][0:SEQS, 0:P], k.tg[0:SEQS, 3:4], None, ALU.mult)
            v.drain()
            v.tensor_scalar(k.mix[:, 0:P], k.mix[:, 0:P], k.tg[0:SEQS, 2:3], None, ALU.mult).then_inc(s.mix, 1)

        @block.tensor
        def _(pe):
            pe.wait_ge(s.loaded, 16 * loads)
            pe.wait_ge(s.cent, 1)
            pe.transpose(k.ps[7][:, 0:40], k.cent[:], k.ident[0:40, 0:40]).then_inc(s.centT, 1)
            pe.wait_ge(s.csum, 1)
            pe.matmul(k.ps[6][0:SEQS, 0:P], k.csum[:], k.w2t[:], start=True, stop=True).then_inc(s.mix0, 1)
            pe.wait_ge(s.rsum, 1)
            pe.transpose(k.ps[5][0:SEQS, 0:P], k.rsum[:], k.ident).then_inc(s.mix1, 1)


def layer0_attention(nc, k, d):
    s = Names(**{n: k.sem("a0_" + n) for n in (
        "ctx_loaded", "ctx_free", "xT", "xTs", "qkv", "qk_read", "v_read", "scores", "centred", "exp", "probs",
        "pT", "pTs", "o", "os", "out", "fT", "hi", "lo", "square", "norm_max", "norm_inv", "logits",
        "logits_read", "copied", "done")})
    norm = Norm(k, "a0_norm")
    blocks = Blocks(k, "a0_blk", k.gu, k.s, k.h[0:2], k.hh[0:2], k.hl[0:2])
    pT, pQ, pK, pV = k.ps[4], k.ps[5], k.ps[6], k.ps[7]
    tile = [slice(j * P, (j + 1) * P) for j in range(T)]
    by_tile = lambda ps: ps[:].rearrange("p (t d) -> p t d", d=P)
    row = lambda b: k.rows[:, b:b + P].unsqueeze(1).to_broadcast([P, T, P])
    each = lambda col: col.unsqueeze(2).to_broadcast([P, T, P])
    with nc.Block() as block:
        @block.sync
        def _(sp):
            with sp.Fori(0, CHUNKS) as it:
                sp.wait_ge(s.ctx_free, it + 1)
                sp.dma_start(k.ctxr[:], d.ctxT[:, bass.ds(it * CW, CW)]).then_inc(s.ctx_loaded, 16)

        @block.gpsimd
        def _(g):
            with g.Fori(0, CHUNKS) as it:
                norm.pool(g, it * 2)
                norm.pool(g, it * 2 + 1)
                g.wait_ge(s.norm_max, it + 1)
                g.tensor_tensor(k.rn[:], k.ss2[:], k.mhalf[:], ALU.pow).then_inc(s.norm_inv, 1)
                g.tensor_copy(k.xn_all[:, bass.ds(it * T, T), :], k.xn[:]).then_inc(s.copied, 1)
                for n in range(2):
                    blocks.pool_lo(g, it * 2 + n, n, P, CW)

        @block.vector
        def _(v):
            v.sem_inc(s.ctx_free, 1)
            blocks.credits(v)
            with v.Fori(0, CHUNKS) as it:
                x = k.x[:, bass.ds(it * T, T), :]
                norm.vector(v, it * 2, [k.x[:, it * T + j, :] for j in range(T)])
                v.wait_ge(s.qkv, it + 1)
                v.tensor_tensor(k.v0[:], by_tile(pV), row(B_BV0), ALU.add).then_inc(s.v_read, 1)
                v.wait_ge(s.scores, it + 1)
                v.reduce_max(k.mx[:, 0:T], by_tile(pV), axis=AX.X)
                v.drain()
                v.tensor_tensor(k.pr[:], by_tile(pV), each(k.mx[:, 0:T]), ALU.subtract).then_inc(s.centred, 1)
                v.wait_ge(s.exp, it + 1)
                v.reduce_sum(k.mx[:, T:2 * T], k.pr[:], axis=AX.X)
                v.drain()
                v.reciprocal(k.mx[:, 2 * T:3 * T], k.mx[:, T:2 * T])
                v.drain()
                v.tensor_tensor(k.pr[:], k.pr[:], each(k.mx[:, 2 * T:3 * T]), ALU.mult).then_inc(s.probs, 1)
                v.tensor_tensor(x, x, row(B_BO0), ALU.add)
                v.drain()
                v.wait_ge(s.out, it + 1)
                v.scalar_tensor_tensor(x, by_tile(pK), k.tg[:, 0:1], x, ALU.mult, ALU.add)
                v.drain()
                norm.vector(v, it * 2 + 1, [k.x[:, it * T + j, :] for j in range(T)])
                v.wait_ge(s.hi, it + 1)
                v.tensor_tensor(k.xl[:], pT[:], k.xh[:].bitcast(F32), ALU.subtract).then_inc(s.lo, 1)
                v.wait_ge(s.square, it + 1)
                v.tensor_scalar(k.ss2[:], k.ss[:], 1e-24, None, ALU.max).then_inc(s.norm_max, 1)
                for n in range(2):
                    blocks.vector_h(v, it * 2 + n, n, n, P, CW, 2)
                v.wait_ge(s.norm_inv, it + 1)
                v.wait_ge(s.logits, it + 1)
                v.tensor_tensor(k.sc[:, bass.ds(it * T, T), :], pQ[:, 0:T * 40].rearrange("p (t n) -> p t n", n=40),
                                k.rn[:].unsqueeze(2).to_broadcast([P, T, 40]), ALU.mult).then_inc(s.logits_read, 1)
                v.wait_ge(blocks.h_free, it * 2 + 4)
                v.scalar_tensor_tensor(x, by_tile(pK), k.tg[:, 4:5], x, ALU.mult, ALU.add).then_inc(s.done, 1)
                v.drain()
                v.wait_ge(s.copied, it + 1)

        @block.scalar
        def _(act):
            with act.Fori(0, CHUNKS) as it:
                act.wait_ge(s.xT, it + 1)
                act.activation(k.xT[:], pT[:], ACT.Copy).then_inc(s.xTs, 1)
                act.wait_ge(s.qkv, it + 1)
                act.activation(k.qT[:], pQ[:], ACT.Identity, bias=k.bcol[:, 0:1])
                act.activation(k.kT[:], pK[:], ACT.Identity, bias=k.bcol[:, 1:2]).then_inc(s.qk_read, 1)
                act.wait_ge(s.centred, it + 1)
                act.activation(k.pr[:], k.pr[:], ACT.Exp, scale=float(P) ** -0.5).then_inc(s.exp, 1)
                act.wait_ge(s.pT, it + 1)
                act.activation(k.pT[:], pT[:], ACT.Copy).then_inc(s.pTs, 1)
                act.wait_ge(s.o, it + 1)
                act.activation(k.oT[:], pQ[:], ACT.Copy).then_inc(s.os, 1)
                act.wait_ge(norm.ready, it * 2 + 2)
                for j in range(T):
                    last = act.activation(k.junk[:, tile[j]], k.xn[:, j, :], ACT.Square, accum_out=k.ss[:, j:j + 1])
                last.then_inc(s.square, 1)
                act.wait_ge(s.fT, it + 1)
                act.activation(k.xh[:], pT[:], ACT.Copy).then_inc(s.hi, 1)
                for n in range(2):
                    blocks.scalar_silu(act, it * 2 + n, n, P, CW)
                for n in range(2):
                    blocks.scalar_hi(act, it * 2 + n, n, P, CW)

        @block.tensor
        def _(pe):
            with pe.Fori(0, CHUNKS) as it:
                pe.wait_ge(s.ctx_loaded, it * 16 + 16)
                pe.matmul(pK[:], k.wa0[:, P:2 * P], k.ctxr[:], start=True, stop=True)
                for j in range(T):
                    last = pe.matmul(pV[:, tile[j]], k.ctxr[:, tile[j]], k.wa0[:, 2 * P:3 * P], start=True, stop=True)
                last.then_inc(s.ctx_free, 1)
                pe.wait_ge(norm.ready, it * 2 + 1)
                for j in range(T):
                    last = pe.transpose(pT[:, tile[j]], k.xn[:, j, :], k.ident)
                last.then_inc(s.xT, 1)
                pe.wait_ge(s.xTs, it + 1)
                pe.matmul(pQ[:], k.wa0[:, 0:P], k.xT[:], start=True, stop=True).then_inc(s.qkv, 1)
                pe.wait_ge(s.v_read, it + 1)
                pe.wait_ge(s.qk_read, it + 1)
                for j in range(T):
                    last = pe.matmul(pV[:, tile[j]], k.qT[:, tile[j]], k.kT[:, tile[j]], start=True, stop=True)
                last.then_inc(s.scores, 1)
                pe.wait_ge(s.probs, it + 1)
                for j in range(T):
                    last = pe.transpose(pT[:, tile[j]], k.pr[:, j, :], k.ident)
                last.then_inc(s.pT, 1)
                pe.wait_ge(s.pTs, it + 1)
                for j in range(T):
                    last = pe.matmul(pQ[:, tile[j]], k.v0[:, j, :], k.pT[:, tile[j]], start=True, stop=True)
                last.then_inc(s.o, 1)
                pe.wait_ge(s.os, it + 1)
                for j in range(T):
                    last = pe.matmul(pK[:, tile[j]], k.oT[:, tile[j]], k.wa0[:, 3 * P:4 * P], start=True, stop=True)
                last.then_inc(s.out, 1)
                pe.wait_ge(norm.ready, it * 2 + 2)
                for j in range(T):
                    last = pe.transpose(pT[:, tile[j]], k.xn[:, j, :], k.ident)
                last.then_inc(s.fT, 1)
                pe.wait_ge(s.lo, it + 1)
                for n in range(2):
                    blocks.tensor_gu(pe, it * 2 + n, n, k.sh0h, k.sh0l, n * P, HID0 + n * P, P, k.xh[:], k.xl[:])
                for j in range(T):
                    last = three_pass(pe, pQ[:, j * 40:(j + 1) * 40], k.xh[:, tile[j]], k.xl[:, tile[j]],
                                      k.g0h[:], k.g0l[:])
                last.then_inc(s.logits, 1)
                for n in range(2):
                    w = slice(2 * HID0 + n * P, 2 * HID0 + (n + 1) * P)
                    blocks.tensor_down(pe, it * 2 + n, n, P, [(j * P, (j + 1) * P) for j in range(T)],
                                       lambda j: pK[:, tile[j]], k.sh0h[:, w], k.sh0l[:, w], n == 0, True)
                pe.wait_ge(s.logits_read, it + 1)
                pe.wait_ge(s.done, it + 1)


def layer0_route(nc, k, d):
    s = Names(**{n: k.sem("route_" + n) for n in ("centred", "exp", "mask", "ranks", "index", "sent", "split")})
    jobs = [(d.wa1[:, 4 * P:8 * P], k.wkh[:, 0:4 * P], k.wkl[:, 0:4 * P]),
            (d.wa1[:, 8 * P:9 * P], k.wkh[:, 4 * P:5 * P], k.wkl[:, 4 * P:5 * P]),
            (d.brow[:, 4 * P:8 * P], k.bkh[:], k.bkl[:])]
    for src, h, l in ((d.w1, k.w1h, k.w1l), (d.w2, k.w2h, k.w2l)):
        jobs += [(src[:, c:c + 864], h[:, c:c + 864], l[:, c:c + 864]) for c in range(0, NB1 * W1C, 864)]
    sync_w, scalar_w, vector_w = load_and_split(nc, k, "route_w", jobs)
    sync_k, scalar_k, vector_k, tensor_k = layer1_keys(nc, k, d)
    flat = lambda a: a.rearrange("p t n -> p (t n)")
    r = k.route
    full = [P, SEQS, E0]
    with nc.Block() as block:
        @block.sync
        def _(sp):
            sync_w(sp, 0, 5)
            sync_k(sp)
            sync_w(sp, 5)

        @block.vector
        def _(v):
            g8 = r.gmask[:]
            topk_mask(v, k.sc[:, :, 0:G0], r.m8, K0, g8, r.t8a[:], r.t8b[:], r.t8c[:], r.cnt[:],
                      k.const0[:, L_R8:L_R8 + SEQS * G0])
            v.tensor_tensor(r.es[:], k.sc[:, :, G0:G0 + E0],
                            k.rows[:, B_BIAS0:B_BIAS0 + E0].unsqueeze(1).to_broadcast(full), ALU.add)
            v.tensor_scalar(r.t8a[:], g8, 1e9, -1e9, ALU.mult, ALU.add)
            v.drain()
            groups = r.es[:].rearrange("p t (g f) -> p (t g) f", f=E0 // G0)
            per_group = lambda a: flat(a).unsqueeze(2).to_broadcast([P, SEQS * G0, E0 // G0])
            v.tensor_tensor(groups, groups, per_group(g8), ALU.mult)
            v.drain()
            v.tensor_tensor(groups, groups, per_group(r.t8a[:]), ALU.add)
            v.drain()
            topk_mask(v, r.es[:], r.m8, K0, r.mask[:], r.gt[:], r.eq[:], r.pre[:], r.cnt[:],
                      k.const0[:, L_R32:L_R32 + SEQS * E0])
            v.tensor_copy(r.maskb[:], flat(r.mask[:])).then_inc(s.mask, 1)
            v.tensor_tensor(r.es[:], r.es[:], r.m8[:, :, 0:1].to_broadcast(full), ALU.subtract).then_inc(s.centred, 1)
            v.tensor_tensor_scan(flat(r.pre[:]), k.const0[:, L_R32:L_R32 + SEQS * E0], flat(r.mask[:]), 0.0,
                                 ALU.mult, ALU.add)
            v.drain()
            v.tensor_tensor(r.pre[:], r.pre[:], r.mask[:], ALU.mult)
            v.wait_ge(s.ranks, 1)
            v.tensor_copy(r.tot[:], k.ps[1][:].rearrange("p (t n) -> p n t", n=E0))
            v.drain()
            v.tensor_tensor_scan(flat(r.cum[:]), k.const0[:, L_R16T:L_R16T + SEQS * E0], flat(r.tot[:]), 0.0,
                                 ALU.mult, ALU.add)
            v.drain()
            v.tensor_tensor(r.cum[:], r.cum[:], r.tot[:], ALU.subtract)
            v.drain()
            v.tensor_tensor(r.slot[:], k.ps[0][:].rearrange("p (t n) -> p t n", n=E0),
                            r.cum[:].rearrange("p n t -> p t n"), ALU.add)
            v.drain()
            v.tensor_scalar(r.gt[:], r.slot[:], float(CAP), None, ALU.is_lt)
            v.tensor_tensor(r.slot[:], r.slot[:], k.const0[:, L_START:L_START + E0].unsqueeze(1).to_broadcast(full), ALU.add)
            v.drain()
            v.scalar_tensor_tensor(r.slot[:], r.slot[:], k.const0[:, L_TRASH:L_TRASH + 1], r.gt[:],
                                   ALU.subtract, ALU.mult)
            v.drain()
            for n in range(K0):
                v.scalar_tensor_tensor(r.eq[:], r.pre[:], n + 1.0, r.slot[:], ALU.is_equal, ALU.mult)
                v.drain()
                v.reduce_sum(r.sl[:, n, :], r.eq[:], axis=AX.X)
                v.drain()
            sl = r.sl[:].rearrange("p k t -> p (k t)")
            v.tensor_scalar(k.index[:], sl, k.const0[:, L_TRASH:L_TRASH + 1], None, ALU.add)
            v.scalar_tensor_tensor(r.own[:], sl, 0.0, k.const0[:, L_SPREAD:L_SPREAD + K0 * SEQS], ALU.is_equal, ALU.mult)
            v.drain()
            v.scalar_tensor_tensor(r.dest[:], sl, k.const0[:, L_TRASH:L_TRASH + 1], r.own[:], ALU.add, ALU.add)\
                .then_inc(s.index, 1)
            v.wait_ge(s.exp, 1)
            v.tensor_tensor(r.es[:], r.es[:], r.mask[:], ALU.mult)
            v.drain()
            v.reduce_sum(r.cnt[:], r.es[:], axis=AX.X)
            v.drain()
            v.reciprocal(r.rec[:], r.cnt[:])
            v.tensor_tensor(r.es[:], r.es[:], r.gt[:], ALU.mult)
            v.drain()
            v.tensor_scalar(r.rec[:], r.rec[:], k.tg[:, 4:5], None, ALU.mult)
            v.drain()
            v.tensor_tensor(r.es[:], r.es[:], r.rec[:].unsqueeze(2).to_broadcast(full), ALU.mult)
            v.drain()
            for n in range(K0):
                v.scalar_tensor_tensor(r.eq[:], r.pre[:], n + 1.0, r.es[:], ALU.is_equal, ALU.mult)
                v.drain()
                v.reduce_sum(k.gate[:, n, :], r.eq[:], axis=AX.X)
                v.drain()
            vector_w(v, 0, 3)
            v.drain().then_inc(s.split, 1)
            vector_k(v)
            vector_w(v, 3)

        @block.scalar
        def _(act):
            act.wait_ge(s.centred, 1)
            act.activation(r.es[:], r.es[:], ACT.Exp).then_inc(s.exp, 1)
            act.activation(k.one_r[:], k.const0[0:33, L_ONE:L_ONE + P], ACT.Copy)
            for j in range(T):
                act.activation(k.one_k[:, j * P:(j + 1) * P], k.const0[0:1, L_ONE:L_ONE + P], ACT.Copy)
            scalar_w(act, 0, 3)
            scalar_k(act)
            scalar_w(act, 3)

        @block.tensor
        def _(pe):
            pe.wait_ge(s.mask, 1)
            pe.matmul(k.ps[0][:], k.ub[:, 0:P], r.maskb[:], start=True, stop=True)
            pe.matmul(k.ps[1][:], k.ub[:, P:2 * P], r.maskb[:], start=True, stop=True).then_inc(s.ranks, 1)
            pe.wait_ge(s.split, 1)
            tensor_k(pe)

        @block.gpsimd
        def _(g):
            g.wait_ge(s.index, 1)
            for n in range(K0):
                for t in range(SEQS):
                    c = n * SEQS + t
                    g.indirect_dma_start(
                        out=d.buf[:, :], out_offset=bass.IndirectOffsetOnAxis(ap=r.dest[:, c:c + 1].bitcast(U32), axis=0),
                        in_=k.xn_all[:, t, :], in_offset=None).then_inc(s.sent, 16)
            g.wait_ge(s.sent, 16 * K0 * SEQS)


def layer0_experts(nc, k, d):
    s = Names(**{n: k.sem("ex_" + n) for n in (
        "gu0", "gu1", "dn0", "dn1", "rows0", "rows1", "gu_free", "dn_free", "rows_free", "gu_split", "dn_split",
        "turned", "x_hi", "x_lo", "out_sb", "stored0", "stored1")})
    raw_gu, raw_dn, rows, stored = (s.gu0, s.gu1), (s.dn0, s.dn1), (s.rows0, s.rows1), (s.stored0, s.stored1)
    e_ = k.ex
    blocks = Blocks(k, "ex_blk", k.gu, k.s, e_.h, e_.hh, e_.hl)
    pX, pO = (k.ps[4], k.ps[7]), (k.ps[5], k.ps[6])
    starts = [j * RT for j in range(3)]
    tiles = [(c, c + m) for c, m in zip(starts, ROWS)]
    last = E0 - 1

    def experts(i, first):
        return [(i * 2 + first, i, first), (i * 2 + first + 1, i + (first + 1) // 2, (first + 1) % 2)]

    with nc.Block() as block:
        @block.sync
        def _(sp):
            def load(e, half, q):
                sp.wait_ge(s.gu_free, e + 1)
                sp.dma_start(e_.raw_gu[q][:], d.w0[e, :, 0:2 * HID0]).then_inc(raw_gu[q], 16)
                sp.wait_ge(s.rows_free, e + 1)
                sp.dma_start(e_.rows[q][0:RT, 0:2, :],
                             d.buf[bass.ds(e * CAP, 2 * RT), :].rearrange("(r p) d -> p r d", p=RT)).then_inc(rows[q], 16)
                sp.dma_start(e_.rows[q][0:ROWS[2], 2, :],
                             d.buf[bass.ds(e * CAP + 2 * RT, ROWS[2]), :]).then_inc(rows[q], 16)
                sp.wait_ge(s.dn_free, e + 1)
                sp.dma_start(e_.raw_dn[q][:], d.w0[e, :, 2 * HID0:3 * HID0]).then_inc(raw_dn[q], 16)

            def store(e, half, q):
                sp.wait_ge(s.out_sb, e + 3)
                sp.dma_start(d.oute[bass.ds(e * CAP, 2 * RT), :].rearrange("(r p) d -> p r d", p=RT),
                             e_.out[q][0:RT, 0:2, :]).then_inc(stored[q], 16)
                sp.dma_start(d.oute[bass.ds(e * CAP + 2 * RT, ROWS[2]), :],
                             e_.out[q][0:ROWS[2], 2, :]).then_inc(stored[q], 16)

            for e in range(4):
                load(e, e // 2, e % 2)
            with sp.Fori(0, E0 // 2 - 2) as i:
                for e, half, q in experts(i, 0):
                    load(e + 4, half + 2, q)
                    store(e, half, q)
            for e in range(E0 - 4, E0):
                store(e, e // 2, e % 2)
            for q in range(2):
                sp.wait_ge(stored[q], 1 + 16 * E0)

        @block.gpsimd
        def _(g):
            with g.Fori(0, E0 // 2) as i:
                for e, half, q in experts(i, 0):
                    for n in range(2):
                        blocks.pool_lo(g, e * 2 + n, 2 * q + n, P, CAP)

        @block.vector
        def _(v):
            def split(e, half, q, raw, loaded, hi, lo, done, free):
                v.wait_ge(loaded, half * 16 + 16)
                v.tensor_copy(hi[:], raw[:])
                v.drain()
                v.tensor_tensor(lo[:], raw[:], hi[:].bitcast(F32), ALU.subtract).then_inc(done, 1)
                v.drain().then_inc(free, 1)

            def split_gu(e, half, q, used=True):
                if used:
                    v.wait_ge(blocks.gu_ready, e * 2 - 2)
                split(e, half, q, e_.raw_gu[q], raw_gu[q], e_.guh[q], e_.gul[q], s.gu_split, s.gu_free)

            def split_dn(e, half, q):
                v.wait_ge(blocks.h_free, e * 2 + 2)
                split(e, half, q, e_.raw_dn[q], raw_dn[q], e_.dnh[q], e_.dnl[q], s.dn_split, s.dn_free)

            def x_low(e, half, q):
                v.wait_ge(s.x_hi, e + 1)
                v.tensor_tensor(e_.xl[q][:], pX[q][:, 0:CAP], e_.xh[q][:].bitcast(F32), ALU.subtract).then_inc(s.x_lo, 1)
                v.drain().then_inc(s.rows_free, 1)

            def turn(e, half, q, gu=True, more=True):
                for n in range(2):
                    blocks.vector_h(v, e * 2 + n, n, 2 * q + n, P, CAP, 4)
                if more:
                    x_low(e + 1, half + q, 1 - q)
                if gu:
                    split_gu(e + 2, half + 1, q)
                if more:
                    split_dn(e + 1, half + q, 1 - q)

            blocks.credits(v)
            for sem in (s.gu_free, s.dn_free, s.rows_free, s.out_sb):
                v.sem_inc(sem, 2)
            for q in range(2):
                v.sem_inc(stored[q], 1)
            split_gu(0, 0, 0, used=False)
            x_low(0, 0, 0)
            split_gu(1, 0, 1, used=False)
            split_dn(0, 0, 0)
            with v.Fori(0, E0 // 2 - 1) as i:
                for e, half, q in experts(i, 0):
                    turn(e, half, q)
            turn(last - 1, last // 2, 0, gu=False)
            turn(last, last // 2, 1, gu=False, more=False)

        @block.scalar
        def _(act):
            def x_high(e, q):
                act.wait_ge(s.turned, e + 1)
                act.activation(e_.xh[q][:], pX[q][:, 0:CAP], ACT.Copy).then_inc(s.x_hi, 1)

            def out(e, half, q):
                act.wait_ge(blocks.h_free, e * 2 + 6)
                act.wait_ge(stored[q], half * 32 + 1)
                act.activation(e_.out[q][0:RT, 0:2, :], pO[q][0:RT, 0:2 * P].rearrange("p (r d) -> p r d", d=P), ACT.Copy)
                act.activation(e_.out[q][0:ROWS[2], 2, :], pO[q][0:ROWS[2], 2 * P:3 * P], ACT.Copy)
                act.drain().then_inc(s.out_sb, 1)

            def turn(e, half, q, x=True, before=None):
                for n in range(2):
                    blocks.scalar_silu(act, e * 2 + n, n, P, CAP)
                if x:
                    x_high(e + 1, 1 - q)
                for n in range(2):
                    blocks.scalar_hi(act, e * 2 + n, 2 * q + n, P, CAP)
                if before is not None:
                    out(*before)

            x_high(0, 0)
            turn(0, 0, 0)
            with act.Fori(0, E0 // 2 - 1) as i:
                for e, half, q in experts(i, 1):
                    turn(e, half, q, before=(e - 1, half if q else half - 1, 1 - q))
            turn(last, last // 2, 1, x=False, before=(last - 1, last // 2, 0))
            out(last, last // 2, 1)

        @block.tensor
        def _(pe):
            def rows_turned(e, half, q):
                pe.wait_ge(rows[q], half * 32 + 32)
                for j, m in enumerate(ROWS):
                    last = pe.transpose(pX[q][:, starts[j]:starts[j] + m], e_.rows[q][0:m, j, :], k.ident[0:m, 0:m])
                last.then_inc(s.turned, 1)

            def gate_up(e, half, q):
                pe.wait_ge(s.gu_split, e + 1)
                pe.wait_ge(s.x_lo, e + 1)
                for n in range(2):
                    blocks.tensor_gu(pe, e * 2 + n, n, e_.guh[q], e_.gul[q], n * P, HID0 + n * P, P, e_.xh[q][:], e_.xl[q][:])

            def down(e, half, q):
                pe.wait_ge(s.dn_split, e + 1)
                pe.wait_ge(s.out_sb, e + 1)
                for n in range(2):
                    w = slice(n * P, (n + 1) * P)
                    blocks.tensor_down(pe, e * 2 + n, 2 * q + n, P, tiles,
                                       lambda j: pO[q][0:ROWS[j], j * P:(j + 1) * P],
                                       e_.dnh[q][:, w], e_.dnl[q][:, w], n == 0, True)

            rows_turned(0, 0, 0)
            gate_up(0, 0, 0)
            rows_turned(1, 0, 1)
            with pe.Fori(0, E0 // 2 - 1) as i:
                for e, half, q in experts(i, 1):
                    gate_up(e, half, q)
                    rows_turned(e + 1, half + q, 1 - q)
                    down(e - 1, half if q else half - 1, 1 - q)
            gate_up(last, last // 2, 1)
            down(last - 1, last // 2, 0)
            down(last, last // 2, 1)


def layer0_combine(nc, k, d):
    RING = 16
    got = [k.sem(f"comb_got{i}") for i in range(4)]
    used = k.sem("comb_used")
    jobs = [(d.w3[e], k.w3h[:, e * W3C:(e + 1) * W3C], k.w3l[:, e * W3C:(e + 1) * W3C]) for e in range(E3 + 1)]
    jobs += [(d.wa1[:, 0:4 * P], k.wa1h[:, 0:4 * P], k.wa1l[:, 0:4 * P]),
             (d.wa1[:, 9 * P:10 * P], k.wa1h[:, 4 * P:5 * P], k.wa1l[:, 4 * P:5 * P]),
             (d.gates, k.gth[:], k.gtl[:]), (d.sel, k.selh[0:E1, :], None), (d.brow[:, 0:4 * P], k.bqh, k.bql)]
    sync_w, scalar_w, vector_w = load_and_split(nc, k, "comb_w", jobs)
    with nc.Block() as block:
        @block.sync
        def _(sp):
            sync_w(sp)

        @block.scalar
        def _(act):
            scalar_w(act)

        @block.gpsimd
        def _(g):
            for i in range(SEQS * K0):
                t, n = divmod(i, K0)
                if i >= RING and i % 4 == 0:
                    g.wait_ge(used, (i - RING) // 4 + 1)
                c = n * SEQS + t
                g.indirect_dma_start(
                    out=k.y[:, i % RING, :], out_offset=None, in_=d.oute[:, :],
                    in_offset=bass.IndirectOffsetOnAxis(ap=k.index[:, c:c + 1].bitcast(U32), axis=0)).then_inc(got[t % 4], 16)

        @block.vector
        def _(v):
            vector_w(v)
            for t in range(SEQS):
                v.wait_ge(got[t % 4], 16 * K0 * (t // 4 + 1))
                for n in range(K0):
                    v.scalar_tensor_tensor(k.x[:, t, :], k.y[:, (t * K0 + n) % RING, :], k.gate[:, n, t:t + 1],
                                           k.x[:, t, :], ALU.mult, ALU.add)
                    last = v.drain()
                last.then_inc(used, 1)


def layer1_keys(nc, k, d):
    s = Names(**{n: k.sem("key_" + n) for n in (
        "loaded", "free", "hi", "lo", "k", "high", "done", "v", "v_done", "v_stored")})
    k_stored = [k.sem(f"key_stored{i}") for i in range(2)]
    bank = (k.ps[2], k.ps[3])
    pV = k.ps[4]
    tile = [slice(j * P, (j + 1) * P) for j in range(T)]

    def sync(sp):
        with sp.Fori(0, CHUNKS) as it:
            sp.wait_ge(s.free, it + 1)
            sp.dma_start(k.ctx1[:], d.ctxT[:, bass.ds(it * CW, CW)]).then_inc(s.loaded, 16)
            for q in range(4):
                sp.wait_ge(s.done, it * 4 + q + 3)
                sp.dma_start(d.keys1[bass.ds(it * T, T), :, q * P:(q + 1) * P].rearrange("j p t -> p j t"),
                             k.k3[q % 2][:].bitcast(F32).rearrange("p (j t) -> p j t", t=P)).then_inc(k_stored[q % 2], 16)
            sp.wait_ge(s.v_done, it + 1)
            sp.dma_start(d.values1[bass.ds(it * T, T), :, :].rearrange("j p c -> p j c"),
                         k.v9k[:].rearrange("p j h d -> p j (h d)")).then_inc(s.v_stored, 16)
        for q in range(2):
            sp.wait_ge(k_stored[q], CHUNKS * 32 + 1)
        sp.wait_ge(s.v_stored, CHUNKS * 16 + 1)

    def scalar(act):
        with act.Fori(0, CHUNKS) as it:
            act.wait_ge(s.loaded, it * 16 + 16)
            act.wait_ge(s.v, it + 1)
            act.activation(k.cth[:], k.ctx1[:], ACT.Copy).then_inc(s.hi, 1)
            for q in range(4):
                act.wait_ge(s.k, it * 4 + q + 1)
                act.activation(k.kh[q % 2][:], bank[q % 2][:], ACT.Copy).then_inc(s.high, 1)

    def vector(v):
        v.memset(k.v9k[:], 1.0)
        for sem in (s.free, s.v, s.v_stored, k_stored[0], k_stored[1]):
            v.sem_inc(sem, 1)
        v.sem_inc(s.done, 2)
        v.drain()
        with v.Fori(0, CHUNKS) as it:
            v.wait_ge(s.hi, it + 1)
            v.tensor_tensor(k.ctl[:], k.ctx1[:], k.cth[:].bitcast(F32), ALU.subtract).then_inc(s.lo, 1)
            v.drain().then_inc(s.free, 1)
            for q in range(4):
                v.wait_ge(s.high, it * 4 + q + 1)
                v.wait_ge(k_stored[q % 2], it * 32 + q // 2 * 16 + 1)
                v.scalar_tensor_tensor(k.k3[q % 2][:], k.kh[q % 2][:].bitcast(F32), k.const[:, C_SPLIT + 1:C_SPLIT + 2],
                                       bank[q % 2][:], ALU.mult, ALU.add).then_inc(s.done, 1)
            v.wait_ge(s.v, it + 2)
            v.wait_ge(s.v_stored, it * 16 + 1)
            for j in range(T):
                last = v.tensor_tensor(k.v9k[:, j, :, 0:HD], pV[:, tile[j]].rearrange("p (h d) -> p h d", d=HD),
                                       k.rows[:, B_BV1:B_BV1 + P].rearrange("p (h d) -> p h d", d=HD), ALU.add)
            last.then_inc(s.v_done, 1)

    def tensor(pe):
        with pe.Fori(0, CHUNKS) as it:
            pe.wait_ge(s.lo, it + 1)
            for q in range(4):
                c = slice(q * P, (q + 1) * P)
                pe.wait_ge(s.done, it * 4 + q + 1)
                three_pass(pe, bank[q % 2][:], k.wkh[:, c], k.wkl[:, c], k.cth[:], k.ctl[:], stop=False)
                pe.matmul(bank[q % 2][:], k.bkh[:, c], k.one_k[:], start=False, stop=False)
                pe.matmul(bank[q % 2][:], k.bkl[:, c], k.one_k[:], start=False, stop=True).then_inc(s.k, 1)
            for j in range(T):
                last = three_pass(pe, pV[:, tile[j]], k.cth[:, tile[j]], k.ctl[:, tile[j]],
                                  k.wkh[:, 4 * P:5 * P], k.wkl[:, 4 * P:5 * P])
            last.then_inc(s.v, 1)
            pe.wait_ge(s.v_done, it + 1)

    return sync, scalar, vector, tensor


def layer0_experts_all(nc, k, d, sb):
    with ExitStack() as rt:
        r = k.route = Names()
        r.m8 = sb("r_m8", [P, SEQS, 8], c=rt)
        r.gmask, r.t8a, r.t8b, r.t8c = (sb("r_" + n, [P, SEQS, 8], c=rt) for n in ("gmask", "t8a", "t8b", "t8c"))
        r.cnt, r.rec = sb("r_cnt", [P, SEQS], c=rt), sb("r_rec", [P, SEQS], c=rt)
        r.sl, r.own = sb("r_sl", [P, K0, SEQS], c=rt), sb("r_own", [P, K0 * SEQS], c=rt)
        r.dest = sb("r_dest", [P, K0 * SEQS], I32, rt)
        r.es, r.mask, r.gt, r.eq, r.pre, r.slot = (
            sb("r_" + n, [P, SEQS, E0], c=rt) for n in ("es", "mask", "gt", "eq", "pre", "slot"))
        r.tot, r.cum = sb("r_tot", [P, E0, SEQS], c=rt), sb("r_cum", [P, E0, SEQS], c=rt)
        r.maskb = sb("r_maskb", [P, SEQS * E0], BF16, rt)
        k.wkh, k.wkl = sb("wkh", [P, 5 * P], F32R, rt), sb("wkl", [P, 5 * P], F32R, rt)
        k.bkh, k.bkl = sb("bkh", [1, 4 * P], F32R, rt), sb("bkl", [1, 4 * P], F32R, rt)
        k.ctx1, k.one_k = sb("ctx1", [P, CW], c=rt), sb("one_k", [1, CW], F32R, rt)
        k.cth, k.ctl = sb("cth", [P, CW], F32R, rt), sb("ctl", [P, CW], F32R, rt)
        k.kh, k.k3 = ([sb(f"{n}{i}", [P, CW], F32R, rt) for i in range(2)] for n in ("kh", "k3"))
        k.v9k = sb("v9k", [P, T, HEADS, HD + 1], c=rt)
        layer0_route(nc, k, d)
    with ExitStack() as ex:
        e = k.ex = Names()
        two = lambda name, shape, dt=F32: [sb(f"e_{name}{i}", shape, dt, ex) for i in range(2)]
        e.raw_gu, e.raw_dn, e.rows = two("rgu", [P, 2 * HID0]), two("rdn", [P, HID0]), two("rows", [P, 3, P])
        e.guh, e.gul = two("guh", [P, 2 * HID0], F32R), two("gul", [P, 2 * HID0], F32R)
        e.dnh, e.dnl = two("dnh", [P, HID0], F32R), two("dnl", [P, HID0], F32R)
        e.xh, e.xl = two("xh", [P, CAP], F32R), two("xl", [P, CAP], F32R)
        e.out = two("out", [P, 3, P])
        e.h = [sb(f"e_h{i}", [P, CAP], c=ex) for i in range(4)]
        e.hh = [sb(f"e_hh{i}", [P, CAP], F32R, ex) for i in range(4)]
        e.hl = [sb(f"e_hl{i}", [P, CAP], F32R, ex) for i in range(4)]
        layer0_experts(nc, k, d)


class Line:
    SLOTS_GU, SLOTS_H, SLOTS_HH = 2, 2, 3

    def __init__(self, k):
        self.k = k
        self.gu_ready = k.sem("line_gu_ready")
        self.gu_free = k.sem("line_gu_free")
        self.silu = k.sem("line_silu")
        self.h_ready = k.sem("line_h_ready")
        self.hi = k.sem("line_hi")
        self.lo = k.sem("line_lo")
        self.down_done = k.sem("line_down_done")
        self.cb, self.cb_free = k.sem("line_cb"), k.sem("line_cb_free")
        self.sum_a = k.sem("line_sum_a")
        self.sum_b = k.sem("line_sum_b")
        self.sum_read = k.sem("line_sum_read")

    def credits(self, v):
        v.sem_inc(self.gu_free, self.SLOTS_GU)
        v.sem_inc(self.lo, self.SLOTS_H)
        v.sem_inc(self.down_done, self.SLOTS_HH)
        v.sem_inc(self.cb_free, 1)
        v.sem_inc(self.sum_read, 1)


STEPS = T * 4 + 2
FILLERS = dict([("norm0", 1), ("turned0", 1)] + [(f"step{u}", 1) for u in range(2, 14)] +
               [("heads", 1), ("out", 1), ("x1", 1), ("logits1", 1), ("groups1", 1), ("weights1", 1), ("sum1", 2),
                ("x2", 1), ("logits2", 1), ("sum2", 2), ("norm4", 1)])
B3 = [(e, m) for e in range(E3 + 1) for m in range(3)]


def turn_order(a, b):
    order, left = [], list(range(len(B3)))
    if not a:
        return [(3, n, n % 2) for n in left]
    for name in FILLERS:
        attends = name.startswith("step") or name in ("norm0", "turned0")
        if b:
            order += [(3, left.pop(0), 0 if attends else (len(order) + i) % 2) for i in range(FILLERS[name])]
        if name in ("weights1", "logits2"):
            order += [(1 if name == "weights1" else 2, n, (len(order) + n) % 2) for n in range(NB1)]
    assert not (b and left)
    return order


class Part:

    def __init__(self, line, eng, n0, it, a=True, b=True):
        self.line, self.k, self.eng, self.n0, self.it, self.b = line, line.k, eng, n0, it, b
        self.order = turn_order(a, b)
        self.at = 0
        self.done = 0

    def rows(self, p):
        layer, n, _ = self.order[p]
        return M3[B3[n][1]] if layer == 3 else P

    def fill(self, name):
        if self.b:
            for _ in range(FILLERS[name]):
                self.block()

    def flush(self):
        while self.done < self.at:
            self.late(True)


class TensorPart(Part):
    def up(self):
        pe, k, line, p = self.eng, self.k, self.line, self.at
        layer, n, g = self.order[p]
        before = [q for q in range(p) if self.order[q][2] == g]
        back = p - before[-1] if before else p + 1
        m = self.rows(p)
        if layer == 3:
            e, part = B3[n]
            wh, wl, x = k.w3h, k.w3l, (k.xbh, k.xbl)
            g0 = e * W3C + part * P
            u0 = g0 + FF3
        else:
            wh, wl = (k.w1h, k.w1l) if layer == 1 else (k.w2h, k.w2l)
            x = (k.xh, k.xl)
            g0 = n * W1C
            u0 = g0 + P
        pe.wait_ge(line.gu_free, self.n0 + (p + 1 + line.SLOTS_GU - back))
        for c0, bank in ((g0, 0), (u0, 1)):
            last = three_pass(pe, k.gu[g][bank][0:m, :], wh[:, c0:c0 + m], wl[:, c0:c0 + m], x[0][:], x[1][:])
        last.then_inc(line.gu_ready, 1)
        self.at += 1

    def weights(self):
        pe, k, line = self.eng, self.k, self.line
        layer, b, _ = self.order[self.at - 1]
        if b < NB1 - 1:
            pe.wait_ge(line.cb_free, self.it * (2 * (NB1 - 1)) + ((layer - 1) * (NB1 - 1) + b + 1))
            sel = k.selh[0:E1, b * P:(b + 1) * P]
            pe.matmul(k.ps[5][:], sel, k.wTl, start=True, stop=False)
            pe.matmul(k.ps[5][:], sel, k.wTh, start=False, stop=True).then_inc(line.cb, 1)

    def late(self, now=False):
        pe, k, line, p = self.eng, self.k, self.line, self.done
        if not now and self.at - p <= 2:
            return
        layer, n, _ = self.order[p]
        if layer == 3:
            e, m = B3[n]
            c = e * W3C + 2 * FF3 + m * P
            wh, wl, out, first, last_one = k.w3h, k.w3l, k.ps[7], m == 0, m == 2
            if first:
                pe.wait_ge(line.sum_read, (self.it - 1) * (E3 + 1) + (e + 1))
        else:
            wh, wl = (k.w1h, k.w1l) if layer == 1 else (k.w2h, k.w2l)
            c = n * W1C + 2 * P
            out, first, last_one = k.ps[6], n == 0, n == NB1 - 1
        m, s = self.rows(p), p % line.SLOTS_HH
        pe.wait_ge(line.lo, self.n0 + (p + 1 + line.SLOTS_H))
        for j in range(T):
            t = slice(j * P, (j + 1) * P)
            last = three_pass(pe, out[:, t], k.hh[s][0:m, t], k.hl[s][0:m, t], wh[0:m, c:c + P], wl[0:m, c:c + P],
                              start=first and j == 0, stop=True, skip=True)
        last.then_inc(line.down_done, 1)
        if last_one:
            pe.drain().then_inc(line.sum_b if layer == 3 else line.sum_a, 1)
        self.done += 1

    def block(self):
        self.up()
        self.late()


class ScalarPart(Part):
    def silu(self):
        k, line, p = self.k, self.line, self.at
        g, m = self.order[p][2], self.rows(p)
        self.eng.wait_ge(line.gu_ready, self.n0 + (p + 1))
        self.eng.activation(k.s[g][0:m, :], k.gu[g][0][0:m, :], ACT.Silu).then_inc(line.silu, 1)
        self.at += 1

    def late(self, now=False):
        k, line, p = self.k, self.line, self.done
        if not now and self.at - p <= 1:
            return
        m, s = self.rows(p), p % line.SLOTS_HH
        self.eng.wait_ge(line.down_done, self.n0 + (p + 1))
        self.eng.wait_ge(line.h_ready, self.n0 + (p + 1))
        self.eng.activation(k.hh[s][0:m, :], k.h[p % line.SLOTS_H][0:m, :], ACT.Copy).then_inc(line.hi, 1)
        self.done += 1

    def block(self):
        self.silu()
        self.late()


class PoolPart(Part):
    def late(self, now=False):
        k, line, p = self.k, self.line, self.done
        if not now and self.at - p <= 1:
            return
        m, s = self.rows(p), p % line.SLOTS_HH
        self.eng.wait_ge(line.hi, self.n0 + (p + 1))
        self.eng.tensor_tensor(k.hl[s][0:m, :], k.h[p % line.SLOTS_H][0:m, :], k.hh[s][0:m, :].bitcast(F32),
                               ALU.subtract).then_inc(line.lo, 1)
        self.done += 1

    def block(self):
        self.at += 1
        self.late()


class VectorPart(Part):
    def late(self, now=False):
        v, k, line, p = self.eng, self.k, self.line, self.done
        if not now and self.at - p <= 2:
            return
        self.done += 1
        layer, n, _ = self.order[p]
        if layer != 3 or B3[n][1] != 2:
            return
        e = B3[n][0]
        v.wait_ge(line.sum_b, (self.it - 1) * (E3 + 1) + (e + 1))
        if e == 0:
            v.tensor_copy(k.acc[:], k.ps[7][:].rearrange("p (t d) -> p t d", d=P))
        else:
            for j in range(T):
                v.scalar_tensor_tensor(k.acc[:, j, :], k.ps[7][:, j * P:(j + 1) * P], k.c8[:, j, e - 1:e],
                                       k.acc[:, j, :], ALU.mult, ALU.add)
        v.drain().then_inc(line.sum_read, 1)

    def block(self):
        v, k, line, p = self.eng, self.k, self.line, self.at
        self.late()
        layer, b, g = self.order[p]
        m = self.rows(p)
        hid = k.h[p % line.SLOTS_H][0:m, :]
        v.wait_ge(line.lo, self.n0 + (p + 1))
        v.wait_ge(line.silu, self.n0 + (p + 1))
        v.tensor_tensor(hid, k.s[g][0:m, :], k.gu[g][1][0:m, :], ALU.mult).then_inc(line.gu_free, 1)
        if layer < 3 and b < NB1 - 1:
            v.drain()
            v.wait_ge(line.cb, self.it * (2 * (NB1 - 1)) + ((layer - 1) * (NB1 - 1) + b + 1))
            v.tensor_tensor(hid, hid, k.ps[5][:], ALU.mult).then_inc(line.cb_free, 1)
        v.drain().then_inc(line.h_ready, 1)
        self.at += 1


class Gate:

    def __init__(self, k, norm):
        self.k, self.norm = k, norm
        (self.turned, self.hi, self.lo, self.logits, self.act, self.centred, self.ready, self.wT, self.wT_hi,
         self.wT_lo) = (k.sem("gate_" + n) for n in (
            "turned", "hi", "lo", "logits", "act", "centred", "ready", "wT", "wT_hi", "wT_lo"))
        self.n = (E1, E1, E3)
        self.c0 = (0, E1, 2 * E1)
        self.x = ((k.xh, k.xl), (k.xh, k.xl), (k.xbh, k.xbl))
        self.fills = (("x1", "logits1", "groups1", "weights1"), ("x2", "logits2", None, None), (None,) * 4)

    def fill(self, part, l, point):
        if self.fills[l][point]:
            part.fill(self.fills[l][point])

    def tensor(self, pe, part, it, l, norm_at):
        k, a, n, c0, (xh, xl) = self.k, it * 3 + l, self.n[l], self.c0[l], self.x[l]
        pe.wait_ge(self.norm.ready, norm_at + 1)
        for j in range(T):
            last = pe.transpose(k.ps[4][:, j * P:(j + 1) * P], k.xn[:, j, :], k.ident)
        last.then_inc(self.turned, 1)
        self.fill(part, l, 0)
        pe.wait_ge(self.lo, a + 1)
        for j in range(T):
            c = slice(j * P, (j + 1) * P)
            last = three_pass(pe, k.ps[5][:, j * n:(j + 1) * n], xh[:, c], xl[:, c],
                              k.gth[:, c0:c0 + n], k.gtl[:, c0:c0 + n])
        last.then_inc(self.logits, 1)
        for point in (1, 2, 3):
            self.fill(part, l, point)

    def tensor_weights(self, pe, it, l):
        k = self.k
        pe.wait_ge(self.ready, it * 3 + l + 1)
        for j in range(T):
            last = pe.transpose(k.ps[4][0:E1, j * P:(j + 1) * P], k.c16[:, j, :], k.ident)
        last.then_inc(self.wT, 1)
        pe.wait_ge(self.wT_lo, it * 2 + l + 1)

    def scalar(self, act, part, it, l):
        k, a, n = self.k, it * 3 + l, self.n[l]
        act.wait_ge(self.turned, a + 1)
        act.activation(self.x[l][0][:], k.ps[4][:], ACT.Copy).then_inc(self.hi, 1)
        self.fill(part, l, 0)
        if l == 0:
            act.wait_ge(self.logits, a + 1)
            act.activation(k.sg[:], k.ps[5][:, 0:T * n].rearrange("p (t n) -> p t n", n=n), ACT.Sigmoid).then_inc(self.act, 1)
        else:
            act.wait_ge(self.centred, it * 2 + l)
            sg = k.sg[:, :, 0:n]
            act.activation(sg, sg, ACT.Exp).then_inc(self.act, 1)
        for point in (1, 2, 3):
            self.fill(part, l, point)

    def scalar_weights(self, act, it, l):
        act.wait_ge(self.wT, it * 2 + l + 1)
        act.activation(self.k.wTh, self.k.ps[4][0:E1, :], ACT.Copy).then_inc(self.wT_hi, 1)

    def pool(self, part, l):
        for point in range(4):
            self.fill(part, l, point)

    def vector(self, v, part, it, l):
        k, a, n = self.k, it * 3 + l, self.n[l]
        xh, xl = self.x[l]
        v.wait_ge(self.hi, a + 1)
        v.tensor_tensor(xl[:], k.ps[4][:], xh[:].bitcast(F32), ALU.subtract).then_inc(self.lo, 1)
        self.fill(part, l, 0)
        sg = k.sg[:, :, 0:n]
        each = lambda c: c.unsqueeze(2).to_broadcast([P, T, n])
        if l == 0:
            v.wait_ge(self.act, a + 1)
        else:
            lg = k.ps[5][:, 0:T * n].rearrange("p (t n) -> p t n", n=n)
            v.wait_ge(self.logits, a + 1)
            v.reduce_max(k.r1[:], lg, axis=AX.X)
            v.drain()
            v.tensor_tensor(sg, lg, each(k.r1[:]), ALU.subtract).then_inc(self.centred, 1)
            v.wait_ge(self.act, a + 1)
            v.reduce_sum(k.r1[:], sg, axis=AX.X)
            v.drain()
            v.reciprocal(k.r2[:], k.r1[:])
            v.drain()
            v.tensor_tensor(sg, sg, each(k.r2[:]), ALU.mult)
            v.drain()
        if l < 2:
            g4 = k.sg[:].rearrange("p t (g f) -> p (t g) f", f=4)
            if l == 0:
                for n0, n1, f0, f1, g0 in ((0, 3, 0, 3, 1), (3, 5, 0, 2, 2), (5, 6, 0, 1, 3)):
                    v.tensor_tensor(k.pairs[:, :, n0:n1], g4[:, :, f0:f1], g4[:, :, g0:g0 + f1 - f0], ALU.add)
                v.drain()
                v.reduce_max(k.g8[:, :, 0:4], k.pairs[:].rearrange("p (t g) f -> p t g f", g=4), axis=AX.X)
            else:
                v.reduce_max(k.g8[:, :, 0:4], k.sg[:].rearrange("p t (g f) -> p t g f", f=4), axis=AX.X)
            self.fill(part, l, 1)
            v.drain()
            topk_mask(v, k.g8[:], k.m8[:], 2, k.gm[:], k.q8[0][:], k.q8[1][:], k.q8[2][:], k.r1[:], k.const[:, C_R8:C_R8 + T * 8])
            inner = lambda x: x.unsqueeze(3).to_broadcast([P, T, 4, 4])
            ms = k.ms[:].rearrange("p t (g f) -> p t g f", f=4)
            v.tensor_tensor(ms, k.sg[:].rearrange("p t (g f) -> p t g f", f=4), inner(k.gm[:, :, 0:4]), ALU.mult)
            if l == 0:
                v.drain()
                v.tensor_scalar(k.gm[:], k.gm[:], 2.0, -2.0, ALU.mult, ALU.add)
                v.drain()
                v.tensor_tensor(ms, ms, inner(k.gm[:, :, 0:4]), ALU.add)
            self.fill(part, l, 2)
            v.drain()
            topk_mask(v, k.ms[:], k.m8[:], K1, k.mask[:], k.q16[0][:], k.q16[1][:], k.q16[2][:], k.r1[:],
                      k.const[:, C_R16:C_R16 + T * E1])
            mask, c = k.mask[:], k.c16[:]
        else:
            topk_mask(v, k.sg[:, :, 0:E3], k.m8[:], K3, k.gm[:], k.q8[0][:], k.q8[1][:], k.q8[2][:], k.r1[:],
                      k.const[:, C_R8:C_R8 + T * 8])
            mask, c = k.gm[:], k.c8[:]
        v.tensor_tensor(c, mask, sg, ALU.mult)
        if l != 1:
            v.drain()
            v.reduce_sum(k.r1[:], c, axis=AX.X)
            v.drain()
            v.tensor_scalar(k.r1[:], k.r1[:], 1e-6 if l == 0 else 1e-20, None, ALU.add)
            v.drain()
            v.reciprocal(k.r2[:], k.r1[:])
            v.drain()
            v.tensor_tensor(c, c, each(k.r2[:]), ALU.mult)
        v.drain().then_inc(self.ready, 1)
        self.fill(part, l, 3)

    def vector_weights(self, v, it, l):
        k = self.k
        v.wait_ge(self.wT_hi, it * 2 + l + 1)
        v.tensor_tensor(k.wTl, k.ps[4][0:E1, :], k.wTh.bitcast(F32), ALU.subtract).then_inc(self.wT_lo, 1)


def later_layers(nc, k, d):
    names = ("kv_free", "mix_loaded", "mix_free", "q", "q_hi", "q3", "scores", "centred", "exp", "turned", "taken",
             "pv", "pv_read", "o_ready", "oT", "o_hi", "o_lo", "out", "l2", "xT", "x_hi", "x_lo", "done", "stored")
    s = Names(**{n: k.sem("m_" + n) for n in names})
    k_loaded = [k.sem(f"m_k_loaded{i}") for i in range(2)]
    norm = Norm(k, "m_norm")
    gate = Gate(k, norm)
    line = Line(k)
    NA, NB = 2 * NB1, len(B3)
    tile = [slice(j * P, (j + 1) * P) for j in range(T)]
    by_tile = lambda ps: ps.rearrange("p (t d) -> p t d", d=P)
    row = lambda r: r.unsqueeze(1).to_broadcast([P, T, P])
    first_block = lambda it: 0 if isinstance(it, int) and it == 0 else it * (NA + NB) - NB
    GROUPS = T * 4
    S = (k.ps[2], k.ps[3])
    KD = HD + 1

    def turns(eng, turn):
        turn(0, True, False)
        with eng.Fori(1, CHUNKS) as it:
            turn(it, True, True)
        turn(CHUNKS, False, True)

    with nc.Block() as block:
        @block.sync
        def _(sp):
            def mix(it, part):
                sp.wait_ge(s.mix_free, it * 2 + part + 1)
                for t in range(T):
                    sp.dma_start(k.mixr[:, t, :], d.mix[it * T + t, part * P:(part + 1) * P].partition_broadcast(P))\
                        .then_inc(s.mix_loaded, 16)

            def turn(it, a, b):
                if a:
                    for j in range(T):
                        sp.wait_ge(s.kv_free, it * T + j + 1)
                        sp.dma_start(k.k3m[j % 2][:].bitcast(F32), d.keys1[it * T + j, :, :]).then_inc(k_loaded[j % 2], 16)
                        sp.dma_start(k.v9[j % 2][:].rearrange("p h d -> p (h d)"), d.values1[it * T + j, :, :])\
                            .then_inc(k_loaded[j % 2], 16)
                        if j == 1:
                            mix(it, 0)
                    mix(it, 1)
                if b:
                    sp.wait_ge(s.done, it)
                    before = bass.ds((it - 1) * T, T)
                    sp.dma_start(d.out[before, :, :].rearrange("t p d -> p t d"), k.x[:, before, :]).then_inc(s.stored, 16)

            turns(sp, turn)
            sp.wait_ge(s.stored, 16 * CHUNKS)

        @block.gpsimd
        def _(g):
            def turn(it, a, b):
                part = PoolPart(line, g, first_block(it), it, a, b)
                if not a:
                    for _ in B3:
                        part.block()
                    part.flush()
                    return
                norm.pool(g, it * 6)
                part.fill("norm0")
                part.fill("turned0")
                for u in range(STEPS):
                    if b and f"step{u}" in FILLERS:
                        part.block()
                part.fill("heads")
                part.fill("out")
                norm.pool(g, it * 6 + 1)
                for l in range(2):
                    gate.pool(part, l)
                    for _ in range(NB1):
                        part.block()
                    part.fill(f"sum{l + 1}")
                    if not b:
                        part.flush()
                    norm.pool(g, it * 6 + 2 * l + 2)
                    if l == 0:
                        norm.pool(g, it * 6 + 3)
                part.fill("norm4")
                part.flush()
                norm.pool(g, it * 6 + 5)

            turns(g, turn)

        @block.vector
        def _(v):
            def add(x, ps, col):
                v.scalar_tensor_tensor(x, by_tile(ps), k.tg[:, col:col + 1], x, ALU.mult, ALU.add)
                v.drain()

            def low(n):
                v.wait_ge(s.x_hi, n)
                v.tensor_tensor(k.xl[:], k.ps[4][:], k.xh[:].bitcast(F32), ALU.subtract).then_inc(s.x_lo, 1)

            def q3(it, j):
                v.wait_ge(s.q_hi, it * T + j + 1)
                v.scalar_tensor_tensor(k.q3[j % 2][:], k.qh[:].bitcast(F32), k.const[:, C_SPLIT:C_SPLIT + 1], k.ps[6][:],
                                       ALU.mult, ALU.add).then_inc(s.q3, 1)

            def evict(it, j):
                v.wait_ge(s.pv, it * T + j + 1)
                v.tensor_copy(k.pv[:].rearrange("p h d -> p (h d)"), k.ps[5][:, 0:HEADS * KD]).then_inc(s.pv_read, 1)
                v.drain()

            def normalize(j):
                v.tensor_tensor(k.good[:], k.pv[:, :, HD], k.pv[:, :, HD], ALU.is_equal)
                v.reciprocal(k.rec[:], k.pv[:, :, HD])
                v.drain()
                v.tensor_tensor(k.pv[:, :, 0:HD], k.pv[:, :, 0:HD], k.rec[:].unsqueeze(2).to_broadcast([P, HEADS, HD]), ALU.mult)
                v.drain()
                v.copy_predicated(k.o[:, j, :].rearrange("p (h d) -> p h d", d=HD),
                                  k.good[:].unsqueeze(2).to_broadcast([P, HEADS, HD]), k.pv[:, :, 0:HD])
                last = v.drain()
                if j == T - 1:
                    last.then_inc(s.o_ready, 1)

            def finish(it, part):
                part.flush()
                x = k.x[:, bass.ds((it - 1) * T, T), :]
                v.scalar_tensor_tensor(x, k.acc[:], k.tg[:, 7:8], x, ALU.mult, ALU.add)
                v.drain().then_inc(s.done, 1)

            def turn(it, a, b):
                part = VectorPart(line, v, first_block(it), it, a, b)
                if not a:
                    for _ in B3:
                        part.block()
                    finish(it, part)
                    return
                x = k.x[:, bass.ds(it * T, T), :]
                xs = [k.x[:, it * T + j, :] for j in range(T)]
                norm.vector(v, it * 6, xs)
                part.fill("norm0")
                low(it * 2 + 1)
                v.tensor_tensor(x, x, row(k.bo1[:]), ALU.add)
                v.memset(k.o[:], 0.0)
                part.fill("turned0")
                q3(it, 0)
                for u in range(STEPS):
                    if u < GROUPS:
                        heads = S[u % 2][:].rearrange("p (h t) -> p h t", t=P)
                        v.wait_ge(s.scores, it * GROUPS + u + 1)
                        v.reduce_max(k.mx4[:, u % 2, :], heads, axis=AX.X)
                        v.drain()
                        if u >= 2:
                            v.wait_ge(s.turned, it * GROUPS + u - 1)
                        v.tensor_tensor(k.e[u % 2][:].rearrange("p (h t) -> p h t", t=P), heads,
                                        k.mx4[:, u % 2, :].unsqueeze(2).to_broadcast([P, 4, P]), ALU.subtract)\
                            .then_inc(s.centred, 1)
                    if u % 4 == 1 and u < GROUPS - 4:
                        q3(it, u // 4 + 1)
                    if u % 4 == 1 and u >= 5:
                        evict(it, u // 4 - 1)
                    if u % 4 == 2 and u >= 6:
                        normalize(u // 4 - 1)
                    if f"step{u}" in FILLERS:
                        part.fill(f"step{u}")
                normalize(T - 1)
                part.fill("heads")
                v.wait_ge(s.o_hi, it + 1)
                v.tensor_tensor(k.xl[:], k.ps[4][:], k.xh[:].bitcast(F32), ALU.subtract).then_inc(s.o_lo, 1)
                part.fill("out")
                v.wait_ge(s.out, it + 1)
                add(x, k.ps[6][:], 1)
                for l in range(2):
                    norm.vector(v, it * 6 + 2 * l + 1, xs)
                    gate.vector(v, part, it, l)
                    gate.vector_weights(v, it, l)
                    for _ in range(NB1):
                        part.block()
                    part.fill(f"sum{l + 1}")
                    v.wait_ge(line.sum_a, it * 2 + l + 1)
                    add(x, k.ps[6][:], 5 + l)
                    norm.vector(v, it * 6 + 2 * l + 2, xs)
                    if l == 0:
                        low(it * 2 + 2)
                        v.wait_ge(s.mix_loaded, it * (32 * T) + 16 * T)
                        v.tensor_tensor(x, x, k.mixr[:], ALU.add)
                        v.drain().then_inc(s.mix_free, 1)
                        v.wait_ge(s.l2, it + 1)
                        add(x, k.ps[6][:], 2)
                part.fill("norm4")
                v.drain()
                v.wait_ge(s.mix_loaded, it * (32 * T) + 32 * T)
                v.scalar_tensor_tensor(k.xn[:], k.xn[:], 0.0, k.mixr[:], ALU.max, ALU.mult)
                v.drain().then_inc(s.mix_free, 1)
                v.tensor_tensor(x, x, k.xn[:], ALU.add)
                v.drain()
                norm.vector(v, it * 6 + 5, xs)
                if b:
                    finish(it, part)
                gate.vector(v, part, it, 2)

            v.sem_inc(s.kv_free, 2)
            v.sem_inc(s.mix_free, 1)
            line.credits(v)
            v.memset(k.g8[:], -3e38)
            v.drain()
            turns(v, turn)

        @block.scalar
        def _(act):
            def high(n):
                act.wait_ge(s.xT, n)
                act.activation(k.xh[:], k.ps[4][:], ACT.Copy).then_inc(s.x_hi, 1)

            def q_high(it, j):
                act.wait_ge(s.q, it * T + j + 1)
                act.activation(k.qh[:], k.ps[6][:], ACT.Copy).then_inc(s.q_hi, 1)

            def turn(it, a, b):
                part = ScalarPart(line, act, first_block(it), it, a, b)
                if not a:
                    for _ in B3:
                        part.block()
                    part.flush()
                    return
                part.fill("norm0")
                high(it * 2 + 1)
                part.fill("turned0")
                q_high(it, 0)
                for u in range(STEPS):
                    fills = b and f"step{u}" in FILLERS
                    if fills:
                        part.late(True)
                    if u < GROUPS:
                        act.wait_ge(s.centred, it * GROUPS + u + 1)
                        act.activation(k.e[u % 2][:], k.e[u % 2][:], ACT.Exp, scale=float(HD) ** -0.5).then_inc(s.exp, 1)
                    if u % 4 == 0 and u < GROUPS - 4:
                        q_high(it, u // 4 + 1)
                    if fills:
                        part.silu()
                    if 1 <= u <= GROUPS:
                        act.wait_ge(s.turned, it * GROUPS + u)
                        act.activation(k.pt[:], k.ps[4][:], ACT.Copy).then_inc(s.taken, 1)
                part.fill("heads")
                act.wait_ge(s.oT, it + 1)
                act.activation(k.xh[:], k.ps[4][:], ACT.Copy).then_inc(s.o_hi, 1)
                part.fill("out")
                for l in range(2):
                    gate.scalar(act, part, it, l)
                    gate.scalar_weights(act, it, l)
                    for _ in range(NB1):
                        part.block()
                    part.fill(f"sum{l + 1}")
                    if not b:
                        part.flush()
                    if l == 0:
                        high(it * 2 + 2)
                part.fill("norm4")
                part.flush()
                gate.scalar(act, part, it, 2)

            turns(act, turn)

        @block.tensor
        def _(pe):
            def x_turned(norm_at):
                pe.wait_ge(norm.ready, norm_at + 1)
                for j in range(T):
                    last = pe.transpose(k.ps[4][:, tile[j]], k.xn[:, j, :], k.ident)
                last.then_inc(s.xT, 1)

            def queries(it, j):
                for q in range(4):
                    c = slice(q * P, (q + 1) * P)
                    three_pass(pe, k.ps[6][:, c], k.wa1h[:, c], k.wa1l[:, c], k.xh[:, tile[j]], k.xl[:, tile[j]], stop=False)
                    pe.matmul(k.ps[6][:, c], k.bqh[:, c], k.one_r[32:33, :], start=False, stop=False)
                    last = pe.matmul(k.ps[6][:, c], k.bql[:, c], k.one_r[32:33, :], start=False, stop=True)
                last.then_inc(s.q, 1)

            def scores(it, u):
                j, g = divmod(u, 4)
                if g == 0:
                    pe.wait_ge(s.q3, it * T + j + 1)
                    pe.wait_ge(k_loaded[j % 2], it * 64 + (j // 2 * 32 + 32))
                if u >= 2:
                    pe.wait_ge(s.centred, it * GROUPS + u - 1)
                r = slice(32 * g, 32 * g + 3 * HD)
                for q in range(4):
                    last = pe.matmul(S[u % 2][:, tile[q]], k.q3[j % 2][r, tile[q]], k.k3m[j % 2][r, tile[q]],
                                     start=True, stop=True)
                last.then_inc(s.scores, 1)

            def turned(it, u):
                pe.wait_ge(s.exp, it * GROUPS + u + 1)
                for q in range(4):
                    last = pe.transpose(k.ps[4][:, tile[q]], k.e[u % 2][:, tile[q]], k.ident)
                last.then_inc(s.turned, 1)

            def values(it, u):
                j, g = divmod(u, 4)
                pe.wait_ge(s.taken, it * GROUPS + u + 1)
                if g == 0 and j:
                    pe.wait_ge(s.pv_read, it * T + j)
                for q in range(4):
                    h = 4 * q + g
                    c = h * KD
                    last = pe.matmul(k.ps[5][:, c:c + KD], k.pt[:, tile[q]], k.v9[j % 2][:, h, :], start=True, stop=True)
                if g == 3:
                    last.then_inc(s.pv, 1)
                    pe.drain().then_inc(s.kv_free, 1)

            def turn(it, a, b):
                part = TensorPart(line, pe, first_block(it), it, a, b)
                if not a:
                    for _ in B3:
                        part.block()
                    part.flush()
                    return
                part.fill("norm0")
                x_turned(it * 6)
                part.fill("turned0")
                pe.wait_ge(s.x_lo, it * 2 + 1)
                queries(it, 0)
                for u in range(STEPS):
                    fills = b and f"step{u}" in FILLERS
                    if u < GROUPS:
                        scores(it, u)
                    if u % 4 == 0 and u < GROUPS - 4:
                        queries(it, u // 4 + 1)
                    if u >= 2:
                        values(it, u - 2)
                    if fills:
                        part.up()
                    if 1 <= u <= GROUPS:
                        turned(it, u - 1)
                    if fills:
                        part.late()
                part.fill("heads")
                pe.wait_ge(s.o_ready, it + 1)
                for j in range(T):
                    last = pe.transpose(k.ps[4][:, tile[j]], k.o[:, j, :], k.ident)
                last.then_inc(s.oT, 1)
                part.fill("out")
                pe.wait_ge(s.o_lo, it + 1)
                for j in range(T):
                    last = three_pass(pe, k.ps[6][:, tile[j]], k.xh[:, tile[j]], k.xl[:, tile[j]],
                                      k.wa1h[:, 4 * P:5 * P], k.wa1l[:, 4 * P:5 * P])
                last.then_inc(s.out, 1)
                for l in range(2):
                    gate.tensor(pe, part, it, l, it * 6 + 2 * l + 1)
                    for n in range(NB1):
                        part.up()
                        if n == 0:
                            gate.tensor_weights(pe, it, l)
                        part.weights()
                        part.late()
                    part.fill(f"sum{l + 1}")
                    if not b:
                        part.flush()
                    if l == 0:
                        x_turned(it * 6 + 2)
                        pe.wait_ge(s.x_lo, it * 2 + 2)
                        for j in range(T):
                            last = three_pass(pe, k.ps[6][:, tile[j]], k.xh[:, tile[j]], k.xl[:, tile[j]],
                                              k.l2wh[:], k.l2wl[:])
                        last.then_inc(s.l2, 1)
                part.fill("norm4")
                part.flush()
                gate.tensor(pe, part, it, 2, it * 6 + 5)

            turns(pe, turn)


def program(nc, d, stop=9):
    k = Names()
    with ExitStack() as ctx:
        def sb(name, shape, dt=F32, c=ctx):
            return c.enter_context(nc.sbuf_tensor(name, shape, dt))

        k.sem = lambda name: nc.alloc_semaphore(name=name)
        k.ps = [ctx.enter_context(nc.psum_tensor(f"ps{i}", [P, 512], F32)) for i in range(8)]
        k.gu = [(k.ps[0], k.ps[1]), (k.ps[2], k.ps[3])]
        k.x = sb("x", [P, SEQS, P])
        k.const = sb("const", [P, C_ALL])
        k.ident = k.const[:, C_ID:C_ID + P]
        k.bo1 = sb("bo1", [P, P])
        k.tg = sb("tg", [P, 8])
        k.eps4, k.mhalf = sb("eps4", [P, T]), sb("mhalf", [P, T])
        k.st6, k.mv = sb("st6", [P, T, 6]), sb("mv", [P, T, 2])
        k.ve, k.rs = sb("ve", [P, T]), sb("rs", [P, T])
        k.xn = sb("xn", [P, T, P])
        k.xh, k.xl = sb("xh", [P, CW], F32R), sb("xl", [P, CW], F32R)
        k.xbh, k.xbl = sb("xbh", [P, CW], F32R), sb("xbl", [P, CW], F32R)
        k.h, k.s = ([sb(f"{n}{i}", [P, CW]) for i in range(2)] for n in ("h", "s"))
        k.hh = [sb(f"hh{i}", [P, CW], F32R) for i in range(3)]
        k.hl = [sb(f"hl{i}", [P, CW], F32R) for i in range(3)]
        k.l2wh, k.l2wl = sb("l2wh", [P, P], F32R), sb("l2wl", [P, P], F32R)
        k.w1h, k.w1l, k.w2h, k.w2l = (sb(n, [P, NB1 * W1C], F32R) for n in ("w1h", "w1l", "w2h", "w2l"))
        k.index, k.gate = sb("index", [P, K0 * SEQS], I32), sb("gate", [P, K0, SEQS])
        k.one_r = sb("one_r", [33, P], F32R)
        unused = nc.snapshot_sems()
        with ExitStack() as l0:
            k.rows = sb("rows", [P, B_ALL], c=l0)
            k.const0 = sb("const0", [P, L_ALL], c=l0)
            k.raw = [sb(f"raw{i}", [P, W3C], c=l0) for i in range(2)]
            k.xn_all = sb("xn_all", [P, SEQS, P], c=l0)
            k.sc = sb("sc", [P, SEQS, 40], c=l0)
            k.ub = sb("ub", [P, 2 * P], BF16, l0)
            with ExitStack() as a0:
                k.junk = sb("junk", [P, CW], c=a0)
                k.sh0h, k.sh0l = sb("sh0h", [P, W0C], F32R, a0), sb("sh0l", [P, W0C], F32R, a0)
                k.g0h, k.g0l = sb("g0h", [P, 40], F32R, a0), sb("g0l", [P, 40], F32R, a0)
                k.wa0, k.bcol = sb("wa0", [P, 4 * P], c=a0), sb("bcol", [P, 2], c=a0)
                with ExitStack() as su:
                    k.cent, k.cs = sb("cent", [40, P], c=su), sb("cs", [40, 3], c=su)
                    k.w2t, k.ctxT = sb("w2t", [P, P], c=su), sb("ctxT", [P, SEQS * P], c=su)
                    k.csum, k.rsum = sb("csum", [P, SEQS], c=su), sb("rsum", [P, SEQS], c=su)
                    k.zero, k.mix = sb("zero", [P, SLOTS // 8], c=su), sb("mix", [SEQS, 2 * P], c=su)
                    setup(nc, k, d)
                k.ctxr = sb("ctxr", [P, CW], c=a0)
                k.xT, k.qT, k.kT, k.pT, k.oT = (sb(n, [P, CW], c=a0) for n in ("xT", "qT", "kT", "pT", "oT"))
                k.v0, k.pr = sb("v0", [P, T, P], c=a0), sb("pr", [P, T, P], c=a0)
                k.mx = sb("mx", [P, 3 * T], c=a0)
                k.ss, k.ss2, k.rn = (sb(n, [P, T], c=a0) for n in ("ss", "ss2", "rn"))
                layer0_attention(nc, k, d)
            nc.clear_and_free_semaphores(nc.allocated_since(unused))
            nc.all_engine_barrier()
            layer0_experts_all(nc, k, d, sb)
        k.w3h, k.w3l = sb("w3h", [P, (E3 + 1) * W3C], F32R), sb("w3l", [P, (E3 + 1) * W3C], F32R)
        k.wa1h, k.wa1l = sb("wa1h", [P, 5 * P], F32R), sb("wa1l", [P, 5 * P], F32R)
        k.gth, k.gtl = sb("gth", [P, 2 * E1 + E3], F32R), sb("gtl", [P, 2 * E1 + E3], F32R)
        k.selh = sb("selh", [33, (NB1 - 1) * P], F32R)
        k.bqh, k.bql = k.selh[32:33, 0:4 * P], k.selh[32:33, 4 * P:8 * P]
        with ExitStack() as comb:
            k.y = sb("y", [P, 16, P], c=comb)
            k.raw = [sb(f"raw_w3_{i}", [P, W3C], c=comb) for i in range(2)]
            layer0_combine(nc, k, d)
        if stop == 2:
            stored = k.sem("stored")
            with nc.Block() as block:
                @block.sync
                def _(sp):
                    sp.dma_start(d.out.rearrange("t p d -> p t d"), k.x[:]).then_inc(stored, 16)
                    sp.wait_ge(stored, 16)
            return
        k.q3, k.k3m = ([sb(f"{n}{i}", [P, 4 * P], F32R) for i in range(2)] for n in ("q3", "k3m"))
        k.v9 = [sb(f"v9{i}", [P, HEADS, HD + 1]) for i in range(2)]
        k.qh, k.oh, k.ol = k.hh[0], k.hh[1], k.hh[2]
        k.acc = sb("acc", [P, T, P])
        k.e = [sb(f"e{i}", [P, 4 * P]) for i in range(2)]
        k.pt, k.qh = sb("pt", [P, 4 * P]), sb("qh", [P, 4 * P], F32R)
        k.o = k.xn
        k.mixr = sb("mixr", [P, T, P])
        k.mx4, k.rec = sb("mx4", [P, 2, 4]), sb("recd", [P, HEADS])
        k.good, k.pv = sb("good", [P, HEADS], I32), sb("pv", [P, HEADS, HD + 1])
        k.sg, k.ms, k.mask, k.c16 = (sb(n, [P, T, E1]) for n in ("sg", "ms", "mask", "c16"))
        k.pairs = sb("pairs", [P, T * 4, 6])
        k.g8, k.m8, k.gm, k.c8 = (sb(n, [P, T, 8]) for n in ("g8", "m8", "gm", "c8"))
        k.q8 = [sb(f"q8_{i}", [P, T, 8]) for i in range(3)]
        k.q16 = [sb(f"q16_{i}", [P, T, E1]) for i in range(3)]
        k.r1, k.r2 = sb("r1", [P, T]), sb("r2", [P, T])
        k.wTh, k.wTl = k.q3[0][0:E1, :], k.q3[1][0:E1, :]
        later_layers(nc, k, d)


def laid_out(i):
    t = lambda a: np.ascontiguousarray(np.swapaxes(a, -1, -2))
    cat = lambda *a: np.ascontiguousarray(np.concatenate(a, axis=-1))
    z = lambda *s: np.zeros(s, np.float32)
    o = {"x": i["x"], "const": constants(), "const0": constants_layer0()}
    o["ctxT"] = t(i["ctx_1024"].reshape(SEQS * P, P))
    o["rows"] = cat(i["L0_xattn_bv"], i["L0_xattn_bo"], i["L0_ffn_bias"], i["L1_xattn_bv"], i["L1_xattn_bo"],
                    i["L2_xattn_b"], i["g_xattn"], i["g_ffn"])[None]
    o["wa0"] = cat(i["L0_xattn_Wq"], i["L0_xattn_Wk"], i["L0_xattn_Wv"], i["L0_xattn_Wo"])
    o["cent"] = np.concatenate([i["L0_ffn_group_centroids"], i["L0_ffn_expert_centroids"]])
    halves = lambda w: cat(w[..., 0:P, :], w[..., P:2 * P, :])
    o["w0"] = np.concatenate([cat(i["L0_ffn_wg"], i["L0_ffn_wu"], halves(i["L0_ffn_wd"])),
                              cat(i["L0_ffn_sg"], i["L0_ffn_su"], halves(i["L0_ffn_sd"]))[None]])
    pair = lambda w: np.concatenate([w[0::2], w[1::2]], axis=2)
    down = lambda w: np.concatenate([w[0::2], w[1::2]], axis=1)
    pack = lambda g, u, dn: np.ascontiguousarray(np.concatenate(list(cat(g, u, dn)), axis=1))
    o["w1"] = pack(np.concatenate([pair(t(i["L1_ffn_w1_e"])), t(i["L1_ffn_w1_s"])[None]]),
                   np.concatenate([pair(t(i["L1_ffn_w3_e"])), t(i["L1_ffn_w3_s"])[None]]),
                   np.concatenate([down(t(i["L1_ffn_w2_e"])), t(i["L1_ffn_w2_s"])[None]]))
    o["w2"] = pack(np.concatenate([pair(i["L2_ffn_w1"]), i["L2_ffn_ws1"][None]]),
                   np.concatenate([pair(i["L2_ffn_w3"]), i["L2_ffn_ws3"][None]]),
                   np.concatenate([down(i["L2_ffn_w2"]), i["L2_ffn_ws2"][None]]))
    o["l2w"] = cat(t(i["L2_xattn_W"][:, 0:P]), t(i["L2_xattn_W"][:, P:2 * P]))
    gate = np.concatenate([i["L3_ffn_shared_gate"][None], i["L3_ffn_expert_gate"]])
    up = np.concatenate([i["L3_ffn_shared_up"][None], i["L3_ffn_expert_up"]])
    dn = t(np.concatenate([i["L3_ffn_shared_down"][None], i["L3_ffn_expert_down"]]))
    dn = np.concatenate([dn, z(E3 + 1, 3 * P - FF3, P)], axis=1).reshape(E3 + 1, 3, P, P)
    o["w3"] = cat(t(gate), t(up), np.swapaxes(dn, 1, 2).reshape(E3 + 1, P, 3 * P))
    def quads(w):
        a = w.reshape(*w.shape[:-1], HEADS, 1, HD)
        a = np.concatenate([a, a, a, np.zeros_like(a)], axis=-2)
        return a.reshape(*w.shape[:-1], 4 * P)
    o["wa1"] = cat(quads(t(i["L1_xattn_Wq"])), quads(t(i["L1_xattn_Wk"])), t(i["L1_xattn_Wv"]), t(i["L1_xattn_Wo"]))
    o["brow"] = cat(quads(i["L1_xattn_bq"]), quads(i["L1_xattn_bk"]))[None]
    o["bcol"] = np.stack([i["L0_xattn_bq"], i["L0_xattn_bk"]], 1)
    o["gates"] = cat(t(i["L1_ffn_w_gate"]), t(i["L2_ffn_gate_w"]), t(i["L3_ffn_gate_w"]))
    o["sel"] = selectors()
    return {n: np.ascontiguousarray(a) for n, a in o.items()}


STOP = 9


def kernel(**inputs):
    import concourse.bacc as bacc
    from concourse.bass_utils import run_bass_kernel_spmd as run

    nc = bacc.Bacc("TRN2", target_bir_lowering=False, num_devices=1)
    arrays = laid_out({n: np.asarray(a) for n, a in inputs.items()})
    d = Names()
    for name, a in arrays.items():
        d[name] = nc.dram_tensor("in_" + name, a.shape, mybir.dt.from_np(a.dtype), kind="ExternalInput").ap()
    d.out = nc.dram_tensor("out_0", (SEQS, P, P), F32, kind="ExternalOutput").ap()
    d.buf = nc.dram_tensor("slot_in", (SLOTS + K0 * SEQS * P, P), F32, kind="Internal").ap()
    d.oute = nc.dram_tensor("slot_out", (SLOTS + P, P), F32, kind="Internal").ap()
    d.mix = nc.dram_tensor("seq_rows", (SEQS, 2 * P), F32, kind="Internal").ap()
    d.keys1 = nc.dram_tensor("l1_keys", (SEQS, P, 4 * P), F32, kind="Internal").ap()
    d.values1 = nc.dram_tensor("l1_values", (SEQS, P, HEADS * (HD + 1)), F32, kind="Internal").ap()
    program(nc, d, STOP)
    r = run(nc, [{"in_" + n: a for n, a in arrays.items()}], core_ids=[0])
    return r.results[0]["out_0"]
```

```python
from contextlib import ExitStack

import numpy as np
import concourse.bass as bass
from concourse import mybir

F32 = mybir.dt.float32
F32R = mybir.dt.float32r
BF16 = mybir.dt.bfloat16
I32 = mybir.dt.int32
U32 = mybir.dt.uint32
ALU = mybir.AluOpType
ACT = mybir.ActivationFunctionType
AX = mybir.AxisListType


class Names(dict):

    def __getattr__(self, name):
        return self[name]

    def __setattr__(self, name, value):
        self[name] = value


P = 128
SEQS = 16
T = 4
CHUNKS = SEQS // T
CW = T * P
EPS = 1e-5

E0, G0, K0, HID0 = 32, 8, 4, 256
CAP = int(SEQS * P / E0 * K0 * 1.25)
ROWS = (112, 112, 96)
RT = 112
SLOTS = E0 * CAP
W0C = 3 * HID0
E1, G1, K1 = 16, 4, 4
NB1 = E1 // 2 + 1
W1C = 3 * P
PIECES = 3 + 2 * CHUNKS
E3, K3 = 8, 2
FF3 = 352
M3 = (128, 128, 96)
W3C = 2 * FF3 + 3 * P
HEADS, HD = 16, 8

C_ID = 0
C_SPLIT = 128
C_R8 = 130
C_R16 = C_R8 + T * 8
C_ALL = C_R16 + T * E1
L_U, L_ONE = 0, 128
L_TRASH = 256
L_START = 257
L_R8 = L_START + E0
L_R32 = L_R8 + SEQS * 8
L_R16T = L_R32 + SEQS * E0
L_SPREAD = L_R16T + SEQS * E0
L_ALL = L_SPREAD + K0 * SEQS
B_BV0, B_BO0, B_BIAS0, B_BV1, B_BO1, B_B2, B_G = 0, 128, 256, 288, 416, 544, 672
B_ALL = 680


def constants():
    c = np.zeros((P, C_ALL), np.float32)
    c[:, C_ID:C_ID + P] = np.eye(P)
    part = (np.arange(P) % 32) // HD
    c[:, C_SPLIT] = -1.0 * (part == 1)
    c[:, C_SPLIT + 1] = -1.0 * (part == 2)
    c[:, C_R8:C_R8 + T * 8] = np.arange(T * 8) % 8 > 0
    c[:, C_R16:C_R16 + T * E1] = np.arange(T * E1) % E1 > 0
    return c


def constants_layer0():
    c = np.zeros((P, L_ALL), np.float32)
    c[:, L_U:L_U + P] = np.triu(np.ones((P, P)), 1)
    c[:, L_ONE:L_ONE + P] = 1
    c[:, L_TRASH] = SLOTS + np.arange(P)
    c[:, L_START:L_START + E0] = np.arange(E0) * CAP
    c[:, L_R8:L_R8 + SEQS * 8] = np.arange(SEQS * 8) % 8 > 0
    c[:, L_R32:L_R32 + SEQS * E0] = np.arange(SEQS * E0) % E0 > 0
    c[:, L_R16T:L_R16T + SEQS * E0] = np.arange(SEQS * E0) % SEQS > 0
    c[:, L_SPREAD:L_SPREAD + K0 * SEQS] = np.arange(K0 * SEQS) * P
    return c


def selectors():
    s = np.zeros((E1, (NB1 - 1) * P), np.float32)
    for b in range(NB1 - 1):
        for p in range(P):
            s[2 * b + p // 64, b * P + p] = 1
    return s


def topk_mask(v, s, m8, k, mask, gt, eq, pre, count, reset):
    tiles, n = s.shape[1], s.shape[2]
    full = [P, tiles, n]
    for t in range(tiles):
        v.max(m8[:, t, :], s[:, t, :])
    v.drain()
    tau = m8[:, :, k - 1:k].to_broadcast(full)
    v.tensor_tensor(gt, s, tau, ALU.is_gt)
    v.tensor_tensor(eq, s, tau, ALU.is_equal)
    v.drain()
    v.reduce_sum(count, gt, axis=AX.X)
    v.tensor_tensor_scan(pre.rearrange("p t n -> p (t n)"), reset, eq.rearrange("p t n -> p (t n)"), 0.0,
                         ALU.mult, ALU.add)
    v.drain()
    v.tensor_tensor(pre, pre, count.unsqueeze(2).to_broadcast(full), ALU.add)
    v.drain()
    v.scalar_tensor_tensor(eq, pre, float(k) + 0.5, eq, ALU.is_lt, ALU.mult)
    v.drain()
    v.tensor_tensor(mask, gt, eq, ALU.add)
    v.drain()


def three_pass(pe, out, lh, ll, rh, rl, start=True, stop=True, skip=False):
    pe.matmul(out, lh, rl, start=start, stop=False, skip_group_check=skip)
    pe.matmul(out, ll, rh, start=False, stop=False, skip_group_check=skip)
    return pe.matmul(out, lh, rh, start=False, stop=stop, skip_group_check=skip)


def half_silu(v, out, tanh, gate, up):
    v.scalar_tensor_tensor(out, tanh, 1.0, up, ALU.add, ALU.mult)
    v.drain()
    return v.scalar_tensor_tensor(out, out, 0.5, gate, ALU.mult, ALU.mult)


class Norm:

    def __init__(self, k, name, xn):
        self.k, self.xn = k, xn
        self.stats = k.sem(name + "_stats")
        self.eps = k.sem(name + "_eps")
        self.rstd = k.sem(name + "_rstd")
        self.ready = k.sem(name + "_ready")

    def vector(self, v, n, x, meanwhile=None):
        k = self.k
        for j in range(T):
            v.bn_stats(k.st6[:, j, :], x[j])
        v.drain()
        for j in range(T):
            last = v.bn_aggr(k.mv[:, j, :], k.st6[:, j, :])
        last.then_inc(self.stats, 1)
        if meanwhile:
            meanwhile()
        v.wait_ge(self.rstd, n + 1)
        for j in range(T):
            last = v.tensor_scalar(self.xn[:, j, :], x[j], k.mv[:, j, 0:1], k.rs[:, j:j + 1],
                                   ALU.subtract, ALU.mult)
        last.then_inc(self.ready, 1)

    def pool(self, g, n):
        k = self.k
        g.wait_ge(self.stats, n + 1)
        g.tensor_tensor(k.ve[:], k.mv[:, :, 1], k.eps4[:], ALU.add).then_inc(self.eps, 1)
        g.wait_ge(self.eps, n + 1)
        g.tensor_tensor(k.rs[:], k.ve[:], k.mhalf[:], ALU.pow).then_inc(self.rstd, 1)


class Blocks:

    def __init__(self, k, name, gu, s, h, hh, hl, tanh=False):
        self.gu, self.s, self.h, self.hh, self.hl, self.tanh = gu, s, h, hh, hl, tanh
        self.gu_ready = k.sem(name + "_gu_ready")
        self.gu_free = k.sem(name + "_gu_free")
        self.silu = k.sem(name + "_silu")
        self.h_ready = k.sem(name + "_h_ready")
        self.hi = k.sem(name + "_hi")
        self.lo = k.sem(name + "_lo")
        self.h_free = k.sem(name + "_h_free")

    def credits(self, v):
        v.sem_inc(self.gu_free, len(self.gu))
        v.sem_inc(self.h_free, len(self.h))

    def tensor_gu(self, pe, a, g, wh, wl, g0, u0, m, xh, xl, back=2):
        w = xh.shape[1]
        pe.wait_ge(self.gu_free, a + 1 + len(self.gu) - back)
        for c0, bank in ((g0, 0), (u0, 1)):
            last = three_pass(pe, self.gu[g][bank][0:m, 0:w], wh[:, c0:c0 + m], wl[:, c0:c0 + m], xh, xl)
        last.then_inc(self.gu_ready, 1)

    def scalar_silu(self, act, a, g, m, w):
        act.wait_ge(self.gu_ready, a + 1)
        if self.tanh:
            act.activation(self.s[g][0:m, 0:w], self.gu[g][0][0:m, 0:w], ACT.Tanh, scale=0.5).then_inc(self.silu, 1)
        else:
            act.activation(self.s[g][0:m, 0:w], self.gu[g][0][0:m, 0:w], ACT.Silu).then_inc(self.silu, 1)

    def vector_h(self, v, a, g, h, m, w, back):
        v.wait_ge(self.h_free, a + 1 + len(self.h) - back)
        v.wait_ge(self.silu, a + 1)
        hid = self.h[h][0:m, 0:w]
        if self.tanh:
            half_silu(v, hid, self.s[g][0:m, 0:w], self.gu[g][0][0:m, 0:w], self.gu[g][1][0:m, 0:w]).then_inc(self.gu_free, 1)
        else:
            v.tensor_tensor(hid, self.s[g][0:m, 0:w], self.gu[g][1][0:m, 0:w], ALU.mult).then_inc(self.gu_free, 1)
        v.drain().then_inc(self.h_ready, 1)

    def scalar_hi(self, act, a, h, m, w):
        act.wait_ge(self.h_ready, a + 1)
        act.activation(self.hh[h][0:m, 0:w], self.h[h][0:m, 0:w], ACT.Copy).then_inc(self.hi, 1)

    def pool_lo(self, g, a, h, m, w):
        g.wait_ge(self.hi, a + 1)
        g.tensor_tensor(self.hl[h][0:m, 0:w], self.h[h][0:m, 0:w], self.hh[h][0:m, 0:w].bitcast(F32),
                        ALU.subtract).then_inc(self.lo, 1)

    def tensor_down(self, pe, a, h, m, tiles, out, w, wl, first, skip):
        pe.wait_ge(self.lo, a + 1)
        for j, (c0, c1) in enumerate(tiles):
            last = three_pass(pe, out(j), self.hh[h][0:m, c0:c1], self.hl[h][0:m, c0:c1], w, wl,
                              start=first and (j == 0 or not skip), stop=True, skip=skip)
        last.then_inc(self.h_free, 1)


def load_and_split(nc, k, name, jobs):
    slots = len(k.raw)
    loaded, hi, lo = [k.sem(f"{name}_loaded{i}") for i in range(slots)], k.sem(name + "_hi"), k.sem(name + "_lo")

    raw = lambda i: k.raw[i % slots][0:jobs[i][0].shape[0], 0:jobs[i][0].shape[1]]


    def sync(sp, first=0, end=len(jobs)):
        for i in range(first, end):
            if i >= slots:
                sp.wait_ge(hi, i - slots + 1)
                sp.wait_ge(lo, i - slots + 1)
            sp.dma_start(raw(i), jobs[i][0]).then_inc(loaded[i % slots], 16)

    def scalar(act, first=0, end=len(jobs)):
        for i in range(first, end):
            act.wait_ge(loaded[i % slots], 16 * (i // slots + 1))
            act.activation(jobs[i][1], raw(i), ACT.Copy).then_inc(hi, 1)

    def vector(v, first=0, end=len(jobs)):
        for i in range(first, end):
            _, high, low = jobs[i]
            v.wait_ge(hi, i + 1)
            if low is None:
                v.drain().then_inc(lo, 1)
            else:
                v.tensor_tensor(low, raw(i), high.bitcast(F32), ALU.subtract).then_inc(lo, 1)

    return sync, scalar, vector


def setup(nc, k, d):
    s = Names(**{n: k.sem("setup_" + n) for n in (
        "loaded", "zero", "tanh", "square", "norm", "cent", "centT", "gh", "stored")})
    sync_w, scalar_w, vector_w = load_and_split(nc, k, "setup_w", [
        (d.w0[E0], k.sh0h[:], k.sh0l[:]), (d.l2w[:, 0:P], k.l2wh[:], k.l2wl[:])])
    loads = 8
    with nc.Block() as block:
        @block.sync
        def _(sp):
            sp.dma_start(k.x[:], d.x.rearrange("t p d -> p t d")).then_inc(s.loaded, 16)
            sp.dma_start(k.const[:], d.const[:, :]).then_inc(s.loaded, 16)
            sp.dma_start(k.const0[:], d.const0[:, :]).then_inc(s.loaded, 16)
            sp.dma_start(k.rows[:], d.rows[0, :].partition_broadcast(P)).then_inc(s.loaded, 16)
            sp.dma_start(k.wa0[:], d.wa0[:, :]).then_inc(s.loaded, 16)
            sp.dma_start(k.bcol[:], d.bcol[:, :]).then_inc(s.loaded, 16)
            sp.dma_start(k.bq[:], d.bq[:, :]).then_inc(s.loaded, 16)
            sp.dma_start(k.cent[:], d.cent[:, :]).then_inc(s.loaded, 16)
            sync_w(sp)
            sp.wait_ge(s.zero, 1)
            sp.dma_start(d.oute[SLOTS:SLOTS + P, :], k.zero[:, 0:P]).then_inc(s.stored, 16)
            sp.wait_ge(s.stored, 16)

        @block.gpsimd
        def _(g):
            g.memset(k.eps4[:], EPS)
            g.memset(k.mhalf[:], -0.5)
            g.drain()
            g.wait_ge(s.square, 1)
            g.tensor_tensor(k.cs[:, 2:3], k.cs[:, 1:2], k.mhalf[0:40, 0:1], ALU.pow).then_inc(s.norm, 1)

        @block.scalar
        def _(act):
            act.wait_ge(s.loaded, 16 * loads)
            act.activation(k.tg[:], k.rows[:, B_G:B_G + 8], ACT.Tanh).then_inc(s.tanh, 1)
            scalar_w(act)
            act.wait_ge(s.centT, 1)
            act.activation(k.g0h[:], k.ps[7][:, 0:40], ACT.Copy).then_inc(s.gh, 1)

        @block.vector
        def _(v):
            v.memset(k.zero[:], 0.0).then_inc(s.zero, 1)
            v.wait_ge(s.loaded, 16 * loads)
            v.wait_ge(s.tanh, 1)
            for out, b, g in ((k.rows[:, B_BO0:B_BO0 + P], B_BO0, 0), (k.bo1[:], B_BO1, 1)):
                v.tensor_scalar(out, k.rows[:, b:b + P], k.tg[:, g:g + 1], None, ALU.mult)
            v.tensor_copy(k.ub[:], k.const0[:, L_U:L_U + 2 * P])
            v.tensor_tensor(k.junk[0:40, 0:P], k.cent[:], k.cent[:], ALU.mult)
            v.drain()
            v.reduce_sum(k.cs[:, 0:1], k.junk[0:40, 0:P], axis=AX.X)
            v.drain()
            v.tensor_scalar(k.cs[:, 1:2], k.cs[:, 0:1], 1e-24, None, ALU.max).then_inc(s.square, 1)
            v.wait_ge(s.norm, 1)
            v.tensor_scalar(k.cent[:], k.cent[:], k.cs[:, 2:3], None, ALU.mult).then_inc(s.cent, 1)
            vector_w(v)
            v.wait_ge(s.gh, 1)
            v.tensor_tensor(k.g0l[:], k.ps[7][:, 0:40], k.g0h[:].bitcast(F32), ALU.subtract)

        @block.tensor
        def _(pe):
            pe.wait_ge(s.loaded, 16 * loads)
            pe.wait_ge(s.cent, 1)
            pe.transpose(k.ps[7][:, 0:40], k.cent[:], k.ident[0:40, 0:40]).then_inc(s.centT, 1)


def layer0_attention(nc, k, d):
    s = Names(**{n: k.sem("a0_" + n) for n in (
        "ctx_loaded", "ctx_free", "xT", "xTs", "qkv", "qk_read", "v_read", "scores", "centred", "exp", "probs",
        "pT", "pTs", "o", "os", "out", "fT", "hi", "lo", "square", "norm_max", "norm_inv", "logits",
        "copied", "zeroed")})
    norm_x, norm_y = Norm(k, "a0_norm_x", k.xn), Norm(k, "a0_norm_y", k.xn2)
    blocks = Blocks(k, "a0_blk", k.gu[0:1], k.s[0:1], k.h[0:2], k.hh[0:2], k.hl[0:2], tanh=True)
    pT, pQ, pK, pV = k.ps[4], k.ps[5], k.ps[6], k.ps[7]
    pX, pSum = k.ps[2], k.ps[3]
    tile = [slice(j * P, (j + 1) * P) for j in range(T)]
    by_tile = lambda ps: ps[:].rearrange("p (t d) -> p t d", d=P)
    row = lambda b: k.rows[:, b:b + P].unsqueeze(1).to_broadcast([P, T, P])
    each = lambda col: col.unsqueeze(2).to_broadcast([P, T, P])

    def turns(eng, turn):
        turn(0, True, False)
        with eng.Fori(1, CHUNKS) as it:
            turn(it, True, True)
        turn(CHUNKS, False, True)

    with nc.Block() as block:
        @block.sync
        def _(sp):
            sp.wait_ge(s.ctx_free, 1)
            sp.dma_start(k.ctxr[:], d.ctxT[:, 0:CW]).then_inc(s.ctx_loaded, 16)
            n = SLOTS // 16
            for i in range(16):
                sp.dma_start(d.buf[i * n:(i + 1) * n, :].rearrange("(p r) d -> p (r d)", p=P),
                             k.zero[:]).then_inc(s.zeroed, 16)
            with sp.Fori(1, CHUNKS) as it:
                sp.wait_ge(s.ctx_free, it + 1)
                sp.dma_start(k.ctxr[:], d.ctxT[:, bass.ds(it * CW, CW)]).then_inc(s.ctx_loaded, 16)
            sp.wait_ge(s.zeroed, 256)

        @block.gpsimd
        def _(g):
            def turn(it, x, y):
                if y:
                    norm_y.pool(g, it - 1)
                if x:
                    norm_x.pool(g, it)
                if y:
                    g.wait_ge(s.norm_max, it)
                    g.tensor_tensor(k.rn[:], k.ss2[:], k.mhalf[:], ALU.pow).then_inc(s.norm_inv, 1)
                    blocks.pool_lo(g, it * 2 - 2, 0, P, CW)
                    g.tensor_copy(k.xn_all[:, bass.ds((it - 1) * T, T), :], k.xn2[:]).then_inc(s.copied, 1)
                    blocks.pool_lo(g, it * 2 - 1, 1, P, CW)

            turns(g, turn)

        @block.vector
        def _(v):
            def turn(it, x, y):
                if x:
                    xs = k.x[:, bass.ds(it * T, T), :]
                if y:
                    ys = k.x[:, bass.ds((it - 1) * T, T), :]
                    norm_y.vector(v, it - 1, [k.x[:, (it - 1) * T + j, :] for j in range(T)])
                    v.drain()
                if x:
                    norm_x.vector(v, it, [k.x[:, it * T + j, :] for j in range(T)])
                if y:
                    v.wait_ge(s.hi, it)
                    v.tensor_tensor(k.xl[:], pX[:], k.xh[:].bitcast(F32), ALU.subtract).then_inc(s.lo, 1)
                    v.wait_ge(s.square, it)
                    v.tensor_scalar(k.ss2[:], k.ss[:], 1e-24, None, ALU.max).then_inc(s.norm_max, 1)
                if x:
                    v.wait_ge(s.qkv, it + 1)
                    v.tensor_tensor(k.v0[:], by_tile(pV), row(B_BV0), ALU.add).then_inc(s.v_read, 1)
                if y:
                    blocks.vector_h(v, it * 2 - 2, 0, 0, P, CW, 2)
                if x:
                    v.wait_ge(s.scores, it + 1)
                    v.reduce_max(k.mx[:, 0:T], by_tile(pV), axis=AX.X)
                    v.drain()
                    v.tensor_tensor(k.pr[:], by_tile(pV), each(k.mx[:, 0:T]), ALU.subtract).then_inc(s.centred, 1)
                if y:
                    blocks.vector_h(v, it * 2 - 1, 0, 1, P, CW, 2)
                if x:
                    v.wait_ge(s.exp, it + 1)
                    v.reduce_sum(k.mx[:, T:2 * T], k.pr[:], axis=AX.X)
                    v.drain()
                    v.reciprocal(k.mx[:, 2 * T:3 * T], k.mx[:, T:2 * T])
                    v.drain()
                    v.tensor_tensor(k.pr[:], k.pr[:], each(k.mx[:, 2 * T:3 * T]), ALU.mult).then_inc(s.probs, 1)
                    v.tensor_tensor(xs, xs, row(B_BO0), ALU.add)
                    v.drain()
                if y:
                    v.wait_ge(s.norm_inv, it)
                    v.wait_ge(s.logits, it)
                    v.tensor_tensor(k.sc[:, bass.ds((it - 1) * T, T), :], pX[:, 0:T * 40].rearrange("p (t n) -> p t n", n=40),
                                    k.rn[:].unsqueeze(2).to_broadcast([P, T, 40]), ALU.mult)
                    v.wait_ge(blocks.h_free, it * 2 + 2)
                    v.scalar_tensor_tensor(ys, by_tile(pSum), k.tg[:, 4:5], ys, ALU.mult, ALU.add)
                if x:
                    v.wait_ge(s.out, it + 1)
                    v.scalar_tensor_tensor(xs, by_tile(pK), k.tg[:, 0:1], xs, ALU.mult, ALU.add)
                v.drain()
                if y:
                    v.wait_ge(s.copied, it)

            v.sem_inc(s.ctx_free, 1)
            blocks.credits(v)
            turns(v, turn)

        @block.scalar
        def _(act):
            def turn(it, x, y):
                if y:
                    act.wait_ge(s.fT, it)
                    act.activation(k.xh[:], pX[:], ACT.Copy).then_inc(s.hi, 1)
                    for j in range(T):
                        last = act.activation(k.junk[:, tile[j]], k.xn2[:, j, :], ACT.Square, accum_out=k.ss[:, j:j + 1])
                    last.then_inc(s.square, 1)
                if x:
                    act.wait_ge(s.xT, it + 1)
                    act.activation(k.xT[:], pT[:], ACT.Copy).then_inc(s.xTs, 1)
                if y:
                    blocks.scalar_silu(act, it * 2 - 2, 0, P, CW)
                if x:
                    act.wait_ge(s.qkv, it + 1)
                    act.activation(k.qT[:], pQ[:], ACT.Identity, bias=k.bcol[:, 0:1])
                    act.activation(k.kT[:], pK[:], ACT.Identity, bias=k.bcol[:, 1:2]).then_inc(s.qk_read, 1)
                if y:
                    blocks.scalar_hi(act, it * 2 - 2, 0, P, CW)
                    blocks.scalar_silu(act, it * 2 - 1, 0, P, CW)
                if x:
                    act.wait_ge(s.centred, it + 1)
                    act.activation(k.pr[:], k.pr[:], ACT.Exp, scale=float(P) ** -0.5).then_inc(s.exp, 1)
                if y:
                    blocks.scalar_hi(act, it * 2 - 1, 1, P, CW)
                if x:
                    act.wait_ge(s.pT, it + 1)
                    act.activation(k.pT[:], pT[:], ACT.Copy).then_inc(s.pTs, 1)
                    act.wait_ge(s.o, it + 1)
                    act.activation(k.oT[:], pQ[:], ACT.Copy).then_inc(s.os, 1)

            turns(act, turn)

        @block.tensor
        def _(pe):
            def gate_up(a, n):
                blocks.tensor_gu(pe, a, 0, k.sh0h, k.sh0l, n * P, HID0 + n * P, P, k.xh[:], k.xl[:], back=1)

            def down(a, n):
                w = slice(2 * HID0 + n * P, 2 * HID0 + (n + 1) * P)
                blocks.tensor_down(pe, a, n, P, [(j * P, (j + 1) * P) for j in range(T)],
                                   lambda j: pSum[:, tile[j]], k.sh0h[:, w], k.sh0l[:, w], n == 0, True)

            def turn(it, x, y):
                if y:
                    pe.wait_ge(norm_y.ready, it)
                    for j in range(T):
                        last = pe.transpose(pX[:, tile[j]], k.xn2[:, j, :], k.ident)
                    last.then_inc(s.fT, 1)
                if x:
                    pe.wait_ge(s.ctx_loaded, it * 16 + 16)
                    pe.matmul(pK[:], k.wa0[:, P:2 * P], k.ctxr[:], start=True, stop=True)
                    for j in range(T):
                        last = pe.matmul(pV[:, tile[j]], k.ctxr[:, tile[j]], k.wa0[:, 2 * P:3 * P], start=True, stop=True)
                    last.then_inc(s.ctx_free, 1)
                    pe.wait_ge(norm_x.ready, it + 1)
                    for j in range(T):
                        last = pe.transpose(pT[:, tile[j]], k.xn[:, j, :], k.ident)
                    last.then_inc(s.xT, 1)
                if y:
                    pe.wait_ge(s.lo, it)
                    gate_up(it * 2 - 2, 0)
                if x:
                    pe.wait_ge(s.xTs, it + 1)
                    pe.matmul(pQ[:], k.wa0[:, 0:P], k.xT[:], start=True, stop=True).then_inc(s.qkv, 1)
                if y:
                    for j in range(T):
                        last = three_pass(pe, pX[:, j * 40:(j + 1) * 40], k.xh[:, tile[j]], k.xl[:, tile[j]],
                                          k.g0h[:], k.g0l[:])
                    last.then_inc(s.logits, 1)
                    gate_up(it * 2 - 1, 1)
                if x:
                    pe.wait_ge(s.v_read, it + 1)
                    pe.wait_ge(s.qk_read, it + 1)
                    for j in range(T):
                        last = pe.matmul(pV[:, tile[j]], k.qT[:, tile[j]], k.kT[:, tile[j]], start=True, stop=True)
                    last.then_inc(s.scores, 1)
                if y:
                    down(it * 2 - 2, 0)
                if x:
                    pe.wait_ge(s.probs, it + 1)
                    for j in range(T):
                        last = pe.transpose(pT[:, tile[j]], k.pr[:, j, :], k.ident)
                    last.then_inc(s.pT, 1)
                if y:
                    down(it * 2 - 1, 1)
                if x:
                    pe.wait_ge(s.pTs, it + 1)
                    for j in range(T):
                        last = pe.matmul(pQ[:, tile[j]], k.v0[:, j, :], k.pT[:, tile[j]], start=True, stop=True)
                    last.then_inc(s.o, 1)
                    pe.wait_ge(s.os, it + 1)
                    for j in range(T):
                        last = pe.matmul(pK[:, tile[j]], k.oT[:, tile[j]], k.wa0[:, 3 * P:4 * P], start=True, stop=True)
                    last.then_inc(s.out, 1)

            turns(pe, turn)


def layer0_route(nc, k, d):
    s = Names(**{n: k.sem("route_" + n) for n in ("centred", "exp", "mask", "ranks", "index", "sent", "split",
        "ctx", "csum", "rsum", "mean", "turned", "mix", "mix_stored")})
    jobs = [(d.wa1[:, 4 * P:8 * P], k.wkh[:, 0:4 * P], k.wkl[:, 0:4 * P]),
            (d.wa1[:, 8 * P:9 * P], k.wkh[:, 4 * P:5 * P], k.wkl[:, 4 * P:5 * P]),
            (d.brow, k.bkh[:], k.bkl[:])]
    for src, h, l in ((d.w1, k.w1h, k.w1l), (d.w2, k.w2h, k.w2l)):
        jobs += [(src[:, c:c + 864], h[:, c:c + 864], l[:, c:c + 864]) for c in range(0, NB1 * W1C, 864)]
    sync_w, scalar_w, vector_w = load_and_split(nc, k, "route_w", jobs)
    assert len(jobs) == PIECES
    sync_k, scalar_k, vector_k, tensor_k = layer1_keys(nc, k, d, sync_w, scalar_w, vector_w)
    flat = lambda a: a.rearrange("p t n -> p (t n)")
    r = k.route
    full = [P, SEQS, E0]
    with nc.Block() as block:
        @block.sync
        def _(sp):
            sync_w(sp, 0, 5)
            sp.dma_start(k.ctxT[:], d.ctxT[:, :]).then_inc(s.ctx, 16)
            sp.dma_start(k.w2t[:], d.l2w[:, P:2 * P]).then_inc(s.ctx, 16)
            sync_k(sp)
            sp.wait_ge(s.mix, 1)
            sp.dma_start(d.mix[:, :], k.mix[:]).then_inc(s.mix_stored, 16)
            sp.wait_ge(s.mix_stored, 16)

        @block.vector
        def _(v):
            g8 = r.gmask[:]
            topk_mask(v, k.sc[:, :, 0:G0], r.m8, K0, g8, r.t8a[:], r.t8b[:], r.t8c[:], r.cnt[:],
                      k.const0[:, L_R8:L_R8 + SEQS * G0])
            v.tensor_tensor(r.es[:], k.sc[:, :, G0:G0 + E0],
                            k.rows[:, B_BIAS0:B_BIAS0 + E0].unsqueeze(1).to_broadcast(full), ALU.add)
            v.tensor_scalar(r.t8a[:], g8, 1e9, -1e9, ALU.mult, ALU.add)
            v.drain()
            groups = r.es[:].rearrange("p t (g f) -> p (t g) f", f=E0 // G0)
            per_group = lambda a: flat(a).unsqueeze(2).to_broadcast([P, SEQS * G0, E0 // G0])
            v.tensor_tensor(groups, groups, per_group(g8), ALU.mult)
            v.drain()
            v.tensor_tensor(groups, groups, per_group(r.t8a[:]), ALU.add)
            v.drain()
            topk_mask(v, r.es[:], r.m8, K0, r.mask[:], r.gt[:], r.eq[:], r.pre[:], r.cnt[:],
                      k.const0[:, L_R32:L_R32 + SEQS * E0])
            v.tensor_copy(r.maskb[:], flat(r.mask[:])).then_inc(s.mask, 1)
            v.tensor_tensor(r.es[:], r.es[:], r.m8[:, :, 0:1].to_broadcast(full), ALU.subtract).then_inc(s.centred, 1)
            v.tensor_tensor_scan(flat(r.pre[:]), k.const0[:, L_R32:L_R32 + SEQS * E0], flat(r.mask[:]), 0.0,
                                 ALU.mult, ALU.add)
            v.drain()
            v.tensor_tensor(r.pre[:], r.pre[:], r.mask[:], ALU.mult)
            v.wait_ge(s.ranks, 1)
            v.tensor_copy(r.tot[:], k.ps[1][:].rearrange("p (t n) -> p n t", n=E0))
            v.drain()
            v.tensor_tensor_scan(flat(r.cum[:]), k.const0[:, L_R16T:L_R16T + SEQS * E0], flat(r.tot[:]), 0.0,
                                 ALU.mult, ALU.add)
            v.drain()
            v.tensor_tensor(r.cum[:], r.cum[:], r.tot[:], ALU.subtract)
            v.drain()
            v.tensor_tensor(r.slot[:], k.ps[0][:].rearrange("p (t n) -> p t n", n=E0),
                            r.cum[:].rearrange("p n t -> p t n"), ALU.add)
            v.drain()
            v.tensor_scalar(r.gt[:], r.slot[:], float(CAP), None, ALU.is_lt)
            v.tensor_tensor(r.slot[:], r.slot[:], k.const0[:, L_START:L_START + E0].unsqueeze(1).to_broadcast(full), ALU.add)
            v.drain()
            v.scalar_tensor_tensor(r.slot[:], r.slot[:], k.const0[:, L_TRASH:L_TRASH + 1], r.gt[:],
                                   ALU.subtract, ALU.mult)
            v.drain()
            for n in range(K0):
                v.scalar_tensor_tensor(r.eq[:], r.pre[:], n + 1.0, r.slot[:], ALU.is_equal, ALU.mult)
                v.drain()
                v.reduce_sum(r.sl[:, n, :], r.eq[:], axis=AX.X)
                v.drain()
            sl = r.sl[:].rearrange("p k t -> p (k t)")
            v.tensor_scalar(k.index[:], sl, k.const0[:, L_TRASH:L_TRASH + 1], None, ALU.add)
            v.scalar_tensor_tensor(r.own[:], sl, 0.0, k.const0[:, L_SPREAD:L_SPREAD + K0 * SEQS], ALU.is_equal, ALU.mult)
            v.drain()
            v.scalar_tensor_tensor(r.dest[:], sl, k.const0[:, L_TRASH:L_TRASH + 1], r.own[:], ALU.add, ALU.add)\
                .then_inc(s.index, 1)
            v.wait_ge(s.exp, 1)
            v.tensor_tensor(r.es[:], r.es[:], r.mask[:], ALU.mult)
            v.drain()
            v.reduce_sum(r.cnt[:], r.es[:], axis=AX.X)
            v.drain()
            v.reciprocal(r.rec[:], r.cnt[:])
            v.tensor_tensor(r.es[:], r.es[:], r.gt[:], ALU.mult)
            v.drain()
            v.tensor_scalar(r.rec[:], r.rec[:], k.tg[:, 4:5], None, ALU.mult)
            v.drain()
            v.tensor_tensor(r.es[:], r.es[:], r.rec[:].unsqueeze(2).to_broadcast(full), ALU.mult)
            v.drain()
            for n in range(K0):
                v.scalar_tensor_tensor(r.eq[:], r.pre[:], n + 1.0, r.es[:], ALU.is_equal, ALU.mult)
                v.drain()
                v.reduce_sum(k.gate[:, n, :], r.eq[:], axis=AX.X)
                v.drain()
            vector_w(v, 0, 3)
            v.drain().then_inc(s.split, 1)
            seqs = k.ctxT[:].rearrange("p (s t) -> p s t", t=P)

            def context(turn):
                if turn == 0:
                    v.wait_ge(s.ctx, 32)
                    v.reduce_sum(k.csum[:], seqs, axis=AX.X).then_inc(s.csum, 1)
                    v.drain()
                elif turn == 1:
                    v.scalar_tensor_tensor(k.ctxT[:], k.ctxT[:], 0.0, k.ctxT[:], ALU.max, ALU.mult)
                    v.drain()
                elif turn == 2:
                    v.reduce_sum(k.rsum[:], seqs, axis=AX.X).then_inc(s.rsum, 1)

            vector_k(v, context)
            v.wait_ge(s.mean, 1)
            v.scalar_tensor_tensor(k.mix[:, 0:P], k.ps[6][0:SEQS, 0:P], 1.0 / P, k.rows[0:SEQS, B_B2:B_B2 + P],
                                   ALU.mult, ALU.add)
            v.wait_ge(s.turned, 1)
            v.tensor_scalar(k.mix[:, P:2 * P], k.ps[5][0:SEQS, 0:P], k.tg[0:SEQS, 3:4], None, ALU.mult)
            v.drain()
            v.tensor_scalar(k.mix[:, 0:P], k.mix[:, 0:P], k.tg[0:SEQS, 2:3], None, ALU.mult).then_inc(s.mix, 1)

        @block.scalar
        def _(act):
            act.wait_ge(s.centred, 1)
            act.activation(r.es[:], r.es[:], ACT.Exp).then_inc(s.exp, 1)
            for j in range(T):
                act.activation(k.one_k[:, j * P:(j + 1) * P], k.const0[0:1, L_ONE:L_ONE + P], ACT.Copy)
            scalar_w(act, 0, 3)
            scalar_k(act)

        @block.tensor
        def _(pe):
            pe.wait_ge(s.mask, 1)
            pe.matmul(k.ps[0][:], k.ub[:, 0:P], r.maskb[:], start=True, stop=True)
            pe.matmul(k.ps[1][:], k.ub[:, P:2 * P], r.maskb[:], start=True, stop=True).then_inc(s.ranks, 1)
            pe.wait_ge(s.split, 1)
            tensor_k(pe)
            pe.wait_ge(s.csum, 1)
            pe.matmul(k.ps[6][0:SEQS, 0:P], k.csum[:], k.w2t[:], start=True, stop=True).then_inc(s.mean, 1)
            pe.wait_ge(s.rsum, 1)
            pe.transpose(k.ps[5][0:SEQS, 0:P], k.rsum[:], k.ident).then_inc(s.turned, 1)

        @block.gpsimd
        def _(g):
            g.wait_ge(s.index, 1)
            for n in range(K0):
                for t in range(SEQS):
                    c = n * SEQS + t
                    g.indirect_dma_start(
                        out=d.buf[:, :], out_offset=bass.IndirectOffsetOnAxis(ap=r.dest[:, c:c + 1].bitcast(U32), axis=0),
                        in_=k.xn_all[:, t, :], in_offset=None).then_inc(s.sent, 16)
            g.wait_ge(s.sent, 16 * K0 * SEQS)


def layer0_experts(nc, k, d):
    s = Names(**{n: k.sem("ex_" + n) for n in (
        "gu0", "gu1", "dn0", "dn1", "rows0", "rows1", "gu_free", "dn_free", "rows_free", "gu_hi", "dn_hi", "gu_lo",
        "dn_lo", "turned", "x_hi", "x_lo", "sum_copied", "sum_turned", "out_sb", "stored0", "stored1")})
    raw_gu, raw_dn, rows, stored = (s.gu0, s.gu1), (s.dn0, s.dn1), (s.rows0, s.rows1), (s.stored0, s.stored1)
    e_ = k.ex
    blocks = Blocks(k, "ex_blk", k.gu, k.s, e_.h, e_.hh, e_.hl)
    pX, pSum, pO = (k.ps[4], k.ps[7]), k.ps[5], k.ps[6]
    starts = [j * RT for j in range(3)]

    def expert(i, r):
        if isinstance(i, int) and not 0 <= 2 * i + r < E0:
            return None
        return i * 2 + r, i + r // 2, r % 2

    def steps(eng, step):
        for e in range(-1, 4):
            step(0, e)
        with eng.Fori(2, E0 // 2 - 2) as i:
            for r in range(2):
                step(i, r)
        for e in range(E0 - 4, E0 + 3):
            step(0, e)

    with nc.Block() as block:
        @block.sync
        def _(sp):
            def load_gu(x):
                if x:
                    e, half, q = x
                    sp.wait_ge(s.gu_free, e + 1)
                    sp.dma_start(e_.raw_gu[q][:], d.w0[e, :, 0:2 * HID0]).then_inc(raw_gu[q], 16)

            def load_dn(x):
                if x:
                    e, half, q = x
                    sp.wait_ge(s.dn_free, e + 1)
                    sp.dma_start(e_.raw_dn[q][:], d.w0[e, :, 2 * HID0:3 * HID0]).then_inc(raw_dn[q], 16)

            def load_rows(x):
                if x:
                    e, half, q = x
                    sp.wait_ge(s.rows_free, e + 1)
                    sp.dma_start(e_.rows[q][0:RT, 0:2, :],
                                 d.buf[bass.ds(e * CAP, 2 * RT), :].rearrange("(r p) d -> p r d", p=RT)).then_inc(rows[q], 16)
                    sp.dma_start(e_.rows[q][0:ROWS[2], 2, :],
                                 d.buf[bass.ds(e * CAP + 2 * RT, ROWS[2]), :]).then_inc(rows[q], 16)

            def store(x):
                if x:
                    e, half, q = x
                    sp.wait_ge(s.out_sb, e + 2)
                    sp.dma_start(d.oute[bass.ds(e * CAP, 2 * RT), :].rearrange("(r p) d -> p r d", p=RT),
                                 e_.out[q][0:RT, 0:2, :]).then_inc(stored[q], 16)
                    sp.dma_start(d.oute[bass.ds(e * CAP + 2 * RT, ROWS[2]), :],
                                 e_.out[q][0:ROWS[2], 2, :]).then_inc(stored[q], 16)

            def step(i, r):
                if isinstance(i, int) and r == -1:
                    for x in (expert(0, n) for n in range(3)):
                        load_gu(x)
                        load_rows(x)
                        if x[0] < 2:
                            load_dn(x)
                    load_gu(expert(0, 3))
                    return
                load_rows(expert(i, r + 3))
                load_gu(expert(i, r + 4))
                load_dn(expert(i, r + 2))
                store(expert(i, r - 3))

            steps(sp, step)
            for q in range(2):
                sp.wait_ge(stored[q], 1 + 16 * E0)

        @block.gpsimd
        def _(g):
            with g.Fori(0, E0 // 2) as i:
                for q in range(2):
                    for n in range(2):
                        blocks.pool_lo(g, i * 4 + (2 * q + n), 2 * q + n, P, CAP)

        @block.vector
        def _(v):
            def x_low(x):
                if x:
                    e, half, q = x
                    v.wait_ge(s.x_hi, e + 1)
                    v.tensor_tensor(e_.xl[q][:], pX[q][:, 0:CAP], e_.xh[q][:].bitcast(F32), ALU.subtract).then_inc(s.x_lo, 1)
                    v.drain().then_inc(s.rows_free, 1)

            def low(x, raw, high, lo, high_done, done, free):
                if x:
                    e, half, q = x
                    v.wait_ge(high_done, e + 1)
                    v.tensor_tensor(lo[q][:], raw[q][:], high[q][:].bitcast(F32), ALU.subtract).then_inc(done, 1)
                    v.drain().then_inc(free, 1)

            def gu_low(x):
                low(x, e_.raw_gu, e_.guh, e_.gul, s.gu_hi, s.gu_lo, s.gu_free)

            def step(i, r):
                x_low(expert(i, r + 1))
                x = expert(i, r)
                if x:
                    for n in range(2):
                        blocks.vector_h(v, x[0] * 2 + n, n, 2 * x[2] + n, P, CAP, 4)
                gu_low(expert(i, r + 2) if not (isinstance(i, int) and r < 0) else None)
                low(x, e_.raw_dn, e_.dnh, e_.dnl, s.dn_hi, s.dn_lo, s.dn_free)

            blocks.credits(v)
            for sem in (s.gu_free, s.dn_free, s.rows_free):
                v.sem_inc(sem, 2)
            for sem in (s.sum_copied, s.out_sb) + stored:
                v.sem_inc(sem, 1)
            gu_low(expert(0, 0))
            gu_low(expert(0, 1))
            steps(v, step)

        @block.scalar
        def _(act):
            def x_high(x):
                if x:
                    e, half, q = x
                    act.wait_ge(s.turned, e + 1)
                    act.activation(e_.xh[q][:], pX[q][:, 0:CAP], ACT.Copy).then_inc(s.x_hi, 1)

            def gu_high(x):
                if x:
                    e, half, q = x
                    if not (isinstance(e, int) and e < 2):
                        act.wait_ge(blocks.gu_ready, e * 2 - 2)
                    act.wait_ge(raw_gu[q], half * 16 + 16)
                    act.activation(e_.guh[q][:], e_.raw_gu[q][:], ACT.Copy).then_inc(s.gu_hi, 1)

            def dn_high(x):
                if x:
                    e, half, q = x
                    act.wait_ge(blocks.h_free, e * 2 + 2)
                    act.wait_ge(raw_dn[q], half * 16 + 16)
                    act.activation(e_.dnh[q][:], e_.raw_dn[q][:], ACT.Copy).then_inc(s.dn_hi, 1)

            def sum_copy(x):
                if x:
                    act.wait_ge(blocks.h_free, x[0] * 2 + 6)
                    act.activation(e_.sum[:], pSum[:, 0:CAP], ACT.Copy).then_inc(s.sum_copied, 1)

            def out(x):
                if x:
                    e, half, q = x
                    act.wait_ge(s.sum_turned, e + 1)
                    act.wait_ge(stored[q], half * 32 + 1)
                    act.activation(e_.out[q][0:RT, 0:2, :], pO[0:RT, 0:2 * P].rearrange("p (r d) -> p r d", d=P), ACT.Copy)
                    act.activation(e_.out[q][0:ROWS[2], 2, :], pO[0:ROWS[2], 2 * P:3 * P], ACT.Copy)
                    act.drain().then_inc(s.out_sb, 1)

            def step(i, r):
                x = expert(i, r)
                x_high(expert(i, r + 1))
                if x:
                    blocks.scalar_silu(act, x[0] * 2, 0, P, CAP)
                out(expert(i, r - 3))
                sum_copy(expert(i, r - 2))
                if x:
                    blocks.scalar_silu(act, x[0] * 2 + 1, 1, P, CAP)
                    blocks.scalar_hi(act, x[0] * 2, 2 * x[2], P, CAP)
                gu_high(expert(i, r + 2) if not (isinstance(i, int) and r < 0) else None)
                if x:
                    blocks.scalar_hi(act, x[0] * 2 + 1, 2 * x[2] + 1, P, CAP)
                dn_high(x)

            gu_high(expert(0, 0))
            gu_high(expert(0, 1))
            steps(act, step)

        @block.tensor
        def _(pe):
            def rows_turned(x):
                if x:
                    e, half, q = x
                    pe.wait_ge(rows[q], half * 32 + 32)
                    for j, m in enumerate(ROWS):
                        last = pe.transpose(pX[q][:, starts[j]:starts[j] + m], e_.rows[q][0:m, j, :], k.ident[0:m, 0:m])
                    last.then_inc(s.turned, 1)

            def gate_up(x, n):
                if x:
                    e, half, q = x
                    if n == 0:
                        pe.wait_ge(s.gu_lo, e + 1)
                        pe.wait_ge(s.x_lo, e + 1)
                    blocks.tensor_gu(pe, e * 2 + n, n, e_.guh[q], e_.gul[q], n * P, HID0 + n * P, P, e_.xh[q][:], e_.xl[q][:])

            def down(x):
                if x:
                    e, half, q = x
                    pe.wait_ge(s.dn_lo, e + 1)
                    pe.wait_ge(s.sum_copied, e + 1)
                    for n in range(2):
                        w = slice(n * P, (n + 1) * P)
                        pe.wait_ge(blocks.lo, e * 2 + n + 1)
                        three_pass(pe, pSum[:, 0:CAP], e_.dnh[q][:, w], e_.dnl[q][:, w],
                                   e_.hh[2 * q + n][:], e_.hl[2 * q + n][:], start=n == 0, stop=n == 1)\
                            .then_inc(blocks.h_free, 1)

            def turn_back(x):
                if x:
                    e = x[0]
                    pe.wait_ge(s.sum_copied, e + 2)
                    pe.wait_ge(s.out_sb, e + 1)
                    for j, m in enumerate(ROWS):
                        last = pe.transpose(pO[0:m, j * P:(j + 1) * P], e_.sum[:, starts[j]:starts[j] + m], k.ident)
                    last.then_inc(s.sum_turned, 1)

            def step(i, r):
                rows_turned(expert(i, r + 1))
                gate_up(expert(i, r), 0)
                turn_back(expert(i, r - 3))
                down(expert(i, r - 2))
                gate_up(expert(i, r), 1)

            steps(pe, step)


class Combine:

    def __init__(self, k, d, slots):
        self.k, self.d, self.slots = k, d, slots
        self.got = [k.sem(f"comb_got{i}") for i in range(2)]
        self.used = k.sem("comb_used")

    def pool(self, g, t):
        k, y = self.k, self.slots[t % 2]
        if t >= 2:
            g.wait_ge(self.used, t - 1)
        for n in range(K0):
            c = n * SEQS + t
            g.indirect_dma_start(
                out=y[:, n * P:(n + 1) * P], out_offset=None, in_=self.d.oute[:, :],
                in_offset=bass.IndirectOffsetOnAxis(ap=k.index[:, c:c + 1].bitcast(U32), axis=0)).then_inc(self.got[t % 2], 16)

    def vector(self, v, t):
        k, y = self.k, self.slots[t % 2]
        v.wait_ge(self.got[t % 2], 16 * K0 * (t // 2 + 1))
        for n in range(K0):
            v.scalar_tensor_tensor(k.x[:, t, :], y[:, n * P:(n + 1) * P], k.gate[:, n, t:t + 1], k.x[:, t, :],
                                   ALU.mult, ALU.add)
            last = v.drain()
        last.then_inc(self.used, 1)


def layer0_combine(nc, k, d):
    jobs = [(d.w3[e], k.w3h[:, e * W3C:(e + 1) * W3C], k.w3l[:, e * W3C:(e + 1) * W3C]) for e in range(E3 + 1)]
    jobs += [(d.wa1[:, 0:4 * P], k.wa1h[:, 0:4 * P], k.wa1l[:, 0:4 * P]),
             (d.wa1[:, 9 * P:10 * P], k.wa1h[:, 4 * P:5 * P], k.wa1l[:, 4 * P:5 * P]),
             (d.gates, k.gth[:], k.gtl[:]), (d.sel, k.selh[:], None)]
    sync_w, scalar_w, vector_w = load_and_split(nc, k, "comb_w", jobs)
    with nc.Block() as block:
        @block.sync
        def _(sp):
            sync_w(sp)

        @block.scalar
        def _(act):
            scalar_w(act)

        @block.gpsimd
        def _(g):
            for t in range(T):
                k.combine.pool(g, t)

        @block.vector
        def _(v):
            for t in range(T):
                vector_w(v, t * len(jobs) // T, (t + 1) * len(jobs) // T)
                k.combine.vector(v, t)


def layer1_keys(nc, k, d, sync_w, scalar_w, vector_w):
    s = Names(**{n: k.sem("key_" + n) for n in (
        "loaded", "free", "hi", "lo", "k", "high", "done", "v", "v_done", "v_stored")})
    k_stored = [k.sem(f"key_stored{i}") for i in range(2)]
    bank = (k.ps[2], k.ps[3])
    pV = k.ps[4]
    tile = [slice(j * P, (j + 1) * P) for j in range(T)]

    def sync(sp):
        def load(it):
            sp.wait_ge(s.free, it + 1)
            sp.dma_start(k.ctx1[:], d.ctxT[:, it * CW:(it + 1) * CW]).then_inc(s.loaded, 16)

        load(0)
        for it in range(CHUNKS):
            if it < CHUNKS - 1:
                load(it + 1)
            for q in range(4):
                sp.wait_ge(s.done, it * 4 + q + 3)
                sp.dma_start(d.keys1[bass.ds(it * T, T), :, q * P:(q + 1) * P].rearrange("j p t -> p j t"),
                             k.k3[q % 2][:].bitcast(F32).rearrange("p (j t) -> p j t", t=P)).then_inc(k_stored[q % 2], 16)
            sync_w(sp, 5 + 2 * it, min(7 + 2 * it, PIECES))
            sp.wait_ge(s.v_done, it + 1)
            sp.dma_start(d.values1[bass.ds(it * T, T), :, :].rearrange("j p c -> p j c"),
                         k.v9k[:].rearrange("p j h d -> p j (h d)")).then_inc(s.v_stored, 16)
        for q in range(2):
            sp.wait_ge(k_stored[q], CHUNKS * 32 + 1)
        sp.wait_ge(s.v_stored, CHUNKS * 16 + 1)

    def scalar(act):
        for it in range(CHUNKS):
            act.wait_ge(s.loaded, it * 16 + 16)
            act.wait_ge(s.v, it + 1)
            act.activation(k.cth[:], k.ctx1[:], ACT.Copy).then_inc(s.hi, 1)
            for q in range(4):
                act.wait_ge(s.k, it * 4 + q + 1)
                act.activation(k.kh[q % 2][:], bank[q % 2][:], ACT.Copy).then_inc(s.high, 1)
                if q % 2:
                    scalar_w(act, 3 + 2 * it + q // 2, 4 + 2 * it + q // 2)

    def vector(v, between):
        v.memset(k.v9k[:], 1.0)
        for sem in (s.free, s.v, s.v_stored, k_stored[0], k_stored[1]):
            v.sem_inc(sem, 1)
        v.sem_inc(s.done, 2)
        v.drain()
        for it in range(CHUNKS):
            v.wait_ge(s.hi, it + 1)
            v.tensor_tensor(k.ctl[:], k.ctx1[:], k.cth[:].bitcast(F32), ALU.subtract).then_inc(s.lo, 1)
            v.drain().then_inc(s.free, 1)
            for q in range(4):
                v.wait_ge(s.high, it * 4 + q + 1)
                v.wait_ge(k_stored[q % 2], it * 32 + q // 2 * 16 + 1)
                v.scalar_tensor_tensor(k.k3[q % 2][:], k.kh[q % 2][:].bitcast(F32), k.const[:, C_SPLIT + 1:C_SPLIT + 2],
                                       bank[q % 2][:], ALU.mult, ALU.add).then_inc(s.done, 1)
                if q == 0:
                    between(it)
                if q % 2:
                    vector_w(v, 3 + 2 * it + q // 2, 4 + 2 * it + q // 2)
            v.wait_ge(s.v, it + 2)
            v.wait_ge(s.v_stored, it * 16 + 1)
            for j in range(T):
                last = v.tensor_tensor(k.v9k[:, j, :, 0:HD], pV[:, tile[j]].rearrange("p (h d) -> p h d", d=HD),
                                       k.rows[:, B_BV1:B_BV1 + P].rearrange("p (h d) -> p h d", d=HD), ALU.add)
            last.then_inc(s.v_done, 1)

    def tensor(pe):
        for it in range(CHUNKS):
            pe.wait_ge(s.lo, it + 1)
            for q in range(4):
                c = slice(q * P, (q + 1) * P)
                pe.wait_ge(s.done, it * 4 + q + 1)
                three_pass(pe, bank[q % 2][:], k.wkh[:, c], k.wkl[:, c], k.cth[:], k.ctl[:], stop=False)
                pe.matmul(bank[q % 2][:], k.bkh[:, c], k.one_k[:], start=False, stop=False)
                pe.matmul(bank[q % 2][:], k.bkl[:, c], k.one_k[:], start=False, stop=True).then_inc(s.k, 1)
            for j in range(T):
                last = three_pass(pe, pV[:, tile[j]], k.cth[:, tile[j]], k.ctl[:, tile[j]],
                                  k.wkh[:, 4 * P:5 * P], k.wkl[:, 4 * P:5 * P])
            last.then_inc(s.v, 1)
            pe.wait_ge(s.v_done, it + 1)

    return sync, scalar, vector, tensor


def layer0_experts_all(nc, k, d, sb):
    with ExitStack() as rt:
        r = k.route = Names()
        r.m8 = sb("r_m8", [P, SEQS, 8], c=rt)
        r.gmask, r.t8a, r.t8b, r.t8c = (sb("r_" + n, [P, SEQS, 8], c=rt) for n in ("gmask", "t8a", "t8b", "t8c"))
        r.cnt, r.rec = sb("r_cnt", [P, SEQS], c=rt), sb("r_rec", [P, SEQS], c=rt)
        r.sl, r.own = sb("r_sl", [P, K0, SEQS], c=rt), sb("r_own", [P, K0 * SEQS], c=rt)
        r.dest = sb("r_dest", [P, K0 * SEQS], I32, rt)
        r.es, r.mask, r.gt, r.eq, r.pre, r.slot = (
            sb("r_" + n, [P, SEQS, E0], c=rt) for n in ("es", "mask", "gt", "eq", "pre", "slot"))
        r.tot, r.cum = sb("r_tot", [P, E0, SEQS], c=rt), sb("r_cum", [P, E0, SEQS], c=rt)
        r.maskb = sb("r_maskb", [P, SEQS * E0], BF16, rt)
        k.wkh, k.wkl = sb("wkh", [P, 5 * P], F32R, rt), sb("wkl", [P, 5 * P], F32R, rt)
        k.bkh, k.bkl = sb("bkh", [1, 4 * P], F32R, rt), sb("bkl", [1, 4 * P], F32R, rt)
        k.ctx1, k.one_k = sb("ctx1", [P, CW], c=rt), sb("one_k", [1, CW], F32R, rt)
        k.cth, k.ctl = sb("cth", [P, CW], F32R, rt), sb("ctl", [P, CW], F32R, rt)
        k.kh, k.k3 = ([sb(f"{n}{i}", [P, CW], F32R, rt) for i in range(2)] for n in ("kh", "k3"))
        k.w2t, k.ctxT = sb("w2t", [P, P], c=rt), sb("ctxT", [P, SEQS * P], c=rt)
        k.csum, k.rsum = sb("csum", [P, SEQS], c=rt), sb("rsum", [P, SEQS], c=rt)
        k.mix = sb("mix", [SEQS, 2 * P], c=rt)
        k.v9k = sb("v9k", [P, T, HEADS, HD + 1], c=rt)
        layer0_route(nc, k, d)
    with ExitStack() as ex:
        e = k.ex = Names()
        two = lambda name, shape, dt=F32: [sb(f"e_{name}{i}", shape, dt, ex) for i in range(2)]
        e.raw_gu, e.raw_dn, e.rows = two("rgu", [P, 2 * HID0]), two("rdn", [P, HID0]), two("rows", [P, 3, P])
        e.guh, e.gul = two("guh", [P, 2 * HID0], F32R), two("gul", [P, 2 * HID0], F32R)
        e.dnh, e.dnl = two("dnh", [P, HID0], F32R), two("dnl", [P, HID0], F32R)
        e.xh, e.xl = two("xh", [P, CAP], F32R), two("xl", [P, CAP], F32R)
        e.out, e.sum = two("out", [P, 3, P]), sb("e_sum", [P, CAP], c=ex)
        e.h = [sb(f"e_h{i}", [P, CAP], c=ex) for i in range(4)]
        e.hh = [sb(f"e_hh{i}", [P, CAP], F32R, ex) for i in range(4)]
        e.hl = [sb(f"e_hl{i}", [P, CAP], F32R, ex) for i in range(4)]
        layer0_experts(nc, k, d)


class Line:
    SLOTS_GU, SLOTS_H, SLOTS_HH = 2, 2, 3

    def __init__(self, k):
        self.k = k
        self.gu_ready = k.sem("line_gu_ready")
        self.gu_free = k.sem("line_gu_free")
        self.silu = k.sem("line_silu")
        self.h_ready = k.sem("line_h_ready")
        self.hi = k.sem("line_hi")
        self.lo = k.sem("line_lo")
        self.down_done = k.sem("line_down_done")
        self.cb, self.cb_free = k.sem("line_cb"), k.sem("line_cb_free")
        self.sum_a = k.sem("line_sum_a")
        self.sum_b = k.sem("line_sum_b")
        self.sum_read = k.sem("line_sum_read")

    def credits(self, v):
        v.sem_inc(self.gu_free, self.SLOTS_GU)
        v.sem_inc(self.lo, self.SLOTS_H)
        v.sem_inc(self.down_done, self.SLOTS_HH)
        v.sem_inc(self.cb_free, 1)
        v.sem_inc(self.sum_read, 1)


STEPS = T * 4 + 2
FILLERS = {"norm0": 1, "turned0": 1, "queries": 0} | {f"step{u}": int(1 <= u <= 16) for u in range(STEPS)} | {
    "heads": 1, "out": 1,
    "norm1": 1, "logits1": 0, "groups1": 0, "top1": 0, "weights1": 1, "sum1": 1,
    "norm2": 1, "norm3": 1, "logits2": 1, "groups2": 0, "top2": 0, "weights2": 0, "sum2": 1,
    "norm4": 0, "norm5": 0}
B3 = [(e, m) for e in range(E3 + 1) for m in range(3)]


def turn_order(a, b):
    order, left = [], list(range(len(B3)))
    if not a:
        return [(3, n, n % 2) for n in left]
    for name in FILLERS:
        attends = name.startswith("step") or name in ("norm0", "turned0")
        if b:
            order += [(3, left.pop(0), 0 if attends else (len(order) + i) % 2) for i in range(FILLERS[name])]
        if name in ("weights1", "weights2"):
            order += [(int(name[-1]), n, (len(order) + n) % 2) for n in range(NB1)]
    assert not (b and left)
    return order


class Part:

    def __init__(self, line, eng, n0, it, a=True, b=True):
        self.line, self.k, self.eng, self.n0, self.it, self.b = line, line.k, eng, n0, it, b
        self.order = turn_order(a, b)
        self.at = 0
        self.done = 0

    def rows(self, p):
        layer, n, _ = self.order[p]
        return M3[B3[n][1]] if layer == 3 else P

    def fill(self, name):
        if self.b:
            for _ in range(FILLERS[name]):
                self.block()

    def catch_up(self):
        last = max(p for p in range(self.at) if self.order[p][0] < 3)
        while self.done <= last:
            self.late(True)

    def flush(self):
        while self.done < self.at:
            self.late(True)


class TensorPart(Part):

    def up(self):
        pe, k, line, p = self.eng, self.k, self.line, self.at
        layer, n, g = self.order[p]
        before = [q for q in range(p) if self.order[q][2] == g]
        back = p - before[-1] if before else p + 1
        m = self.rows(p)
        if layer == 3:
            e, part = B3[n]
            wh, wl, x = k.w3h, k.w3l, (k.xbh, k.xbl)
            g0 = e * W3C + part * P
            u0 = g0 + FF3
        else:
            wh, wl = (k.w1h, k.w1l) if layer == 1 else (k.w2h, k.w2l)
            x = (k.xh, k.xl)
            g0 = n * W1C
            u0 = g0 + P
        pe.wait_ge(line.gu_free, self.n0 + (p + 1 + line.SLOTS_GU - back))
        for c0, bank in ((g0, 0), (u0, 1)):
            last = three_pass(pe, k.gu[g][bank][0:m, :], wh[:, c0:c0 + m], wl[:, c0:c0 + m], x[0][:], x[1][:])
        last.then_inc(line.gu_ready, 1)
        self.at += 1

    def weights(self):
        pe, k, line = self.eng, self.k, self.line
        layer, b, _ = self.order[self.at - 1]
        if b < NB1 - 1:
            pe.wait_ge(line.cb_free, self.it * (2 * (NB1 - 1)) + ((layer - 1) * (NB1 - 1) + b + 1))
            sel = k.selh[0:E1, b * P:(b + 1) * P]
            pe.matmul(k.ps[5][:], sel, k.wTl, start=True, stop=False)
            pe.matmul(k.ps[5][:], sel, k.wTh, start=False, stop=True).then_inc(line.cb, 1)

    def late(self, now=False):
        pe, k, line, p = self.eng, self.k, self.line, self.done
        if not now and self.at - p <= 2:
            return
        layer, n, _ = self.order[p]
        if layer == 3:
            e, m = B3[n]
            c = e * W3C + 2 * FF3 + m * P
            wh, wl, out, first, last_one = k.w3h, k.w3l, k.ps[7], m == 0, m == 2
            if first:
                pe.wait_ge(line.sum_read, (self.it - 1) * (E3 + 1) + (e + 1))
        else:
            wh, wl = (k.w1h, k.w1l) if layer == 1 else (k.w2h, k.w2l)
            c = n * W1C + 2 * P
            out, first, last_one = k.ps[6], n == 0, n == NB1 - 1
        m, s = self.rows(p), p % line.SLOTS_HH
        pe.wait_ge(line.lo, self.n0 + (p + 1 + line.SLOTS_H))
        if layer < 3:
            last = three_pass(pe, out[:], wh[:, c:c + P], wl[:, c:c + P], k.hh[s][:], k.hl[s][:],
                              start=first, stop=last_one)
        else:
            for j in range(T):
                t = slice(j * P, (j + 1) * P)
                last = three_pass(pe, out[:, t], k.hh[s][0:m, t], k.hl[s][0:m, t], wh[0:m, c:c + P], wl[0:m, c:c + P],
                                  start=first and j == 0, stop=True, skip=True)
        last.then_inc(line.down_done, 1)
        if last_one:
            pe.drain().then_inc(line.sum_b if layer == 3 else line.sum_a, 1)
        self.done += 1

    def block(self):
        self.up()
        self.late()


class ScalarPart(Part):

    def silu(self):
        k, line, p = self.k, self.line, self.at
        g, m = self.order[p][2], self.rows(p)
        self.eng.wait_ge(line.gu_ready, self.n0 + (p + 1))
        self.eng.activation(k.s[g][0:m, :], k.gu[g][0][0:m, :], ACT.Tanh, scale=0.5).then_inc(line.silu, 1)
        self.at += 1

    def late(self, now=False):
        k, line, p = self.k, self.line, self.done
        if not now and self.at - p <= 1:
            return
        m, s = self.rows(p), p % line.SLOTS_HH
        self.eng.wait_ge(line.down_done, self.n0 + (p + 1))
        self.eng.wait_ge(line.h_ready, self.n0 + (p + 1))
        self.eng.activation(k.hh[s][0:m, :], k.h[p % line.SLOTS_H][0:m, :], ACT.Copy).then_inc(line.hi, 1)
        self.done += 1

    def block(self):
        self.silu()
        self.late()


class PoolPart(Part):

    def late(self, now=False):
        k, line, p = self.k, self.line, self.done
        if not now and self.at - p <= 1:
            return
        m, s = self.rows(p), p % line.SLOTS_HH
        self.eng.wait_ge(line.hi, self.n0 + (p + 1))
        self.eng.tensor_tensor(k.hl[s][0:m, :], k.h[p % line.SLOTS_H][0:m, :], k.hh[s][0:m, :].bitcast(F32),
                               ALU.subtract).then_inc(line.lo, 1)
        self.done += 1

    def block(self):
        self.at += 1
        self.late()


class VectorPart(Part):

    def late(self, now=False):
        v, k, line, p = self.eng, self.k, self.line, self.done
        if not now and self.at - p <= 2:
            return
        self.done += 1
        layer, n, _ = self.order[p]
        if layer != 3 or B3[n][1] != 2:
            return
        e = B3[n][0]
        v.wait_ge(line.sum_b, (self.it - 1) * (E3 + 1) + (e + 1))
        if e == 0:
            v.tensor_copy(k.acc[:], k.ps[7][:].rearrange("p (t d) -> p t d", d=P))
        else:
            for j in range(T):
                v.scalar_tensor_tensor(k.acc[:, j, :], k.ps[7][:, j * P:(j + 1) * P], k.c8[:, j, e - 1:e],
                                       k.acc[:, j, :], ALU.mult, ALU.add)
        v.drain().then_inc(line.sum_read, 1)

    def block(self):
        v, k, line, p = self.eng, self.k, self.line, self.at
        self.late()
        layer, b, g = self.order[p]
        m = self.rows(p)
        hid = k.h[p % line.SLOTS_H][0:m, :]
        v.wait_ge(line.lo, self.n0 + (p + 1))
        v.wait_ge(line.silu, self.n0 + (p + 1))
        half_silu(v, hid, k.s[g][0:m, :], k.gu[g][0][0:m, :], k.gu[g][1][0:m, :]).then_inc(line.gu_free, 1)
        if layer < 3 and b < NB1 - 1:
            v.drain()
            v.wait_ge(line.cb, self.it * (2 * (NB1 - 1)) + ((layer - 1) * (NB1 - 1) + b + 1))
            v.tensor_tensor(hid, hid, k.ps[5][:], ALU.mult).then_inc(line.cb_free, 1)
        v.drain().then_inc(line.h_ready, 1)
        self.at += 1


class Gate:

    def __init__(self, k, norm):
        self.k, self.norm = k, norm
        (self.turned, self.hi, self.lo, self.logits, self.act, self.centred, self.ready, self.wT, self.wT_hi,
         self.wT_lo) = (k.sem("gate_" + n) for n in (
            "turned", "hi", "lo", "logits", "act", "centred", "ready", "wT", "wT_hi", "wT_lo"))
        self.n = (E1, E1, E3)
        self.c0 = (0, E1, 2 * E1)
        self.x = ((k.xh, k.xl), (k.xh, k.xl), (k.xbh, k.xbl))

    def fill(self, part, l, *points):
        if l < 2:
            for point in points:
                part.fill(f"{point}{l + 1}")

    def tensor(self, pe, part, it, l, norm_at):
        k, a, n, c0, (xh, xl) = self.k, it * 3 + l, self.n[l], self.c0[l], self.x[l]
        pe.wait_ge(self.norm.ready, norm_at + 1)
        for j in range(T):
            last = pe.transpose(k.ps[4][:, j * P:(j + 1) * P], k.xn[:, j, :], k.ident)
        last.then_inc(self.turned, 1)
        self.fill(part, l, "logits")
        pe.wait_ge(self.lo, a + 1)
        for j in range(T):
            c = slice(j * P, (j + 1) * P)
            last = three_pass(pe, k.ps[5][:, j * n:(j + 1) * n], xh[:, c], xl[:, c],
                              k.gth[:, c0:c0 + n], k.gtl[:, c0:c0 + n])
        last.then_inc(self.logits, 1)
        self.fill(part, l, "groups", "top", "weights")

    def tensor_weights(self, pe, it, l):
        k = self.k
        pe.wait_ge(self.ready, it * 3 + l + 1)
        for j in range(T):
            last = pe.transpose(k.ps[4][0:E1, j * P:(j + 1) * P], k.c16[:, j, :], k.ident)
        last.then_inc(self.wT, 1)
        pe.wait_ge(self.wT_lo, it * 2 + l + 1)

    def scalar(self, act, part, it, l):
        k, a, n = self.k, it * 3 + l, self.n[l]
        act.wait_ge(self.turned, a + 1)
        act.activation(self.x[l][0][:], k.ps[4][:], ACT.Copy).then_inc(self.hi, 1)
        self.fill(part, l, "logits")
        if l == 0:
            act.wait_ge(self.logits, a + 1)
            act.activation(k.sg[:], k.ps[5][:, 0:T * n].rearrange("p (t n) -> p t n", n=n), ACT.Tanh, scale=0.5)\
                .then_inc(self.act, 1)
        else:
            act.wait_ge(self.centred, it * 2 + l)
            sg = k.sg[:, :, 0:n]
            act.activation(sg, sg, ACT.Exp).then_inc(self.act, 1)
        self.fill(part, l, "groups", "top", "weights")

    def scalar_weights(self, act, it, l):
        act.wait_ge(self.wT, it * 2 + l + 1)
        act.activation(self.k.wTh, self.k.ps[4][0:E1, :], ACT.Copy).then_inc(self.wT_hi, 1)

    def vector(self, v, part, it, l):
        k, a, n = self.k, it * 3 + l, self.n[l]
        xh, xl = self.x[l]
        v.wait_ge(self.hi, a + 1)
        v.tensor_tensor(xl[:], k.ps[4][:], xh[:].bitcast(F32), ALU.subtract).then_inc(self.lo, 1)
        self.fill(part, l, "logits")
        sg = k.sg[:, :, 0:n]
        each = lambda c: c.unsqueeze(2).to_broadcast([P, T, n])
        if l == 0:
            v.wait_ge(self.act, a + 1)
            v.tensor_scalar(sg, sg, 0.5, 0.5, ALU.mult, ALU.add)
            v.drain()
        else:
            lg = k.ps[5][:, 0:T * n].rearrange("p (t n) -> p t n", n=n)
            v.wait_ge(self.logits, a + 1)
            v.reduce_max(k.r1[:], lg, axis=AX.X)
            v.drain()
            v.tensor_tensor(sg, lg, each(k.r1[:]), ALU.subtract).then_inc(self.centred, 1)
            v.wait_ge(self.act, a + 1)
            v.reduce_sum(k.r1[:], sg, axis=AX.X)
            v.drain()
            v.reciprocal(k.r2[:], k.r1[:])
            v.drain()
            v.tensor_tensor(sg, sg, each(k.r2[:]), ALU.mult)
            v.drain()
        if l < 2:
            g4 = k.sg[:].rearrange("p t (g f) -> p (t g) f", f=4)
            if l == 0:
                for n0, n1, f0, f1, g0 in ((0, 3, 0, 3, 1), (3, 5, 0, 2, 2), (5, 6, 0, 1, 3)):
                    v.tensor_tensor(k.pairs[:, :, n0:n1], g4[:, :, f0:f1], g4[:, :, g0:g0 + f1 - f0], ALU.add)
                v.drain()
                v.reduce_max(k.g8[:, :, 0:4], k.pairs[:].rearrange("p (t g) f -> p t g f", g=4), axis=AX.X)
            else:
                v.reduce_max(k.g8[:, :, 0:4], k.sg[:].rearrange("p t (g f) -> p t g f", f=4), axis=AX.X)
            self.fill(part, l, "groups")
            v.drain()
            topk_mask(v, k.g8[:], k.m8[:], 2, k.gm[:], k.q8[0][:], k.q8[1][:], k.q8[2][:], k.r1[:], k.const[:, C_R8:C_R8 + T * 8])
            inner = lambda x: x.unsqueeze(3).to_broadcast([P, T, 4, 4])
            ms = k.ms[:].rearrange("p t (g f) -> p t g f", f=4)
            v.tensor_tensor(ms, k.sg[:].rearrange("p t (g f) -> p t g f", f=4), inner(k.gm[:, :, 0:4]), ALU.mult)
            if l == 0:
                v.drain()
                v.tensor_scalar(k.gm[:], k.gm[:], 2.0, -2.0, ALU.mult, ALU.add)
                v.drain()
                v.tensor_tensor(ms, ms, inner(k.gm[:, :, 0:4]), ALU.add)
            self.fill(part, l, "top")
            v.drain()
            topk_mask(v, k.ms[:], k.m8[:], K1, k.mask[:], k.q16[0][:], k.q16[1][:], k.q16[2][:], k.r1[:],
                      k.const[:, C_R16:C_R16 + T * E1])
            mask, c = k.mask[:], k.c16[:]
        else:
            topk_mask(v, k.sg[:, :, 0:E3], k.m8[:], K3, k.gm[:], k.q8[0][:], k.q8[1][:], k.q8[2][:], k.r1[:],
                      k.const[:, C_R8:C_R8 + T * 8])
            mask, c = k.gm[:], k.c8[:]
        v.tensor_tensor(c, mask, sg, ALU.mult)
        if l != 1:
            v.drain()
            v.reduce_sum(k.r1[:], c, axis=AX.X)
            v.drain()
            v.tensor_scalar(k.r1[:], k.r1[:], 1e-6 if l == 0 else 1e-20, None, ALU.add)
            v.drain()
            v.reciprocal(k.r2[:], k.r1[:])
            v.drain()
            v.tensor_tensor(c, c, each(k.r2[:]), ALU.mult)
        v.drain().then_inc(self.ready, 1)
        self.fill(part, l, "weights")

    def vector_weights(self, v, it, l):
        k = self.k
        v.wait_ge(self.wT_hi, it * 2 + l + 1)
        v.tensor_tensor(k.wTl, k.ps[4][0:E1, :], k.wTh.bitcast(F32), ALU.subtract).then_inc(self.wT_lo, 1)


def later_layers(nc, k, d):
    names = ("kv_free", "mix_loaded", "mix_free", "q", "q_all", "q_hi", "q3", "scores", "centred", "exp", "turned", "taken",
             "pv", "pv_read", "o_ready", "oT", "o_hi", "o_lo", "out", "l2", "xT", "x_hi", "x_lo", "sum_copied", "sum_turned", "done", "stored")
    s = Names(**{n: k.sem("m_" + n) for n in names})
    k_loaded = [k.sem(f"m_k_loaded{i}") for i in range(2)]
    norm = Norm(k, "m_norm", k.xn)
    gate = Gate(k, norm)
    line = Line(k)
    NA, NB = 2 * NB1, len(B3)
    tile = [slice(j * P, (j + 1) * P) for j in range(T)]
    by_tile = lambda ps: ps.rearrange("p (t d) -> p t d", d=P)
    row = lambda r: r.unsqueeze(1).to_broadcast([P, T, P])
    first_block = lambda it: 0 if isinstance(it, int) and it == 0 else it * (NA + NB) - NB
    GROUPS = T * 4
    S = (k.ps[2], k.ps[3])
    QUAD = (k.ps[6], k.ps[5], k.ps[2], k.ps[3])
    KD = HD + 1

    def turns(eng, turn):
        turn(0, True, False)
        with eng.Fori(1, CHUNKS) as it:
            turn(it, True, True)
        turn(CHUNKS, False, True)

    with nc.Block() as block:
        @block.sync
        def _(sp):
            def mix(it, part):
                sp.wait_ge(s.mix_free, it * 2 + part + 1)
                for t in range(T):
                    sp.dma_start(k.mixr[:, t, :], d.mix[it * T + t, part * P:(part + 1) * P].partition_broadcast(P))\
                        .then_inc(s.mix_loaded, 16)

            def turn(it, a, b):
                if a:
                    for j in range(T):
                        sp.wait_ge(s.kv_free, it * T + j + 1)
                        sp.dma_start(k.k3m[j % 2][:].bitcast(F32), d.keys1[it * T + j, :, :]).then_inc(k_loaded[j % 2], 16)
                        sp.dma_start(k.v9[j % 2][:].rearrange("p h d -> p (h d)"), d.values1[it * T + j, :, :])\
                            .then_inc(k_loaded[j % 2], 16)
                        if j == 1:
                            mix(it, 0)
                    mix(it, 1)
                if b:
                    sp.wait_ge(s.done, it)
                    before = bass.ds((it - 1) * T, T)
                    sp.dma_start(d.out[before, :, :].rearrange("t p d -> p t d"), k.x[:, before, :]).then_inc(s.stored, 16)

            turns(sp, turn)
            sp.wait_ge(s.stored, 16 * CHUNKS)

        @block.gpsimd
        def _(g):
            def turn(it, a, b):
                part = PoolPart(line, g, first_block(it), it, a, b)
                if not a:
                    for _ in B3:
                        part.block()
                    part.flush()
                    return
                norm.pool(g, it * 6)
                part.fill("norm0")
                part.fill("turned0")
                part.fill("queries")
                for u in range(STEPS):
                    if not b and u < SEQS - T:
                        k.combine.pool(g, T + u)
                    part.fill(f"step{u}")
                part.fill("heads")
                part.fill("out")
                for l in range(2):
                    norm.pool(g, it * 6 + 2 * l + 1)
                    part.fill(f"norm{2 * l + 1}")
                    gate.fill(part, l, "logits", "groups", "top", "weights")
                    for _ in range(NB1):
                        part.block()
                    part.fill(f"sum{l + 1}")
                    part.catch_up()
                    norm.pool(g, it * 6 + 2 * l + 2)
                    part.fill(f"norm{2 * l + 2}")
                norm.pool(g, it * 6 + 5)
                part.fill("norm5")
                part.flush()

            turns(g, turn)

        @block.vector
        def _(v):
            def add(x, ps, col):
                v.scalar_tensor_tensor(x, by_tile(ps), k.tg[:, col:col + 1], x, ALU.mult, ALU.add)
                v.drain()

            def low(n):
                v.wait_ge(s.x_hi, n)
                v.tensor_tensor(k.xl[:], k.ps[4][:], k.xh[:].bitcast(F32), ALU.subtract).then_inc(s.x_lo, 1)

            def q3(it, q):
                v.wait_ge(s.q_hi, it * 4 + q + 1)
                v.scalar_tensor_tensor(k.q3[q][:], k.qh[:].bitcast(F32), k.const[:, C_SPLIT:C_SPLIT + 1], k.qf[q % 2][:],
                                       ALU.mult, ALU.add).then_inc(s.q3, 1)

            def evict(it, j):
                v.wait_ge(s.pv, it * T + j + 1)
                v.tensor_copy(k.pv[:].rearrange("p h d -> p (h d)"), k.ps[5][:, 0:HEADS * KD]).then_inc(s.pv_read, 1)
                v.drain()

            def normalize(j):
                v.tensor_tensor(k.good[:], k.pv[:, :, HD], k.pv[:, :, HD], ALU.is_equal)
                v.reciprocal(k.rec[:], k.pv[:, :, HD])
                v.drain()
                v.tensor_tensor(k.pv[:, :, 0:HD], k.pv[:, :, 0:HD], k.rec[:].unsqueeze(2).to_broadcast([P, HEADS, HD]), ALU.mult)
                v.drain()
                v.copy_predicated(k.o[:, j, :].rearrange("p (h d) -> p h d", d=HD),
                                  k.good[:].unsqueeze(2).to_broadcast([P, HEADS, HD]), k.pv[:, :, 0:HD])
                last = v.drain()
                if j == T - 1:
                    last.then_inc(s.o_ready, 1)

            def finish(it, part):
                part.flush()
                x = k.x[:, bass.ds((it - 1) * T, T), :]
                v.scalar_tensor_tensor(x, k.acc[:], k.tg[:, 7:8], x, ALU.mult, ALU.add)
                v.drain().then_inc(s.done, 1)

            def turn(it, a, b):
                part = VectorPart(line, v, first_block(it), it, a, b)
                if not a:
                    for _ in B3:
                        part.block()
                    finish(it, part)
                    return
                x = k.x[:, bass.ds(it * T, T), :]
                xs = [k.x[:, it * T + j, :] for j in range(T)]
                norm_fill = lambda n: norm.vector(v, it * 6 + n, xs, lambda: part.fill(f"norm{n}"))
                norm_fill(0)
                low(it * 2 + 1)
                v.tensor_tensor(x, x, row(k.bo1[:]), ALU.add)
                v.memset(k.o[:], 0.0)
                part.fill("turned0")
                for q in range(4):
                    q3(it, q)
                part.fill("queries")
                for u in range(STEPS):
                    if u < GROUPS:
                        heads = S[u % 2][:].rearrange("p (h t) -> p h t", t=P)
                        v.wait_ge(s.scores, it * GROUPS + u + 1)
                        v.reduce_max(k.mx4[:, u % 2, :], heads, axis=AX.X)
                        v.drain()
                        if u >= 2:
                            v.wait_ge(s.turned, it * GROUPS + u - 1)
                        v.tensor_tensor(k.e[u % 2][:].rearrange("p (h t) -> p h t", t=P), heads,
                                        k.mx4[:, u % 2, :].unsqueeze(2).to_broadcast([P, 4, P]), ALU.subtract)\
                            .then_inc(s.centred, 1)
                    if u % 4 == 1 and u >= 5:
                        evict(it, u // 4 - 1)
                    if u % 4 == 2 and u >= 6:
                        normalize(u // 4 - 1)
                    if not b and u >= 2 and u - 2 < SEQS - T:
                        k.combine.vector(v, T + u - 2)
                    part.fill(f"step{u}")
                normalize(T - 1)
                part.fill("heads")
                v.wait_ge(s.o_hi, it + 1)
                v.tensor_tensor(k.xl[:], k.ps[4][:], k.xh[:].bitcast(F32), ALU.subtract).then_inc(s.o_lo, 1)
                part.fill("out")
                v.wait_ge(s.out, it + 1)
                add(x, k.ps[6][:], 1)
                for l in range(2):
                    norm_fill(2 * l + 1)
                    gate.vector(v, part, it, l)
                    gate.vector_weights(v, it, l)
                    for _ in range(NB1):
                        part.block()
                    part.fill(f"sum{l + 1}")
                    v.wait_ge(s.sum_turned, it * 2 + l + 1)
                    add(x, k.ps[4][:], 5 + l)
                    norm_fill(2 * l + 2)
                    if l == 0:
                        low(it * 2 + 2)
                        v.wait_ge(s.mix_loaded, it * (32 * T) + 16 * T)
                        v.tensor_tensor(x, x, k.mixr[:], ALU.add)
                        v.drain().then_inc(s.mix_free, 1)
                        v.wait_ge(s.l2, it + 1)
                        add(x, k.ps[6][:], 2)
                v.drain()
                v.wait_ge(s.mix_loaded, it * (32 * T) + 32 * T)
                v.scalar_tensor_tensor(k.xn[:], k.xn[:], 0.0, k.mixr[:], ALU.max, ALU.mult)
                v.drain().then_inc(s.mix_free, 1)
                v.tensor_tensor(x, x, k.xn[:], ALU.add)
                v.drain()
                norm_fill(5)
                if b:
                    finish(it, part)
                gate.vector(v, part, it, 2)

            v.sem_inc(s.kv_free, 2)
            v.sem_inc(s.mix_free, 1)
            line.credits(v)
            v.memset(k.g8[:], -3e38)
            v.drain()
            turns(v, turn)

        @block.scalar
        def _(act):
            def high(n):
                act.wait_ge(s.xT, n)
                act.activation(k.xh[:], k.ps[4][:], ACT.Copy).then_inc(s.x_hi, 1)

            def q_high(it, q):
                act.wait_ge(s.q if q < 2 else s.q_all, it * 2 + q + 1 if q < 2 else it + 1)
                act.activation(k.qf[q % 2][:], QUAD[q][:], ACT.Identity, bias=k.bq[:, q:q + 1])
                act.drain()
                if q:
                    act.wait_ge(s.q3, it * 4 + q)
                act.activation(k.qh[:], k.qf[q % 2][:], ACT.Copy).then_inc(s.q_hi, 1)

            def turn(it, a, b):
                part = ScalarPart(line, act, first_block(it), it, a, b)
                if not a:
                    for _ in B3:
                        part.block()
                    part.flush()
                    return
                part.fill("norm0")
                high(it * 2 + 1)
                part.fill("turned0")
                for q in range(4):
                    q_high(it, q)
                part.fill("queries")
                for u in range(STEPS):
                    fills = b and FILLERS[f"step{u}"]
                    if fills:
                        part.late(True)
                    if u < GROUPS:
                        act.wait_ge(s.centred, it * GROUPS + u + 1)
                        act.activation(k.e[u % 2][:], k.e[u % 2][:], ACT.Exp, scale=float(HD) ** -0.5).then_inc(s.exp, 1)
                    if fills:
                        part.silu()
                    if 1 <= u <= GROUPS:
                        act.wait_ge(s.turned, it * GROUPS + u)
                        act.activation(k.pt[:], k.ps[4][:], ACT.Copy).then_inc(s.taken, 1)
                part.fill("heads")
                act.wait_ge(s.oT, it + 1)
                act.activation(k.xh[:], k.ps[4][:], ACT.Copy).then_inc(s.o_hi, 1)
                part.fill("out")
                for l in range(2):
                    part.fill(f"norm{2 * l + 1}")
                    gate.scalar(act, part, it, l)
                    gate.scalar_weights(act, it, l)
                    for _ in range(NB1):
                        part.block()
                    part.fill(f"sum{l + 1}")
                    part.catch_up()
                    act.wait_ge(line.sum_a, it * 2 + l + 1)
                    act.activation(k.pt[:], k.ps[6][:], ACT.Copy).then_inc(s.sum_copied, 1)
                    part.fill(f"norm{2 * l + 2}")
                    if l == 0:
                        high(it * 2 + 2)
                part.fill("norm5")
                part.flush()
                gate.scalar(act, part, it, 2)

            turns(act, turn)

        @block.tensor
        def _(pe):
            def x_turned(norm_at):
                pe.wait_ge(norm.ready, norm_at + 1)
                for j in range(T):
                    last = pe.transpose(k.ps[4][:, tile[j]], k.xn[:, j, :], k.ident)
                last.then_inc(s.xT, 1)

            def queries():
                for q in range(4):
                    c = slice(q * P, (q + 1) * P)
                    last = three_pass(pe, QUAD[q][:], k.wa1h[:, c], k.wa1l[:, c], k.xh[:], k.xl[:])
                    if q < 2:
                        last.then_inc(s.q, 1)
                last.then_inc(s.q_all, 1)

            def scores(it, u):
                j, g = divmod(u, 4)
                if g == 0:
                    if j == 0:
                        pe.wait_ge(s.q3, it * 4 + 4)
                    pe.wait_ge(k_loaded[j % 2], it * 64 + (j // 2 * 32 + 32))
                if u >= 2:
                    pe.wait_ge(s.centred, it * GROUPS + u - 1)
                r = slice(32 * g, 32 * g + 3 * HD)
                for q in range(4):
                    last = pe.matmul(S[u % 2][:, tile[q]], k.q3[q][r, tile[j]], k.k3m[j % 2][r, tile[q]],
                                     start=True, stop=True)
                last.then_inc(s.scores, 1)

            def turned(it, u):
                pe.wait_ge(s.exp, it * GROUPS + u + 1)
                for q in range(4):
                    last = pe.transpose(k.ps[4][:, tile[q]], k.e[u % 2][:, tile[q]], k.ident)
                last.then_inc(s.turned, 1)

            def values(it, u):
                j, g = divmod(u, 4)
                pe.wait_ge(s.taken, it * GROUPS + u + 1)
                if g == 0 and j:
                    pe.wait_ge(s.pv_read, it * T + j)
                for q in range(4):
                    h = 4 * q + g
                    c = h * KD
                    last = pe.matmul(k.ps[5][:, c:c + KD], k.pt[:, tile[q]], k.v9[j % 2][:, h, :], start=True, stop=True)
                if g == 3:
                    last.then_inc(s.pv, 1)
                    pe.drain().then_inc(s.kv_free, 1)

            def turn(it, a, b):
                part = TensorPart(line, pe, first_block(it), it, a, b)
                if not a:
                    for _ in B3:
                        part.block()
                    part.flush()
                    return
                part.fill("norm0")
                x_turned(it * 6)
                part.fill("turned0")
                pe.wait_ge(s.x_lo, it * 2 + 1)
                queries()
                part.fill("queries")
                for u in range(STEPS):
                    fills = b and FILLERS[f"step{u}"]
                    if u < GROUPS:
                        scores(it, u)
                    if u >= 2:
                        values(it, u - 2)
                    if fills:
                        part.up()
                    if 1 <= u <= GROUPS:
                        turned(it, u - 1)
                    if fills:
                        part.late()
                part.fill("heads")
                pe.wait_ge(s.o_ready, it + 1)
                for j in range(T):
                    last = pe.transpose(k.ps[4][:, tile[j]], k.o[:, j, :], k.ident)
                last.then_inc(s.oT, 1)
                part.fill("out")
                pe.wait_ge(s.o_lo, it + 1)
                for j in range(T):
                    last = three_pass(pe, k.ps[6][:, tile[j]], k.xh[:, tile[j]], k.xl[:, tile[j]],
                                      k.wa1h[:, 4 * P:5 * P], k.wa1l[:, 4 * P:5 * P])
                last.then_inc(s.out, 1)
                for l in range(2):
                    part.fill(f"norm{2 * l + 1}")
                    gate.tensor(pe, part, it, l, it * 6 + 2 * l + 1)
                    for n in range(NB1):
                        part.up()
                        if n == 0:
                            gate.tensor_weights(pe, it, l)
                        part.late()
                        part.weights()
                    part.fill(f"sum{l + 1}")
                    part.catch_up()
                    pe.wait_ge(s.sum_copied, it * 2 + l + 1)
                    for j in range(T):
                        last = pe.transpose(k.ps[4][:, tile[j]], k.pt[:, tile[j]], k.ident)
                    last.then_inc(s.sum_turned, 1)
                    part.fill(f"norm{2 * l + 2}")
                    if l == 0:
                        x_turned(it * 6 + 2)
                        pe.wait_ge(s.x_lo, it * 2 + 2)
                        for j in range(T):
                            last = three_pass(pe, k.ps[6][:, tile[j]], k.xh[:, tile[j]], k.xl[:, tile[j]],
                                              k.l2wh[:], k.l2wl[:])
                        last.then_inc(s.l2, 1)
                part.fill("norm5")
                part.flush()
                gate.tensor(pe, part, it, 2, it * 6 + 5)

            turns(pe, turn)


def program(nc, d):
    k = Names()
    with ExitStack() as ctx:
        def sb(name, shape, dt=F32, c=ctx):
            return c.enter_context(nc.sbuf_tensor(name, shape, dt))

        k.sem = lambda name: nc.alloc_semaphore(name=name)
        k.ps = [ctx.enter_context(nc.psum_tensor(f"ps{i}", [P, 512], F32)) for i in range(8)]
        k.gu = [(k.ps[0], k.ps[1]), (k.ps[2], k.ps[3])]
        k.x = sb("x", [P, SEQS, P])
        k.const = sb("const", [P, C_ALL])
        k.ident = k.const[:, C_ID:C_ID + P]
        k.bo1 = sb("bo1", [P, P])
        k.tg = sb("tg", [P, 8])
        k.eps4, k.mhalf = sb("eps4", [P, T]), sb("mhalf", [P, T])
        k.st6, k.mv = sb("st6", [P, T, 6]), sb("mv", [P, T, 2])
        k.ve, k.rs = sb("ve", [P, T]), sb("rs", [P, T])
        k.xn = sb("xn", [P, T, P])
        k.xh, k.xl = sb("xh", [P, CW], F32R), sb("xl", [P, CW], F32R)
        k.xbh, k.xbl = sb("xbh", [P, CW], F32R), sb("xbl", [P, CW], F32R)
        k.h, k.s = ([sb(f"{n}{i}", [P, CW]) for i in range(2)] for n in ("h", "s"))
        k.hh = [sb(f"hh{i}", [P, CW], F32R) for i in range(3)]
        k.hl = [sb(f"hl{i}", [P, CW], F32R) for i in range(3)]
        k.l2wh, k.l2wl = sb("l2wh", [P, P], F32R), sb("l2wl", [P, P], F32R)
        k.w1h, k.w1l, k.w2h, k.w2l = (sb(n, [P, NB1 * W1C], F32R) for n in ("w1h", "w1l", "w2h", "w2l"))
        k.index, k.gate = sb("index", [P, K0 * SEQS], I32), sb("gate", [P, K0, SEQS])
        k.bq = sb("bq", [P, 4])
        unused = nc.snapshot_sems()
        with ExitStack() as l0:
            k.rows = sb("rows", [P, B_ALL], c=l0)
            k.const0 = sb("const0", [P, L_ALL], c=l0)
            k.raw = [sb(f"raw{i}", [P, W3C], c=l0) for i in range(2)]
            k.xn_all = sb("xn_all", [P, SEQS, P], c=l0)
            k.sc = sb("sc", [P, SEQS, 40], c=l0)
            k.ub = sb("ub", [P, 2 * P], BF16, l0)
            with ExitStack() as a0:
                k.xn2 = sb("xn2", [P, T, P], c=a0)
                k.zero = sb("zero", [P, SLOTS // 16], c=a0)
                k.junk = sb("junk", [P, CW], c=a0)
                k.sh0h, k.sh0l = sb("sh0h", [P, W0C], F32R, a0), sb("sh0l", [P, W0C], F32R, a0)
                k.g0h, k.g0l = sb("g0h", [P, 40], F32R, a0), sb("g0l", [P, 40], F32R, a0)
                k.wa0, k.bcol = sb("wa0", [P, 4 * P], c=a0), sb("bcol", [P, 2], c=a0)
                with ExitStack() as su:
                    k.cent, k.cs = sb("cent", [40, P], c=su), sb("cs", [40, 3], c=su)
                    setup(nc, k, d)
                k.ctxr = sb("ctxr", [P, CW], c=a0)
                k.xT, k.qT, k.kT, k.pT, k.oT = (sb(n, [P, CW], c=a0) for n in ("xT", "qT", "kT", "pT", "oT"))
                k.v0, k.pr = sb("v0", [P, T, P], c=a0), sb("pr", [P, T, P], c=a0)
                k.mx = sb("mx", [P, 3 * T], c=a0)
                k.ss, k.ss2, k.rn = (sb(n, [P, T], c=a0) for n in ("ss", "ss2", "rn"))
                layer0_attention(nc, k, d)
            nc.clear_and_free_semaphores(nc.allocated_since(unused))
            nc.all_engine_barrier()
            layer0_experts_all(nc, k, d, sb)
        k.w3h, k.w3l = sb("w3h", [P, (E3 + 1) * W3C], F32R), sb("w3l", [P, (E3 + 1) * W3C], F32R)
        k.wa1h, k.wa1l = sb("wa1h", [P, 5 * P], F32R), sb("wa1l", [P, 5 * P], F32R)
        k.gth, k.gtl = sb("gth", [P, 2 * E1 + E3], F32R), sb("gtl", [P, 2 * E1 + E3], F32R)
        k.selh = sb("selh", [E1, (NB1 - 1) * P], F32R)
        k.acc = sb("acc", [P, T, P])
        with ExitStack() as comb:
            k.combine = Combine(k, d, (k.acc[:].rearrange("p t d -> p (t d)"), k.xbh[:].bitcast(F32)))
            k.raw = [sb(f"raw_w3_{i}", [P, W3C], c=comb) for i in range(4)]
            layer0_combine(nc, k, d)
        k.q3, k.k3m = ([sb(f"{n}{i}", [P, 4 * P], F32R) for i in range(2)] for n in ("q3", "k3m"))
        k.q3 += [k.xh, k.xl]
        k.v9 = [sb(f"v9{i}", [P, HEADS, HD + 1]) for i in range(2)]
        k.qh, k.oh, k.ol = k.hh[0], k.hh[1], k.hh[2]
        k.e = [sb(f"e{i}", [P, 4 * P]) for i in range(2)]
        k.pt, k.qh = sb("pt", [P, 4 * P]), sb("qh", [P, 4 * P], F32R)
        k.qf = (k.pt, k.e[1])
        k.o = k.xn
        k.mixr = sb("mixr", [P, T, P])
        k.mx4, k.rec = sb("mx4", [P, 2, 4]), sb("recd", [P, HEADS])
        k.good, k.pv = sb("good", [P, HEADS], I32), sb("pv", [P, HEADS, HD + 1])
        k.sg, k.ms, k.mask, k.c16 = (sb(n, [P, T, E1]) for n in ("sg", "ms", "mask", "c16"))
        k.pairs = sb("pairs", [P, T * 4, 6])
        k.g8, k.m8, k.gm, k.c8 = (sb(n, [P, T, 8]) for n in ("g8", "m8", "gm", "c8"))
        k.q8 = [sb(f"q8_{i}", [P, T, 8]) for i in range(3)]
        k.q16 = [sb(f"q16_{i}", [P, T, E1]) for i in range(3)]
        k.r1, k.r2 = sb("r1", [P, T]), sb("r2", [P, T])
        k.wTh, k.wTl = k.q3[0][0:E1, :], k.q3[1][0:E1, :]
        later_layers(nc, k, d)


def laid_out(i):
    t = lambda a: np.ascontiguousarray(np.swapaxes(a, -1, -2))
    cat = lambda *a: np.ascontiguousarray(np.concatenate(a, axis=-1))
    z = lambda *s: np.zeros(s, np.float32)
    o = {"x": i["x"], "const": constants(), "const0": constants_layer0()}
    o["ctxT"] = t(i["ctx_1024"].reshape(SEQS * P, P))
    o["rows"] = cat(i["L0_xattn_bv"], i["L0_xattn_bo"], i["L0_ffn_bias"], i["L1_xattn_bv"], i["L1_xattn_bo"],
                    i["L2_xattn_b"], i["g_xattn"], i["g_ffn"])[None]
    o["wa0"] = cat(i["L0_xattn_Wq"], i["L0_xattn_Wk"], i["L0_xattn_Wv"], i["L0_xattn_Wo"])
    o["cent"] = np.concatenate([i["L0_ffn_group_centroids"], i["L0_ffn_expert_centroids"]])
    halves = lambda w: cat(w[..., 0:P, :], w[..., P:2 * P, :])
    o["w0"] = np.concatenate([cat(i["L0_ffn_wg"], i["L0_ffn_wu"], halves(i["L0_ffn_wd"])),
                              cat(i["L0_ffn_sg"], i["L0_ffn_su"], halves(i["L0_ffn_sd"]))[None]])
    pair = lambda w: np.concatenate([w[0::2], w[1::2]], axis=2)
    down = lambda w: np.concatenate([w[0::2], w[1::2]], axis=1)
    pack = lambda g, u, dn: np.ascontiguousarray(np.concatenate(list(cat(g, u, dn)), axis=1))
    o["w1"] = pack(np.concatenate([pair(t(i["L1_ffn_w1_e"])), t(i["L1_ffn_w1_s"])[None]]),
                   np.concatenate([pair(t(i["L1_ffn_w3_e"])), t(i["L1_ffn_w3_s"])[None]]),
                   np.concatenate([down(t(i["L1_ffn_w2_e"])), t(i["L1_ffn_w2_s"])[None]]))
    o["w2"] = pack(np.concatenate([pair(i["L2_ffn_w1"]), i["L2_ffn_ws1"][None]]),
                   np.concatenate([pair(i["L2_ffn_w3"]), i["L2_ffn_ws3"][None]]),
                   np.concatenate([down(i["L2_ffn_w2"]), i["L2_ffn_ws2"][None]]))
    o["l2w"] = cat(t(i["L2_xattn_W"][:, 0:P]), t(i["L2_xattn_W"][:, P:2 * P]))
    gate = np.concatenate([i["L3_ffn_shared_gate"][None], i["L3_ffn_expert_gate"]])
    up = np.concatenate([i["L3_ffn_shared_up"][None], i["L3_ffn_expert_up"]])
    dn = t(np.concatenate([i["L3_ffn_shared_down"][None], i["L3_ffn_expert_down"]]))
    dn = np.concatenate([dn, z(E3 + 1, 3 * P - FF3, P)], axis=1).reshape(E3 + 1, 3, P, P)
    o["w3"] = cat(t(gate), t(up), np.swapaxes(dn, 1, 2).reshape(E3 + 1, P, 3 * P))
    def quads(w):
        a = w.reshape(*w.shape[:-1], HEADS, 1, HD)
        a = np.concatenate([a, a, a, np.zeros_like(a)], axis=-2)
        return a.reshape(*w.shape[:-1], 4 * P)
    o["wa1"] = cat(quads(t(i["L1_xattn_Wq"])), quads(t(i["L1_xattn_Wk"])), t(i["L1_xattn_Wv"]), t(i["L1_xattn_Wo"]))
    o["brow"] = quads(i["L1_xattn_bk"])[None]
    o["bq"] = quads(i["L1_xattn_bq"]).reshape(4, P).T
    o["bcol"] = np.stack([i["L0_xattn_bq"], i["L0_xattn_bk"]], 1)
    o["gates"] = cat(t(i["L1_ffn_w_gate"]), t(i["L2_ffn_gate_w"]), t(i["L3_ffn_gate_w"]))
    o["sel"] = selectors()
    return {n: np.ascontiguousarray(a) for n, a in o.items()}


def kernel(**inputs):
    import concourse.bacc as bacc
    from concourse.bass_utils import run_bass_kernel_spmd as run

    nc = bacc.Bacc("TRN2", target_bir_lowering=False, num_devices=1)
    arrays = laid_out({n: np.asarray(a) for n, a in inputs.items()})
    d = Names()
    for name, a in arrays.items():
        d[name] = nc.dram_tensor("in_" + name, a.shape, mybir.dt.from_np(a.dtype), kind="ExternalInput").ap()
    d.out = nc.dram_tensor("out_0", (SEQS, P, P), F32, kind="ExternalOutput").ap()
    d.buf = nc.dram_tensor("slot_in", (SLOTS + K0 * SEQS * P, P), F32, kind="Internal").ap()
    d.oute = nc.dram_tensor("slot_out", (SLOTS + P, P), F32, kind="Internal").ap()
    d.mix = nc.dram_tensor("seq_rows", (SEQS, 2 * P), F32, kind="Internal").ap()
    d.keys1 = nc.dram_tensor("l1_keys", (SEQS, P, 4 * P), F32, kind="Internal").ap()
    d.values1 = nc.dram_tensor("l1_values", (SEQS, P, HEADS * (HD + 1)), F32, kind="Internal").ap()
    program(nc, d)
    r = run(nc, [{"in_" + n: a for n, a in arrays.items()}], core_ids=[0])
    return r.results[0]["out_0"]
```
